# Optimizing a Trainium2 kernel written in Bass

```python
import numpy as np
import jax
import jax.numpy as jnp

def _softmax(x, axis=-1):
    return jax.nn.softmax(x, axis=axis)

def _gelu(x):
    return jax.nn.gelu(x, approximate=True)

def _silu(x):
    return jax.nn.silu(x)

def _sigmoid(x):
    return jax.nn.sigmoid(x)

def _layernorm(x, axis=-1, eps=1e-05):
    m = jnp.mean(x, axis=axis, keepdims=True)
    v = jnp.var(x, axis=axis, keepdims=True)
    return (x - m) / jnp.sqrt(v + eps)

def _scatter_add(tgt, idx, src, axis=0):
    return tgt.at[idx].add(src)

def _segment_sum(src, seg, n):
    return jax.ops.segment_sum(src, seg, n)
kernel_name = 'mk_prb_d2_jaxref_r8_40acb0'

def setup_inputs(seed: int=0):
    np.random.seed(seed)
    _w = jnp.asarray

    def _L0_attn_setup():
        import jax, jax.numpy as jnp
        import numpy as np
        N_EMBD = 128
        N_HEAD = 16
        HORIZON = 64
        HS = N_EMBD // N_HEAD
        BD = max(HS // 4, 16)

        def _windows(t, delta):
            B, nh, T, D = t.shape
            padded = jnp.pad(t, ((0, 0), (0, 0), (delta - 1, 0), (0, 0)))
            idx = jnp.arange(T)[:, None] + jnp.arange(delta)[None, :]
            return padded[:, :, idx]
        key = jax.random.key(seed)
        ks = jax.random.split(key, 12)
        s = 0.02
        B, T = (2, 128)
        return {'x': jax.random.normal(ks[0], (B, T, N_EMBD), jnp.float32), 'W_disp': jax.random.normal(ks[1], (N_EMBD, N_HEAD * BD), jnp.float32) * s, 'W_val': jax.random.normal(ks[2], (N_EMBD, N_EMBD), jnp.float32) * s, 'rel_pos_emb': jax.random.normal(ks[3], (HORIZON, BD), jnp.float32) * s, 'W_strain': jax.random.normal(ks[4], (BD, BD), jnp.float32) * s, 'W_pos': jax.random.normal(ks[5], (BD, BD), jnp.float32) * s, 'W_bond': jax.random.normal(ks[6], (BD, 1), jnp.float32) * s, 'W_dmg': jax.random.normal(ks[7], (BD, BD), jnp.float32) * s, 'b_dmg': jnp.zeros((BD,), jnp.float32), 'W_dmg_out': jax.random.normal(ks[8], (BD, 1), jnp.float32) * s, 'b_dmg_out': jnp.full((1,), -3.0, jnp.float32), 'W_cproj': jax.random.normal(ks[9], (N_EMBD, N_EMBD), jnp.float32) * s}
    _L0_attn_in = _L0_attn_setup()

    def _L0_ffn_setup():
        import jax, jax.numpy as jnp
        import numpy as np
        ALPHA = 1.702
        LIMIT = 7.0
        EPS = 1e-05
        E = 16
        K = 4

        def _swiglu(h):
            x_glu = jnp.minimum(h[..., ::2], LIMIT)
            x_lin = jnp.clip(h[..., 1::2], LIMIT, LIMIT)
            return x_glu * jax.nn.sigmoid(ALPHA * x_glu) * (x_lin + 1.0)
        key = jax.random.key(seed)
        ks = jax.random.split(key, 7)
        B, T, H, I = (1, 256, 128, 128)
        x = jax.random.normal(ks[0], (B, T, H), jnp.float32)
        scale = jnp.ones((H,), jnp.float32)
        gate_w = jax.random.normal(ks[1], (E, H), jnp.float32) * 0.02
        gate_b = jnp.zeros((E,), jnp.float32)
        mlp1_w = jax.random.normal(ks[2], (E, 2 * I, H), jnp.float32) * 0.02
        mlp1_b = jax.random.normal(ks[3], (E, 2 * I), jnp.float32) * 0.02
        mlp2_w = jax.random.normal(ks[4], (E, H, I), jnp.float32) * 0.02
        mlp2_b = jax.random.normal(ks[5], (E, H), jnp.float32) * 0.02
        return dict(x=x, scale=scale, gate_w=gate_w, gate_b=gate_b, mlp1_w=mlp1_w, mlp1_b=mlp1_b, mlp2_w=mlp2_w, mlp2_b=mlp2_b)
    _L0_ffn_in = _L0_ffn_setup()

    def _L1_attn_setup():
        import jax, jax.numpy as jnp
        import numpy as np
        N_FILTERS = 128
        N_HEADS = 16
        key = jax.random.key(seed)
        k1, k2, k3 = jax.random.split(key, 3)
        x = jax.random.normal(k1, (8, 128, N_FILTERS), dtype=jnp.float32)
        w_qkv = jax.random.normal(k2, (N_FILTERS, N_FILTERS * 3), dtype=jnp.float32) * (0.02 / N_FILTERS) ** 0.5
        w_out = jax.random.normal(k3, (N_FILTERS, N_FILTERS), dtype=jnp.float32) * (0.02 / N_FILTERS) ** 0.5
        return {'x': x, 'w_qkv': w_qkv, 'w_out': w_out}
    _L1_attn_in = _L1_attn_setup()

    def _L1_ffn_setup():
        import jax, jax.numpy as jnp
        import numpy as np
        EMBED = 128
        D_FF = 4 * EMBED
        N_EXPERTS = 8
        TOP_K = 2
        B, S = (2, 128)
        key = jax.random.key(seed)
        ks = jax.random.split(key, 10)
        sc_d = 1.0 / np.sqrt(EMBED)
        sc_h = 1.0 / np.sqrt(D_FF)
        return {'inputs': jax.random.normal(ks[0], (B, S, EMBED), jnp.float32), 'rw1': jax.random.normal(ks[1], (EMBED, D_FF), jnp.float32) * sc_d, 'rb1': jnp.zeros((D_FF,), jnp.float32), 'rw2': jax.random.normal(ks[2], (D_FF, N_EXPERTS), jnp.float32) * sc_h, 'rb2': jnp.zeros((N_EXPERTS,), jnp.float32), 'W1': jax.random.normal(ks[3], (N_EXPERTS, EMBED, D_FF), jnp.float32) * sc_d, 'b1': jnp.zeros((N_EXPERTS, D_FF), jnp.float32), 'W2': jax.random.normal(ks[4], (N_EXPERTS, D_FF, EMBED), jnp.float32) * sc_h, 'b2': jnp.zeros((N_EXPERTS, EMBED), jnp.float32)}
    _L1_ffn_in = _L1_ffn_setup()
    _d = {'L0_attn_x': _L0_attn_in['x'], 'L0_attn_W_disp': _L0_attn_in['W_disp'], 'L0_attn_W_val': _L0_attn_in['W_val'], 'L0_attn_rel_pos_emb': _L0_attn_in['rel_pos_emb'], 'L0_attn_W_strain': _L0_attn_in['W_strain'], 'L0_attn_W_pos': _L0_attn_in['W_pos'], 'L0_attn_W_bond': _L0_attn_in['W_bond'], 'L0_attn_W_dmg': _L0_attn_in['W_dmg'], 'L0_attn_b_dmg': _L0_attn_in['b_dmg'], 'L0_attn_W_dmg_out': _L0_attn_in['W_dmg_out'], 'L0_attn_b_dmg_out': _L0_attn_in['b_dmg_out'], 'L0_attn_W_cproj': _L0_attn_in['W_cproj'], 'L0_ffn_scale': _L0_ffn_in['scale'], 'L0_ffn_gate_w': _L0_ffn_in['gate_w'], 'L0_ffn_gate_b': _L0_ffn_in['gate_b'], 'L0_ffn_mlp1_w': _L0_ffn_in['mlp1_w'], 'L0_ffn_mlp1_b': _L0_ffn_in['mlp1_b'], 'L0_ffn_mlp2_w': _L0_ffn_in['mlp2_w'], 'L0_ffn_mlp2_b': _L0_ffn_in['mlp2_b'], 'L1_attn_w_qkv': _L1_attn_in['w_qkv'], 'L1_attn_w_out': _L1_attn_in['w_out'], 'L1_ffn_rw1': _L1_ffn_in['rw1'], 'L1_ffn_rb1': _L1_ffn_in['rb1'], 'L1_ffn_rw2': _L1_ffn_in['rw2'], 'L1_ffn_rb2': _L1_ffn_in['rb2'], 'L1_ffn_W1': _L1_ffn_in['W1'], 'L1_ffn_b1': _L1_ffn_in['b1'], 'L1_ffn_W2': _L1_ffn_in['W2'], 'L1_ffn_b2': _L1_ffn_in['b2']}
    _x0 = _d['L0_attn_x']
    _d['L0_attn_x'] = jax.random.normal(jax.random.fold_in(jax.random.key(seed), 1), (4, 512, 128), dtype=_x0.dtype)
    del _x0
    return _d

def reference(L0_attn_x, L0_attn_W_disp, L0_attn_W_val, L0_attn_rel_pos_emb, L0_attn_W_strain, L0_attn_W_pos, L0_attn_W_bond, L0_attn_W_dmg, L0_attn_b_dmg, L0_attn_W_dmg_out, L0_attn_b_dmg_out, L0_attn_W_cproj, L0_ffn_scale, L0_ffn_gate_w, L0_ffn_gate_b, L0_ffn_mlp1_w, L0_ffn_mlp1_b, L0_ffn_mlp2_w, L0_ffn_mlp2_b, L1_attn_w_qkv, L1_attn_w_out, L1_ffn_rw1, L1_ffn_rb1, L1_ffn_rw2, L1_ffn_rb2, L1_ffn_W1, L1_ffn_b1, L1_ffn_W2, L1_ffn_b2):

    def _L0_attn_ref(x, W_disp, W_val, rel_pos_emb, W_strain, W_pos, W_bond, W_dmg, b_dmg, W_dmg_out, b_dmg_out, W_cproj):
        import jax, jax.numpy as jnp
        import numpy as np
        N_EMBD = 128
        N_HEAD = 16
        HORIZON = 64
        HS = N_EMBD // N_HEAD
        BD = max(HS // 4, 16)

        def _windows(t, delta):
            B, nh, T, D = t.shape
            padded = jnp.pad(t, ((0, 0), (0, 0), (delta - 1, 0), (0, 0)))
            idx = jnp.arange(T)[:, None] + jnp.arange(delta)[None, :]
            return padded[:, :, idx]
        B, T, C = x.shape
        nh, bd, hs = (N_HEAD, BD, HS)
        delta = min(HORIZON, T)
        disp = (x @ W_disp).reshape(B, T, nh, bd).transpose(0, 2, 1, 3)
        val = (x @ W_val).reshape(B, T, nh, hs).transpose(0, 2, 1, 3)
        disp_win = _windows(disp, delta)
        val_win = _windows(val, delta)
        cmask = jnp.arange(T)[:, None] - delta + 1 + jnp.arange(delta)[None, :] >= 0
        strain = disp_win - disp[:, :, :, None, :]
        rel_emb = rel_pos_emb[:delta]
        bond_act = jax.nn.gelu(strain @ W_strain + rel_emb @ W_pos, approximate=False)
        bond_logits = (bond_act @ W_bond)[..., 0]
        damage_act = jax.nn.gelu(strain @ W_dmg + b_dmg, approximate=False)
        damage = jax.nn.sigmoid((damage_act @ W_dmg_out)[..., 0] + b_dmg_out[0])
        logits = bond_logits - 10.0 * damage
        logits = jnp.where(cmask[None, None], logits, -jnp.inf)
        weights = jax.nn.softmax(logits, axis=-1)
        out = jnp.einsum('bntd,bntde->bnte', weights, val_win)
        out = out.transpose(0, 2, 1, 3).reshape(B, T, C)
        return out @ W_cproj

    def _L0_ffn_ref(x, scale, gate_w, gate_b, mlp1_w, mlp1_b, mlp2_w, mlp2_b):
        import jax, jax.numpy as jnp
        import numpy as np
        ALPHA = 1.702
        LIMIT = 7.0
        EPS = 1e-05
        E = 16
        K = 4

        def _swiglu(h):
            x_glu = jnp.minimum(h[..., ::2], LIMIT)
            x_lin = jnp.clip(h[..., 1::2], LIMIT, LIMIT)
            return x_glu * jax.nn.sigmoid(ALPHA * x_glu) * (x_lin + 1.0)
        t = x * jax.lax.rsqrt(jnp.mean(x * x, axis=-1, keepdims=True) + EPS) * scale
        g = jnp.einsum('bth,eh->bte', t, gate_w) + gate_b
        vals, idx = jax.lax.top_k(g, K)
        w = jax.nn.softmax(vals, axis=-1)
        route = jnp.sum(jax.nn.one_hot(idx, E, dtype=t.dtype) * w[..., None], axis=-2)
        route_e = jnp.moveaxis(route, -1, 0)

        def step(acc, p):
            w1, b1, w2, b2, r = p
            h = jnp.einsum('bth,ih->bti', t, w1) + b1
            s = _swiglu(h)
            y = jnp.einsum('bti,hi->bth', s, w2) + b2
            return (acc + r[..., None] * y, None)
        acc, _ = jax.lax.scan(step, jnp.zeros_like(x), (mlp1_w, mlp1_b, mlp2_w, mlp2_b, route_e))
        return x + acc

    def _L1_attn_ref(x, w_qkv, w_out):
        import jax, jax.numpy as jnp
        import numpy as np
        N_FILTERS = 128
        N_HEADS = 16
        b, n, c = x.shape
        h = N_HEADS
        d = c // h
        qkv = jnp.einsum('bnc,ce->bne', x, w_qkv)
        q, k, v = jnp.split(qkv, 3, axis=-1)
        to_heads = lambda t: t.reshape(b, n, h, d).transpose(0, 2, 1, 3)
        q, k, v = (to_heads(q), to_heads(k), to_heads(v))
        scale = jnp.sqrt(jnp.asarray(c, jnp.float32))
        attn = jnp.einsum('bhnd,bhmd->bhnm', q, k) / scale
        attn = jax.nn.softmax(attn, axis=-1)
        out = jnp.einsum('bhnm,bhmd->bhnd', attn, v)
        out = out.transpose(0, 2, 1, 3).reshape(b, n, c)
        return jnp.einsum('bnc,co->bno', out, w_out)

    def _L1_ffn_ref(inputs, rw1, rb1, rw2, rb2, W1, b1, W2, b2):
        import jax, jax.numpy as jnp
        import numpy as np
        EMBED = 128
        D_FF = 4 * EMBED
        N_EXPERTS = 8
        TOP_K = 2
        B, S = (2, 128)
        Bb, Ss, D = inputs.shape
        T = Bb * Ss
        xf = inputs.reshape(T, D)
        score = jax.nn.relu(xf @ rw1 + rb1) @ rw2 + rb2
        _, topi = jax.lax.top_k(score, TOP_K)
        mask = jnp.zeros(score.shape, bool).at[jnp.arange(T)[:, None], topi].set(True)
        gate = jax.nn.softmax(jnp.where(mask, score, -jnp.inf), axis=-1)
        out = jnp.zeros_like(xf)
        for e in range(N_EXPERTS):
            h = jax.nn.relu(xf @ W1[e] + b1[e])
            y = h @ W2[e] + b2[e]
            out = out + gate[:, e:e + 1] * y
        return out.reshape(Bb, Ss, D)
    x = L0_attn_x
    xn = _layernorm(x, axis=-1)
    x = x + _L0_attn_ref(xn, L0_attn_W_disp, L0_attn_W_val, L0_attn_rel_pos_emb, L0_attn_W_strain, L0_attn_W_pos, L0_attn_W_bond, L0_attn_W_dmg, L0_attn_b_dmg, L0_attn_W_dmg_out, L0_attn_b_dmg_out, L0_attn_W_cproj) + _L0_ffn_ref(xn, L0_ffn_scale, L0_ffn_gate_w, L0_ffn_gate_b, L0_ffn_mlp1_w, L0_ffn_mlp1_b, L0_ffn_mlp2_w, L0_ffn_mlp2_b)
    xn = _layernorm(x, axis=-1)
    x = x + _L1_attn_ref(xn, L1_attn_w_qkv, L1_attn_w_out) + _L1_ffn_ref(xn, L1_ffn_rw1, L1_ffn_rb1, L1_ffn_rw2, L1_ffn_rb2, L1_ffn_W1, L1_ffn_b1, L1_ffn_W2, L1_ffn_b2)
    return x

_drawn_inputs = setup_inputs


def setup_inputs(seed=0):
    import zlib

    import numpy as np

    out = dict(_drawn_inputs(seed))
    spreads = {'L0_attn_b_dmg': (0.0, 2.0),
     'L0_ffn_scale': (1.0, 0.2),
     'L0_ffn_gate_b': (0.0, 0.1),
     'L1_ffn_rb1': (0.0, 0.1),
     'L1_ffn_rb2': (0.0, 0.1),
     'L1_ffn_b1': (0.0, 0.323),
     'L1_ffn_b2': (0.0, 0.1)}
    factors = {'L0_attn_W_disp': 8.0,
     'L0_attn_W_val': 6.228,
     'L0_attn_rel_pos_emb': 26.751,
     'L0_attn_W_strain': 8.0,
     'L0_attn_W_pos': 29.101,
     'L0_attn_W_bond': 8.0,
     'L0_attn_W_dmg': 8.0,
     'L0_attn_W_dmg_out': 8.0,
     'L0_attn_W_cproj': 4.67,
     'L0_ffn_mlp1_b': 4.124,
     'L0_ffn_mlp2_b': 3.544,
     'L1_attn_w_qkv': 8.0,
     'L1_attn_w_out': 8.0}
    for name, (base, spread) in spreads.items():
        noise = np.random.default_rng([zlib.crc32(name.encode()), seed]).standard_normal(out[name].shape)
        drawn = base * np.exp(spread * noise) if base else spread * noise
        out[name] = jnp.asarray(drawn.astype(out[name].dtype))
    for name, factor in factors.items():
        out[name] = (out[name] * factor).astype(out[name].dtype)
    return out
```

```python
from contextlib import ExitStack

import concourse.bass as bass
from concourse import mybir

F32 = mybir.dt.float32
F32R = mybir.dt.float32r
ALU = mybir.AluOpType
ACT = mybir.ActivationFunctionType
AX = mybir.AxisListType

P = 128
B, T, C = 4, 512, 128
NT = T // P
TT = B * NT
H0, BD, HS = 16, 16, 8
WIN = 64
G = 2
HG = H0 // G
PAD = WIN - 1
TP = PAD + T + 1
JQ = WIN // 4
E0, K0, I0 = 16, 4, 128
LIMIT, ALPHA = 7.0, 1.702
H1, HD = 16, 8
HQ = 4
E1, K1, FF = 8, 2, 512
FQ = FF // P
EPS = 1e-5
MASKED = -3.0e38
RING = 4
SCALE1 = float(C) ** -0.5


class Count:

    def __init__(self, sem):
        self.sem, self.n = sem, 0

    def inc(self, instruction, by=1):
        instruction.then_inc(self.sem, by)
        self.n += by
        return self.n


def chain_of(engine, count):

    def link(instruction):
        engine.wait_ge(count.sem, count.inc(instruction))

    return link


def dram_rows(tensor, offset, dims):
    return bass.AP(tensor=tensor.tensor, offset=tensor.offset + offset, ap=dims)


def build(nc, t_in, out):
    ctx = ExitStack()
    with ctx:
        def sb(name, shape, dt=F32, where=ctx):
            return where.enter_context(nc.sbuf_tensor(name, shape, dt))

        def psum(name, shape, where=ctx):
            return where.enter_context(nc.psum_tensor(name, shape, F32))

        def sem(name):
            return ctx.enter_context(nc.semaphore(name))

        ident = sb("ident", [P, P])
        ACC = sb("ACC", [P, TT, C])
        nhalf = sb("nhalf", [P, TT])
        stats = sb("stats", [P, TT, 6])
        mv = sb("mv", [P, TT, 2])
        rstd = sb("rstd", [P, TT])

        with ExitStack() as l0:
            first_layer(nc, t_in, l0, sb, psum, sem, ident, ACC, nhalf, stats, mv, rstd)
        with ExitStack() as l1:
            second_layer(nc, t_in, out, l1, sb, psum, sem, ident, ACC, nhalf, stats, mv, rstd)


def top_k_route(v, link, scores, route, m8, gt, eq, c0, c1, small, n_exp, k, exp_ready, exp_done):
    n = scores.shape[1]
    for t in range(n):
        last = v.max(m8[:, t, :], scores[:, t, :])
    link(last)
    full = [P, n, n_exp]
    kth = m8[:, :, k - 1:k].to_broadcast(full)
    v.tensor_tensor(gt[:], scores[:], kth, ALU.is_gt)
    link(v.tensor_tensor(eq[:], scores[:], kth, ALU.is_equal))
    v.tensor_reduce(small[:, 0, :], gt[:], AX.X, ALU.add)
    src, dst = eq, c0
    step = 1
    while step < n_exp:
        v.tensor_copy(dst[:, :, 0:step], src[:, :, 0:step])
        link(v.tensor_tensor(dst[:, :, step:], src[:, :, step:], src[:, :, :n_exp - step], ALU.add))
        src, dst = dst, (c1 if dst is c0 else c0)
        step *= 2
    link(v.tensor_scalar(small[:, 1, :], small[:, 0, :], -1.0, float(k), ALU.mult, ALU.add))
    need = small[:, 1, :].unsqueeze(2).to_broadcast(full)
    link(v.tensor_tensor(dst[:], src[:], need, ALU.is_le))
    link(v.tensor_tensor(dst[:], dst[:], eq[:], ALU.mult))
    link(v.tensor_tensor(gt[:], gt[:], dst[:], ALU.add))
    v.tensor_tensor(route[:], scores[:], m8[:, :, 0:1].to_broadcast(full), ALU.subtract).then_inc(exp_ready, 1)
    v.wait_ge(exp_done, 1)
    link(v.tensor_tensor(route[:], route[:], gt[:], ALU.mult))
    link(v.tensor_reduce(small[:, 0, :], route[:], AX.X, ALU.add))
    link(v.reciprocal(small[:, 1, :], small[:, 0, :]))
    return v.tensor_tensor(route[:], route[:], small[:, 1, :].unsqueeze(2).to_broadcast(full), ALU.mult)


def first_layer(nc, t_in, l0, sb, psum, sem, ident, ACC, nhalf, stats, mv, rstd):
    x = t_in["L0_attn_x"].rearrange("b t c -> (b t) c").rearrange("(n p) c -> p n c", p=P)
    nv, ns, ng, npl, nt = nc.vector, nc.scalar, nc.gpsimd, nc.gpsimd, nc.tensor

    xnT = sb("xnT", [P, B, TP], F32, l0)
    tT = sb("tT", [P, B, T], F32, l0)
    w1T = sb("w1T", [P, E0, I0], F32, l0)
    w2T = sb("w2T", [P, E0, C], F32, l0)
    b1T = sb("b1T", [P, E0], F32, l0)
    route = sb("route", [P, TT, E0], F32, l0)
    wad = sb("wad", [P, G, 2, P], F32, l0)
    PT = sb("PT", [P, WIN], F32, l0)
    lred = sb("lred", [P, 2, 4, 32], F32, l0)
    mz = sb("mz", [P, JQ, WIN], F32, l0)
    bdmg = sb("bdmg", [P, 1], F32, l0)
    bdo = sb("bdo", [P, 1], F32, l0)
    wval = sb("wval", [P, C], F32, l0)
    wcp = sb("wcp", [P, G, C], F32, l0)
    lones = sb("lones", [P, 4, 32], F32, l0)
    AD = sb("AD", [P, 2, B, TP], F32, l0)
    attT = sb("attT", [P, G, 2, T], F32, l0)
    vp = sb("vp", [P, 8, HG, 32], F32, l0)
    Z = sb("Z", [P, JQ, T], F32, l0)

    d_x = [sem(f"d_x{b}") for b in range(B)]
    d_attn_w, d_gate_w, d_mlp_w, d_band0 = sem("d_attn_w"), sem("d_gate_w"), sem("d_mlp_w"), sem("d_band0")
    band = nc.dram_tensor("band", [2, 2, 32, 64, P], F32, kind="Internal").ap()

    with ExitStack() as su:
        X = sb("X", [P, TT, C], F32, su)
        XN = sb("XN", [P, TT, C], F32, su)
        TF = sb("TF", [P, TT, C], F32, su)
        w1r = sb("w1r", [P, E0, C], F32, su)
        w2r = sb("w2r", [P, E0, C], F32, su)
        b1r = sb("b1r", [E0, 2 * I0], F32, su)
        b2r = sb("b2r", [E0, C], F32, su)
        wdisp = sb("wdisp", [P, G, P], F32, su)
        wdispT = sb("wdispT", [P, G, P], F32, su)
        wrep = sb("wrep", [P, 2, BD], F32, su)
        wcol = sb("wcol", [P, 2], F32, su)
        wblk = sb("wblk", [P, 2, HG, BD], F32, su)
        rel = sb("rel", [WIN, BD], F32, su)
        relT = sb("relT", [BD, WIN], F32, su)
        wpos = sb("wpos", [BD, HG, BD], F32, su)
        gw = sb("gw", [E0, C], F32, su)
        gwT = sb("gwT", [P, E0], F32, su)
        gb = sb("gb", [P, E0], F32, su)
        scl = sb("scl", [P, 1], F32, su)
        mask8 = sb("mask8", [P, HG], F32, su)
        ones8 = sb("ones8", [P, HG], F32, su)
        mt = sb("mt", [WIN, WIN], F32, su)
        mt2 = sb("mt2", [WIN, JQ, 32, 4], F32, su)
        zero = sb("zero", [P, 2048], F32, su)
        ss = sb("ss", [P, TT], F32, su)
        r2 = sb("r2", [P, TT], F32, su)
        gsc = sb("gsc", [P, TT, E0], F32, su)
        m8 = sb("m8", [P, TT, 8], F32, su)
        gt = sb("gt", [P, TT, E0], F32, su)
        eq = sb("eq", [P, TT, E0], F32, su)
        c0 = sb("c0", [P, TT, E0], F32, su)
        c1 = sb("c1", [P, TT, E0], F32, su)
        small = sb("small", [P, 2, TT], F32, su)
        routeT = sb("routeT", [E0, TT, P], F32, su)
        S = [psum(f"su{i}", [P, 512], su) for i in range(8)]
        block = su.enter_context(nc.Block())

        s_pool, s_dve = Count(sem("su_pool")), Count(sem("su_dve"))
        mv_ready, rstd_ready, ss_ready, r2_ready = (sem(n) for n in ("mv_ready", "rstd_ready", "ss_ready", "r2_ready"))
        const_ready, xn_ready, tf_ready = sem("const_ready"), sem("xn_ready"), sem("tf_ready")
        blk_ready, zero_ready, mt_ready = sem("blk_ready"), sem("zero_ready"), sem("mt_ready")
        xnT_pe, tT_pe, xnT_sb, tT_sb = sem("xnT_pe"), sem("tT_pe"), sem("xnT_sb"), sem("tT_sb")
        wt_pe, wt_sb, wad_pe, wad_sb = sem("wt_pe"), sem("wt_sb"), sem("wad_pe"), sem("wad_sb")
        gate_pe, exp_ready, exp_done, route_ready = sem("gate_pe"), sem("exp_ready"), sem("exp_done"), sem("route_ready")
        misc_pe, misc_sb, mlp_pe, mlp_sb = sem("misc_pe"), sem("misc_sb"), sem("mlp_pe"), sem("mlp_sb")
        mzt_pe, mzt_sb, rt_pe, rt_sb, b2_pe, b2_sb = (sem(n) for n in ("mzt_pe", "mzt_sb", "rt_pe", "rt_sb", "b2_pe", "b2_sb"))

        @block.sync
        def _(sp):
            for b in range(B):
                sp.dma_start(X[:, NT * b:NT * b + NT, :], x[:, NT * b:NT * b + NT, :]).then_inc(d_x[b], 16)
            wd = t_in["L0_attn_W_disp"]
            with nc.allow_non_contiguous_dma(reason="small weights"):
                sp.dma_start(wdisp[:], wd.rearrange("k (g n) -> k g n", g=G)).then_inc(d_attn_w, 16)
                for s, n in enumerate(("L0_attn_W_strain", "L0_attn_W_dmg")):
                    sp.dma_start(wrep[:, s, :], dram_rows(t_in[n], 0, [[0, HG], [BD, BD], [1, BD]])).then_inc(d_attn_w, 16)
                for s, n in enumerate(("L0_attn_W_bond", "L0_attn_W_dmg_out")):
                    sp.dma_start(wcol[:, s:s + 1], dram_rows(t_in[n], 0, [[0, HG], [1, BD], [1, 1]])).then_inc(d_attn_w, 16)
                sp.dma_start(bdmg[:], dram_rows(t_in["L0_attn_b_dmg"], 0, [[0, HG], [1, BD], [1, 1]])).then_inc(d_attn_w, 16)
                sp.dma_start(bdo[:], dram_rows(t_in["L0_attn_b_dmg_out"], 0, [[0, P], [1, 1]])).then_inc(d_attn_w, 16)
                sp.dma_start(rel[:], t_in["L0_attn_rel_pos_emb"]).then_inc(d_attn_w, 16)
                sp.dma_start(wpos[:], dram_rows(t_in["L0_attn_W_pos"], 0, [[BD, BD], [0, HG], [1, BD]])).then_inc(d_attn_w, 16)
                sp.dma_start(wval[:], t_in["L0_attn_W_val"]).then_inc(d_attn_w, 16)
                for half in range(2):
                    sp.dma_start(wcp[64 * half:64 * half + 64, :, :],
                                 t_in["L0_attn_W_cproj"].rearrange("(g r) n -> r g n", g=G)).then_inc(d_attn_w, 16)
                sp.dma_start(gw[:], t_in["L0_ffn_gate_w"]).then_inc(d_gate_w, 16)
                sp.dma_start(gb[:], dram_rows(t_in["L0_ffn_gate_b"], 0, [[0, P], [1, E0]])).then_inc(d_gate_w, 16)
                sp.dma_start(scl[:], dram_rows(t_in["L0_ffn_scale"], 0, [[1, P], [1, 1]])).then_inc(d_gate_w, 16)
                sp.dma_start(w1r[:], dram_rows(t_in["L0_ffn_mlp1_w"], 0, [[2 * C, I0], [2 * I0 * C, E0], [1, C]])).then_inc(d_mlp_w, 16)
                sp.dma_start(w2r[:], t_in["L0_ffn_mlp2_w"].rearrange("e h i -> h e i")).then_inc(d_mlp_w, 16)
                sp.dma_start(b1r[:], t_in["L0_ffn_mlp1_b"]).then_inc(d_mlp_w, 16)
                sp.dma_start(b2r[:], t_in["L0_ffn_mlp2_b"]).then_inc(d_mlp_w, 16)
            sp.wait_ge(zero_ready, 1)
            flat = band.rearrange("a k n r s -> (a k n r s)").rearrange("(p f) -> p f", p=P)
            for i in range(4):
                sp.dma_start(flat[:, 2048 * i:2048 * i + 2048], zero[:]).then_inc(d_band0, 16)
            sp.wait_ge(d_band0, 64)

        @block.gpsimd
        def _(pool):
            link = chain_of(pool, s_pool)
            link(pool.memset(ident[:], 0.0))
            pool.affine_select(out=ident[:], in_=ident[:], compare_op=ALU.not_equal, fill=1.0, base=0,
                               pattern=[[-1, P]], channel_multiplier=1).then_inc(const_ready, 1)
            pool.memset(nhalf[:], -0.5)
            link(pool.memset(ones8[:], 1.0))
            link(pool.affine_select(out=mask8[:], in_=ones8[:], compare_op=ALU.is_ge, fill=0.0, base=0,
                                    pattern=[[-BD, HG]], channel_multiplier=1))
            pool.affine_select(out=mask8[:], in_=mask8[:], compare_op=ALU.is_ge, fill=0.0, base=BD - 1,
                               pattern=[[BD, HG]], channel_multiplier=-1).then_inc(const_ready, 1)
            link(pool.memset(zero[:], 0.0))
            link(pool.affine_select(out=mt[:], in_=zero[0:WIN, 0:WIN], compare_op=ALU.is_ge, fill=MASKED,
                                    base=-PAD, pattern=[[1, WIN]], channel_multiplier=1))
            pool.tensor_copy(mt2[:], mt[:].rearrange("t (q j) -> t q j", j=4).unsqueeze(2).to_broadcast([WIN, JQ, 32, 4])
                             ).then_inc(mt_ready, 1)
            pool.memset(lones[:], 0.0)
            link(pool.memset(vp[:], 0.0))
            for hh in range(4):
                last = pool.memset(lones[:, hh, 8 * hh:8 * hh + 8], 1.0)
            link(last)
            pool.memset(AD[:, :, :, 0:PAD], 0.0)
            pool.memset(AD[:, :, :, PAD + T:TP], 0.0)
            pool.memset(xnT[:, :, 0:PAD], 0.0)
            pool.memset(xnT[:, :, PAD + T:TP], 0.0).then_inc(zero_ready, 1)
            pool.wait_ge(mv_ready, 1)
            link(pool.tensor_scalar(rstd[:], mv[:, :, 1], EPS, 1.0, ALU.add, ALU.mult))
            pool.tensor_tensor(rstd[:], rstd[:], nhalf[:], ALU.pow).then_inc(rstd_ready, 1)
            pool.wait_ge(ss_ready, 1)
            link(pool.tensor_scalar(r2[:], ss[:], 1.0 / C, EPS, ALU.mult, ALU.add))
            pool.tensor_tensor(r2[:], r2[:], nhalf[:], ALU.pow).then_inc(r2_ready, 1)

        @block.vector
        def _(v):
            link = chain_of(v, s_dve)
            for b in range(B):
                v.wait_ge(d_x[b], 16)
                for t in range(NT * b, NT * b + NT):
                    last = v.bn_stats(stats[:, t, :], X[:, t, :])
            link(last)
            for t in range(TT):
                last = v.bn_aggr(mv[:, t, :], stats[:, t, :])
            last.then_inc(mv_ready, 1)
            v.wait_ge(d_attn_w, 16 * 12)
            v.wait_ge(const_ready, 2)
            for s in range(2):
                v.tensor_tensor(wblk[:, s, :, :], wrep[:, s, :].unsqueeze(1).to_broadcast([P, HG, BD]),
                                mask8[:].unsqueeze(2).to_broadcast([P, HG, BD]), ALU.mult)
            link(v.memset(lred[:], 0.0))
            for s in range(2):
                for a in range(4):
                    last = v.tensor_scalar(lred[:, s, a, a:32:4], mask8[:], wcol[:, s:s + 1], None, ALU.mult)
            v.tensor_scalar(bdo[:], bdo[:], 0.5, None, ALU.mult).then_inc(blk_ready, 1)
            v.wait_ge(rstd_ready, 1)
            for t in range(TT):
                last = v.tensor_scalar(XN[:, t, :], X[:, t, :], mv[:, t, 0:1], rstd[:, t:t + 1], ALU.subtract, ALU.mult)
            last.then_inc(xn_ready, 1)
            v.wait_ge(xn_ready, 1)
            for t in range(TT):
                last = v.tensor_tensor_reduce(TF[:, t, :], XN[:, t, :], XN[:, t, :], 1.0, 0.0, ALU.mult, ALU.add,
                                              ss[:, t:t + 1])
            last.then_inc(ss_ready, 1)
            link(v.tensor_tensor(ACC[:], X[:], XN[:], ALU.add))
            v.wait_ge(r2_ready, 1)
            v.wait_ge(ss_ready, 1)
            for t in range(TT):
                last = v.tensor_scalar(TF[:, t, :], XN[:, t, :], r2[:, t:t + 1], None, ALU.mult)
            last.then_inc(tf_ready, 1)
            v.wait_ge(misc_pe, 1)
            v.tensor_copy(gwT[:], S[0][:, 0:E0])
            v.tensor_copy(relT[:], S[0][0:BD, 64:64 + WIN])
            v.tensor_copy(b1T[:], S[0][:, 128:128 + E0]).then_inc(misc_sb, 1)
            v.wait_ge(misc_pe, 2)
            v.tensor_copy(PT[:], S[0][:, 256:256 + WIN]).then_inc(misc_sb, 1)
            v.wait_ge(gate_pe, 1)
            v.wait_ge(d_gate_w, 48)
            link(v.tensor_tensor(gsc[:], S[1][:, 0:TT * E0].rearrange("p (t e) -> p t e", e=E0),
                                 gb[:].unsqueeze(1).to_broadcast([P, TT, E0]), ALU.add))
            top_k_route(v, link, gsc, route, m8, gt, eq, c0, c1, small, E0, K0, exp_ready, exp_done).then_inc(route_ready, 1)
            for i in range(4):
                v.wait_ge(rt_pe, i + 1)
                v.tensor_copy(routeT[:, 4 * i:4 * i + 4, :].rearrange("e t p -> e (t p)"), S[2 + i % 2][0:E0, :]).then_inc(rt_sb, 1)
            for i in range(4):
                v.wait_ge(b2_pe, i + 1)
                a = ACC[:, 4 * i:4 * i + 4, :].rearrange("p t c -> p (t c)")
                v.tensor_tensor(a, a, S[2 + i % 2][:, :], ALU.add).then_inc(b2_sb, 1)

        @block.scalar
        def _(act):
            for b in range(B):
                act.wait_ge(xnT_pe, b + 1)
                act.copy(xnT[:, b, PAD:PAD + T], S[2 + b][:, :]).then_inc(xnT_sb, 1)
            act.wait_ge(wt_pe, 1)
            act.copy(wdispT[:], S[6][:, 0:G * P]).then_inc(wt_sb, 1)
            act.wait_ge(wad_pe, 1)
            act.copy(wad[:], S[7][:]).then_inc(wad_sb, 1)
            act.wait_ge(d_gate_w, 48)
            for b in range(B):
                act.wait_ge(tT_pe, b + 1)
                act.activation(tT[:, b, :], S[2 + b][:, :], ACT.Copy, scale=scl[:, 0:1]).then_inc(tT_sb, 1)
            act.wait_ge(exp_ready, 1)
            act.activation(route[:], route[:], ACT.Exp).then_inc(exp_done, 1)
            for i in range(8):
                act.wait_ge(mlp_pe, i + 1)
                dst, e = (w1T, 4 * i) if i < 4 else (w2T, 4 * i - 16)
                act.activation(dst[:, e:e + 4, :].rearrange("p e c -> p (e c)"), S[6 + i % 2][:, :], ACT.Copy,
                               scale=1.0 if i < 4 else (LIMIT + 1.0) / 2).then_inc(mlp_sb, 1)
            for i in range(4):
                act.wait_ge(mzt_pe, i + 1)
                act.copy(mz[:, 4 * i:4 * i + 4, :].rearrange("p q t -> p (q t)"), S[4 + i % 2][:, 0:256]).then_inc(mzt_sb, 1)

        @block.tensor
        def _(pe):
            pe.wait_ge(const_ready, 1)
            pe.wait_ge(d_attn_w, 16 * 12)
            for g in range(G):
                last = pe.transpose(S[6][:, P * g:P * g + P], wdisp[:, g, :], ident[:])
            last.then_inc(wt_pe, 1)
            pe.wait_ge(d_gate_w, 48)
            pe.wait_ge(d_mlp_w, 64)
            pe.transpose(S[0][:, 0:E0], gw[:], ident[0:E0, 0:E0])
            pe.transpose(S[0][0:BD, 64:64 + WIN], rel[:], ident[0:WIN, 0:WIN])
            pe.transpose(S[0][:, 128:128 + E0], b1r[:, 0:2 * I0:2], ident[0:E0, 0:E0]).then_inc(misc_pe, 1)
            pe.wait_ge(xn_ready, 1)
            for b in range(B):
                for i in range(NT):
                    last = pe.transpose(S[2 + b][:, P * i:P * i + P], XN[:, NT * b + i, :], ident[:])
                last.then_inc(xnT_pe, 1)
            pe.wait_ge(wt_sb, 1)
            pe.wait_ge(blk_ready, 1)
            for g in range(G):
                for s in range(2):
                    at = P * (2 * g + s)
                    last = pe.matmul(S[7][:, at:at + P], wdispT[:, g, :], wblk[:, s, :, :].rearrange("p h c -> p (h c)"),
                                     start=True, stop=True)
            last.then_inc(wad_pe, 1)
            pe.wait_ge(tf_ready, 1)
            for b in range(B):
                pe.wait_ge(xnT_sb, b + 1)
                for i in range(NT):
                    last = pe.transpose(S[2 + b][:, P * i:P * i + P], TF[:, NT * b + i, :], ident[:])
                last.then_inc(tT_pe, 1)
            pe.wait_ge(misc_sb, 1)
            pe.matmul(S[0][:, 256:256 + WIN], wpos[:].rearrange("k h c -> k (h c)"), relT[:], start=True, stop=True).then_inc(misc_pe, 1)
            pe.wait_ge(tT_sb, B)
            for t in range(TT):
                last = pe.matmul(S[1][:, E0 * t:E0 * t + E0], tT[:, t // NT, P * (t % NT):P * (t % NT) + P], gwT[:],
                                 start=True, stop=True)
            last.then_inc(gate_pe, 1)
            pe.wait_ge(wad_sb, 1)
            for i in range(8):
                if i >= 2:
                    pe.wait_ge(mlp_sb, i - 1)
                src, e = (w1r, 4 * i) if i < 4 else (w2r, 4 * i - 16)
                for n in range(4):
                    last = pe.transpose(S[6 + i % 2][:, P * n:P * n + P], src[:, e + n, :], ident[:])
                last.then_inc(mlp_pe, 1)
            pe.wait_ge(mt_ready, 1)
            for i in range(4):
                if i >= 2:
                    pe.wait_ge(mzt_sb, i - 1)
                for n in range(4):
                    last = pe.transpose(S[4 + i % 2][:, WIN * n:WIN * n + WIN],
                                        mt2[:, 4 * i + n, :, :].rearrange("t n j -> t (n j)"), ident[0:WIN, 0:WIN])
                last.then_inc(mzt_pe, 1)
            pe.wait_ge(route_ready, 1)
            for i in range(4):
                if i >= 2:
                    pe.wait_ge(rt_sb, i - 1)
                for n in range(4):
                    last = pe.transpose(S[2 + i % 2][0:E0, P * n:P * n + P], route[:, 4 * i + n, :], ident[:])
                last.then_inc(rt_pe, 1)
            pe.wait_ge(rt_sb, 4)
            for i in range(4):
                if i >= 2:
                    pe.wait_ge(b2_sb, i - 1)
                for n in range(4):
                    last = pe.matmul(S[2 + i % 2][:, P * n:P * n + P], routeT[:, 4 * i + n, :], b2r[:], start=True, stop=True)
                last.then_inc(b2_pe, 1)

    items_reduced, banks_free = sem("items_reduced"), sem("banks_free")
    strain_ready, gelu_done, th_ready = sem("strain_ready"), sem("gelu_done"), sem("th_ready")
    w1_staged, h_ready, xg_ready, sig_ready, s_ready, y_ready, y_used = (
        sem(n) for n in ("w1_staged", "h_ready", "xg_ready", "sig_ready", "s_ready", "y_ready", "y_used"))
    ad_pe, ad_sb = sem("ad_pe"), sem("ad_sb")
    zm_ready, zt_ready, mx_ready, zs_ready, ex_ready = (sem(n) for n in ("zm_ready", "zt_ready", "mx_ready", "zs_ready", "ex_ready"))
    d_out = [sem("d_skew0"), sem("d_skew1")]
    d_in = [sem("d_band_in0"), sem("d_band_in1")]
    band_pe, band_act, band_dve, vw_pe, vw_sb, nd_pe, rc_ready, att_ready = (
        sem(n) for n in ("band_pe", "band_act", "band_dve", "vw_pe", "vw_sb", "nd_pe", "rc_ready", "att_ready"))
    cp_pe = sem("cp_pe")

    for g in range(G):
        with ExitStack() as lp:
            ring = sb(f"ring{g}", [P, RING, 2, B, T], F32, lp)
            xg = sb(f"xg{g}", [P, 2, T], F32, lp)
            t2 = sb(f"t2{g}", [P, 2, T], F32, lp)
            w1s = sb(f"w1s{g}", [P, I0], F32, lp)
            LG = psum(f"LG{g}", [P, 2, 2, T], lp)
            PH = psum(f"PH{g}", [P, 2, T], lp)
            PY = psum(f"PY{g}", [P, 2, 4, C], lp)
            block = lp.enter_context(nc.Block())
            N0 = g * WIN
            Q0 = g * JQ
            U0 = g * 32

            @block.gpsimd
            def _(pool):
                if g == 0:
                    pool.sem_inc(items_reduced, RING)
                    pool.sem_inc(banks_free, 2)
                    pool.sem_inc(y_used, 2)
                    pool.sem_inc(xg_ready, 1)
                def stage(it):
                    pool.tensor_copy(w1s[:], w1T[:, bass.ds(HG * g + it, 1), :]).then_inc(w1_staged, 1)
                stage(0)
                with pool.Fori(0, 7) as it:
                    pool.wait_ge(h_ready, U0 + 4 * it + 4)
                    stage(it + 1)

            @block.vector
            def _(v):
                for i in range(4):
                    v.wait_ge(ad_pe, 8 * g + 2 * i + 2)
                    v.tensor_copy(AD[:, i // 2, 2 * (i % 2) + 1, PAD:PAD + T], LG[:, i % 2, 1, :]).then_inc(ad_sb, 1)
                v.wait_ge(ad_sb, 8 * g + 8)

                def item(n, j):
                    slot = n % RING
                    v.wait_ge(items_reduced, N0 + j + 1)
                    for s, extra in ((0, PT[:, bass.ds(j, 1)]), (1, bdmg[:, 0:1])):
                        v.scalar_tensor_tensor(out=ring[:, slot, s, :, :], in0=AD[:, s, :, bass.ds(j, T)], scalar=extra,
                                               in1=AD[:, s, :, PAD:PAD + T], op0=ALU.add, op1=ALU.subtract
                                               ).then_inc(strain_ready, 1)

                def logits(par, q):
                    v.wait_ge(th_ready, Q0 + q + 1)
                    zq = Z[:, bass.ds(q, 1), :].rearrange("p o t -> p (o t)")
                    v.scalar_tensor_tensor(out=zq, in0=zq, scalar=-5.0, in1=LG[:, par, 0, :], op0=ALU.mult, op1=ALU.add
                                           ).then_inc(banks_free, 1)

                def glu_in(c, it, u):
                    v.wait_ge(h_ready, u + 1)
                    v.tensor_scalar(xg[:, c % 2, :], PH[:, c % 2, :], b1T[:, bass.ds(HG * g + it, 1)], LIMIT,
                                    ALU.add, ALU.min).then_inc(xg_ready, 1)

                def glu_out(c, u):
                    v.wait_ge(sig_ready, u + 1)
                    v.scalar_tensor_tensor(out=xg[:, c % 2, :], in0=t2[:, c % 2, :], scalar=1.0, in1=xg[:, c % 2, :],
                                           op0=ALU.add, op1=ALU.mult).then_inc(s_ready, 1)

                def combine(c, it, u):
                    v.wait_ge(y_ready, u + 1)
                    for i in range(4):
                        a = ACC[:, 4 * c + i, :]
                        ins = v.scalar_tensor_tensor(out=a, in0=PY[:, c % 2, i, :], scalar=route[:, 4 * c + i, bass.ds(HG * g + it, 1)],
                                                     in1=a, op0=ALU.mult, op1=ALU.add)
                    ins.then_inc(y_used, 1)

                def body(it, last=False):
                    j, u = 8 * it, U0 + 4 * it
                    glu_in(0, it, u)
                    item(2, j + 2)
                    glu_out(0, u)
                    item(3, j + 3)
                    glu_in(1, it, u + 1)
                    item(4, j + 4)
                    combine(0, it, u)
                    glu_out(1, u + 1)
                    item(5, j + 5)
                    logits(0, 2 * it)
                    glu_in(2, it, u + 2)
                    item(6, j + 6)
                    combine(1, it, u + 1)
                    glu_out(2, u + 2)
                    glu_in(3, it, u + 3)
                    item(7, j + 7)
                    combine(2, it, u + 2)
                    glu_out(3, u + 3)
                    if not last:
                        item(0, j + 8)
                        item(1, j + 9)
                    combine(3, it, u + 3)
                    logits(1, 2 * it + 1)

                item(0, 0)
                item(1, 1)
                with v.Fori(0, 7) as it:
                    body(it)
                body(7, True)

            @block.scalar
            def _(act):
                for i in range(4):
                    act.wait_ge(ad_pe, 8 * g + 2 * i + 1)
                    act.copy(AD[:, i // 2, 2 * (i % 2), PAD:PAD + T], LG[:, i % 2, 0, :]).then_inc(ad_sb, 1)

                def gelu(n, j):
                    slot = n % RING
                    act.wait_ge(strain_ready, 2 * (N0 + j) + 2)
                    act.activation(ring[:, slot], ring[:, slot], ACT.Gelu).then_inc(gelu_done, 1)

                def tanh(par, q):
                    act.wait_ge(items_reduced, RING + N0 + 4 * q + 4)
                    act.activation(Z[:, bass.ds(q, 1), :].rearrange("p o t -> p (o t)"), LG[:, par, 1, :], ACT.Tanh, bias=bdo[:, 0:1], scale=0.5).then_inc(th_ready, 1)

                def sig(c, u):
                    act.wait_ge(xg_ready, u + 2)
                    act.activation(t2[:, c % 2, :], xg[:, c % 2, :], ACT.Tanh, scale=ALPHA / 2).then_inc(sig_ready, 1)

                def body(it, last=False):
                    j, u = 8 * it, U0 + 4 * it
                    sig(0, u)
                    gelu(1, j + 1)
                    gelu(2, j + 2)
                    sig(1, u + 1)
                    gelu(3, j + 3)
                    gelu(4, j + 4)
                    tanh(0, 2 * it)
                    gelu(5, j + 5)
                    sig(2, u + 2)
                    gelu(6, j + 6)
                    sig(3, u + 3)
                    gelu(7, j + 7)
                    if not last:
                        gelu(0, j + 8)
                    tanh(1, 2 * it + 1)

                gelu(0, 0)
                with act.Fori(0, 7) as it:
                    body(it)
                body(7, True)

            @block.tensor
            def _(pe):
                for i in range(8):
                    s, b = i // 4, i % 4
                    bank = LG[:, (i // 2) % 2, i % 2, :]
                    if i >= 4:
                        pe.wait_ge(ad_sb, 8 * g + 4)
                    pe.matmul(bank, wad[:, g, s, :], xnT[:, b, PAD:PAD + T], start=True, stop=True).then_inc(ad_pe, 1)
                pe.wait_ge(ad_sb, 8 * g + 8)

                def reduce(n, j, q):
                    slot, par = n % RING, (n // 4) % 2
                    if n % 4 == 0:
                        pe.wait_ge(banks_free, Q0 + q + 1)
                    pe.wait_ge(gelu_done, N0 + j + 1)
                    for s in range(2):
                        for b in range(B):
                            mm = pe.matmul(LG[32 * b:32 * b + 32, par, s, :], lred[:, s, n % 4, :], ring[:, slot, s, b, :],
                                           start=(n % 4 == 0), stop=(n % 4 == 3))
                    mm.then_inc(items_reduced, 1)

                def hidden(c, u, staged):
                    pe.wait_ge(w1_staged, staged)
                    pe.wait_ge(xg_ready, u)
                    pe.matmul(PH[:, c % 2, :], w1s[:], tT[:, c, :], start=True, stop=True).then_inc(h_ready, 1)

                def expert_out(c, it, u):
                    pe.wait_ge(s_ready, u + 1)
                    pe.wait_ge(y_used, u + 1)
                    for i in range(4):
                        mm = pe.matmul(PY[:, c % 2, i, :], xg[:, c % 2, P * i:P * i + P], w2T[:, bass.ds(HG * g + it, 1), :].rearrange("p o c -> p (o c)"),
                                       start=True, stop=True)
                    mm.then_inc(y_ready, 1)

                def body(it, last=False):
                    j, u, w = 8 * it, U0 + 4 * it, HG * g + it + 1
                    reduce(0, j, 2 * it)
                    hidden(1, u + 1, w)
                    expert_out(0, it, u)
                    reduce(1, j + 1, 2 * it)
                    reduce(2, j + 2, 2 * it)
                    hidden(2, u + 2, w)
                    expert_out(1, it, u + 1)
                    reduce(3, j + 3, 2 * it)
                    hidden(3, u + 3, w)
                    reduce(4, j + 4, 2 * it + 1)
                    expert_out(2, it, u + 2)
                    reduce(5, j + 5, 2 * it + 1)
                    if not last:
                        hidden(0, u + 4, w + 1)
                    reduce(6, j + 6, 2 * it + 1)
                    expert_out(3, it, u + 3)
                    reduce(7, j + 7, 2 * it + 1)

                hidden(0, U0, HG * g + 1)
                with pe.Fori(0, 7) as it:
                    body(it)
                body(7, True)

        with ExitStack() as sm:
            zs = sb(f"zs{g}", [P, 2, 32, JQ, 4], F32, sm)
            wide = sb(f"wide{g}", [P, 2, 32, P], F32, sm)
            wtT = sb(f"wtT{g}", [P, 32, P], F32, sm)
            mx = sb(f"mx{g}", [P, 2, 32], F32, sm)
            rc = sb(f"rc{g}", [P, 2, P], F32, sm)
            ZT = psum(f"ZT{g}", [P, JQ, P], sm)
            W = [psum(f"W{g}{i}", [P, 4, P], sm) for i in range(4)]
            block = sm.enter_context(nc.Block())
            M0 = NT * g

            def steps(weigh, gather):
                weigh(0)
                for ti in range(1, NT):
                    weigh(ti)
                    gather(ti - 1)
                gather(NT - 1)

            @block.sync
            def _(sp):
                for ti in range(NT):
                    m, par = M0 + ti, ti % 2
                    sp.wait_ge(ex_ready, m + 1)
                    for k in range(2):
                        dst = dram_rows(band, (par * 2 + k) * 32 * 64 * P, [[P + 1, 64], [64 * P, 32], [1, WIN]])
                        sp.dma_start(dst, zs[64 * k:64 * k + 64, par].rearrange("r n q j -> r n (q j)")).then_inc(d_out[par], 16)
                    sp.wait_ge(d_out[par], 32 * (m // 2 + 1))
                    if ti >= 2:
                        sp.wait_ge(band_pe, 8 * (m - 1))
                    for k in range(2):
                        sp.dma_start(wide[64 * k:64 * k + 64, par], band[par, k].rearrange("n r s -> r n s")).then_inc(d_in[par], 16)

            @block.vector
            def _(v):
                zh = Z[:, :, 0:WIN]
                v.tensor_tensor(zh, zh, mz[:], ALU.add).then_inc(zm_ready, 1)

                def weigh(ti):
                    m, par = M0 + ti, ti % 2
                    v.wait_ge(zt_ready, m + 1)
                    zt = ZT[:].rearrange("p q (n j) -> p n q j", j=4)
                    v.tensor_reduce(mx[:, par], zt, AX.XY, ALU.max).then_inc(mx_ready, 1)
                    v.wait_ge(mx_ready, m + 1)
                    if ti >= 2:
                        v.wait_ge(d_out[par], 32 * (m // 2))
                    v.tensor_tensor(zs[:, par], zt, mx[:, par].unsqueeze(2).unsqueeze(3).to_broadcast([P, 32, JQ, 4]),
                                    ALU.subtract).then_inc(zs_ready, 1)

                def gather(ti):
                    m = M0 + ti
                    for i in range(1, 8, 2):
                        v.wait_ge(band_pe, 8 * m + i + 1)
                        v.tensor_copy(wtT[:, 4 * i:4 * i + 4, :], W[i % 2][:]).then_inc(band_dve, 1)
                    v.wait_ge(nd_pe, m + 1)
                    v.reciprocal(rc[:], W[3][:, 0:2, :]).then_inc(rc_ready, 1)
                    v.wait_ge(rc_ready, m + 1)
                    v.tensor_tensor(attT[:, g, :, P * ti:P * ti + P], W[3][:, 2:4, :], rc[:], ALU.mult).then_inc(att_ready, 1)

                steps(weigh, gather)

            @block.scalar
            def _(act):
                def weigh(ti):
                    m, par = M0 + ti, ti % 2
                    act.wait_ge(zs_ready, m + 1)
                    act.activation(zs[:, par], zs[:, par], ACT.Exp).then_inc(ex_ready, 1)

                def gather(ti):
                    m = M0 + ti
                    act.wait_ge(vw_pe, m + 1)
                    act.wait_ge(nd_pe, m)
                    for hh in range(4):
                        ins = act.copy(vp[:, :, hh:HG:4, 8 * hh:8 * hh + 8],
                                       W[2][:].rearrange("p a c -> p (a c)").rearrange("p (n h e) -> p n h e", n=8, e=HS)[:, :, hh:HG:4, :])
                    ins.then_inc(vw_sb, 1)
                    for i in range(0, 8, 2):
                        act.wait_ge(band_pe, 8 * m + i + 1)
                        act.copy(wtT[:, 4 * i:4 * i + 4, :], W[i % 2][:]).then_inc(band_act, 1)

                steps(weigh, gather)

            @block.tensor
            def _(pe):
                def weigh(ti):
                    m = M0 + ti
                    pe.wait_ge(zs_ready, m)
                    for q in range(JQ):
                        mm = pe.transpose(ZT[:, q, :], Z[:, q, P * ti:P * ti + P], ident[:])
                    mm.then_inc(zt_ready, 1)

                def gather(ti):
                    m, par = M0 + ti, ti % 2
                    pe.wait_ge(vw_sb, m)
                    for n in range(8):
                        b, k = n // 2, 2 * ti + n % 2
                        mm = pe.matmul(W[2][:].rearrange("p a c -> p (a c)")[:, 64 * n:64 * n + 64], xnT[:, b, 64 * k:64 * k + P],
                                       wval[:, 64 * g:64 * g + 64], start=True, stop=True)
                    mm.then_inc(vw_pe, 1)
                    pe.wait_ge(d_in[par], 32 * (m // 2 + 1))
                    for i in range(8):
                        pe.wait_ge(band_dve if i % 2 else band_act, 4 * m + i // 2)
                        for n in range(4):
                            mm = pe.transpose(W[i % 2][:, n, :], wide[:, par, 4 * i + n, :], ident[:])
                        mm.then_inc(band_pe, 1)
                    pe.wait_ge(band_act, 4 * m + 4)
                    pe.wait_ge(band_dve, 4 * m + 4)
                    pe.wait_ge(vw_sb, m + 1)
                    pe.wait_ge(att_ready, m)
                    for bb in range(2):
                        for hh in range(4):
                            for t4 in range(4):
                                b, qd = 2 * bb + t4 // 2, t4 % 2
                                n = HG * b + 4 * qd + hh
                                pe.matmul(W[3][32 * t4:32 * t4 + 32, bb, :], lones[:, hh, :], wtT[:, n, :],
                                          start=(hh == 0), stop=(hh == 3))
                    for bb in range(2):
                        for k in range(2):
                            for hh in range(4):
                                for t4 in range(4):
                                    b, qd = 2 * bb + t4 // 2, t4 % 2
                                    n = HG * b + 4 * qd + hh
                                    mm = pe.matmul(W[3][32 * t4:32 * t4 + 32, 2 + bb, 64 * k:64 * k + 64],
                                                   vp[:, 2 * b + k, 4 * qd + hh, :], wtT[:, n, 64 * k:64 * k + 64],
                                                   start=(hh == 0), stop=(hh == 3))
                    mm.then_inc(nd_pe, 1)

                pe.wait_ge(zm_ready, g + 1)
                steps(weigh, gather)

    with ExitStack() as cp:
        O = [psum(f"O{i}", [P, 4, C], cp) for i in range(4)]
        block = cp.enter_context(nc.Block())

        @block.tensor
        def _(pe):
            for b in range(B):
                r = 64 * (b % 2)
                for i in range(NT):
                    for g in range(G):
                        mm = pe.matmul(O[b][:, i, :], attT[r:r + 64, g, b // 2, P * i:P * i + P], wcp[r:r + 64, g, :],
                                       start=(g == 0), stop=(g == G - 1))
                mm.then_inc(cp_pe, 1)

        @block.vector
        def _(v):
            for b in range(B):
                v.wait_ge(cp_pe, b + 1)
                a = ACC[:, NT * b:NT * b + NT, :]
                v.tensor_tensor(a, a, O[b][:], ALU.add)


def second_layer(nc, t_in, out, l1, sb, psum, sem, ident, ACC, nhalf, stats, mv, rstd):
    xT = sb("xT", [P, B, T], F32, l1)
    W1 = sb("W1", [P, E1, FF], F32, l1)
    W2 = sb("W2", [P, E1, FQ, C], F32, l1)
    b1c = sb("b1c", [P, E1, FQ], F32, l1)
    rw1 = sb("rw1", [P, FF], F32, l1)
    rb1c = sb("rb1c", [P, FQ], F32, l1)
    rw2 = sb("rw2", [P, FQ, E1], F32, l1)
    wq = sb("wq", [P, HQ, 4, 4, 8], F32, l1)
    wk = sb("wk", [P, HQ, 4, 4, 8], F32, l1)
    wv = sb("wv", [P, C], F32, l1)
    wo = sb("wo", [P, HQ, C], F32, l1)
    gate = sb("gate", [P, TT, E1], F32, l1)
    gateT = sb("gateT", [E1, TT, P], F32, l1)
    b2r1 = sb("b2r1", [E1, C], F32, l1)
    neglo = sb("neglo", [P, 2], F32, l1)
    onesrow = sb("onesrow", [P, 1], F32, l1)
    zcol = sb("zcol", [P, 1], F32, l1)
    sel = sb("sel", [P, P], F32, l1)
    outd = out.rearrange("b t c -> (b t) c").rearrange("(n p) c -> p n c", p=P)

    d_w = [sem(f"l1_w{i}") for i in range(3)]
    with ExitStack() as su:
        wqkv = sb("wqkv", [P, 3, C], F32, su)
        XN = sb("XN2", [P, TT, C], F32, su)
        b1r = sb("b1r1", [E1 * FQ, P], F32, su)
        rb1r = sb("rb1r", [FQ, P], F32, su)
        rb2 = sb("rb2", [P, E1], F32, su)
        HR = sb("HR", [P, FQ, B, T], F32, su)
        sc = sb("sc", [P, TT, E1], F32, su)
        m8 = sb("m81", [P, TT, 8], F32, su)
        gt = sb("gt1", [P, TT, E1], F32, su)
        eq = sb("eq1", [P, TT, E1], F32, su)
        c0 = sb("c01", [P, TT, E1], F32, su)
        c1 = sb("c11", [P, TT, E1], F32, su)
        small = sb("small1", [P, 2, TT], F32, su)
        ones = sb("ones1", [P, P], F32, su)
        S = [psum(f"sv{i}", [P, 512], su) for i in range(8)]
        block = su.enter_context(nc.Block())
        s_pool, s_dve = Count(sem("sv_pool")), Count(sem("sv_dve"))
        mv_ready, rstd_ready, xn_ready = sem("mv_ready1"), sem("rstd_ready1"), sem("xn_ready1")
        w_zero, w_ready, xT_pe, xT_sb = sem("w_zero"), sem("w_ready"), sem("xT_pe"), sem("xT_sb")
        b_pe, b_sb, hr_pe, hr_sb, sc_pe = sem("b_pe"), sem("b_sb"), sem("hr_pe"), sem("hr_sb"), sem("sc_pe")
        exp_ready, exp_done, gate_ready = sem("exp_ready1"), sem("exp_done1"), sem("gate_ready")
        gt_pe, gt_sb, b2_pe, b2_sb = sem("gt_pe"), sem("gt_sb"), sem("b2_pe1"), sem("b2_sb1")

        @block.sync
        def _(sp):
            with nc.allow_non_contiguous_dma(reason="small weights"):
                sp.dma_start(wqkv[:], t_in["L1_attn_w_qkv"].rearrange("k (s n) -> k s n", s=3)).then_inc(d_w[0], 16)
                sp.dma_start(wv[:], t_in["L1_attn_w_qkv"][:, 2 * C:3 * C]).then_inc(d_w[0], 16)
                sp.dma_start(rw1[:], t_in["L1_ffn_rw1"]).then_inc(d_w[0], 16)
                sp.dma_start(rb1r[:], t_in["L1_ffn_rb1"].rearrange("(a p) -> a p", p=P)).then_inc(d_w[0], 16)
                sp.dma_start(rw2[:], t_in["L1_ffn_rw2"].rearrange("(a p) e -> p a e", p=P)).then_inc(d_w[0], 16)
                sp.dma_start(rb2[:], dram_rows(t_in["L1_ffn_rb2"], 0, [[0, P], [1, E1]])).then_inc(d_w[0], 16)
                sp.dma_start(b1r[:], t_in["L1_ffn_b1"].rearrange("e (a p) -> (e a) p", p=P)).then_inc(d_w[0], 16)
                sp.dma_start(b2r1[:], t_in["L1_ffn_b2"]).then_inc(d_w[0], 16)
                sp.dma_start(W1[:], t_in["L1_ffn_W1"].rearrange("e k f -> k e f")).then_inc(d_w[1], 16)
                sp.dma_start(W2[:], t_in["L1_ffn_W2"].rearrange("e (a p) c -> p e a c", p=P)).then_inc(d_w[1], 16)
                sp.wait_ge(w_zero, 1)
                wout = t_in["L1_attn_w_out"].rearrange("(q h e) n -> h e q n", q=HQ, e=HD)
                for hh in range(4):
                    sp.dma_start(wo[32 * hh:32 * hh + HD, :, :], wout[hh]).then_inc(d_w[2], 16)
            sp.wait_ge(d_w[1], 32)
            sp.wait_ge(d_w[2], 64)

        @block.gpsimd
        def _(pool):
            link = chain_of(pool, s_pool)
            pool.memset(wo[:], 0.0).then_inc(w_zero, 1)
            pool.memset(wq[:], 0.0)
            pool.memset(wk[:], 0.0)
            link(pool.memset(ones[:], 1.0))
            pool.wait_ge(mv_ready, 1)
            link(pool.tensor_scalar(rstd[:], mv[:, :, 1], EPS, 1.0, ALU.add, ALU.mult))
            pool.tensor_tensor(rstd[:], rstd[:], nhalf[:], ALU.pow).then_inc(rstd_ready, 1)
            def pick(out_ap, in_ap, op, base, pattern, mult, fill):
                return pool.affine_select(out=out_ap, in_=in_ap, compare_op=op, fill=fill, base=base, pattern=pattern,
                                          channel_multiplier=mult)
            link(pool.memset(sel[:], 0.0))
            link(pick(sel[:].rearrange("p (a c) -> p a c", a=4), sel[:].rearrange("p (a c) -> p a c", a=4), ALU.not_equal,
                      -HD, [[-32, 4], [0, 32]], 1, 1.0))
            def rows(lo, hi, dst):
                pool_tmp = small[:, 0, 0:4]
                link(pick(pool_tmp, ones[:, 0:4], ALU.is_ge, -lo, [[-32, 4]], 1, 0.0))
                link(pick(pool_tmp, pool_tmp, ALU.is_ge, hi, [[32, 4]], -1, 0.0))
                link(pool.tensor_tensor(small[:, 1, 0:2], small[:, 0, 0:2], small[:, 0, 2:4], ALU.add))
                link(pool.tensor_tensor(dst, small[:, 1, 0:1], small[:, 1, 1:2], ALU.add))
            rows(16, 23, neglo[:, 0:1])
            rows(8, 15, neglo[:, 1:2])
            link(pool.tensor_scalar(neglo[:], neglo[:], -1.0, 1.0, ALU.mult, ALU.mult))
            rows(24, 25, onesrow[:, 0:1])
            link(pool.tensor_tensor(neglo[:, 1:2], neglo[:, 1:2], onesrow[:], ALU.add))
            pool.memset(zcol[:], 0.0)
            pool.wait_ge(d_w[0], 16 * 8)
            for q in range(HQ):
                for dst, n in ((wq, 0), (wk, 1)):
                    for s in range(3):
                        last = pool.tensor_copy(dst[:, q, :, s, :], wqkv[:, n, 32 * q:32 * q + 32].rearrange("p (h d) -> p h d", d=HD))
            last.then_inc(w_ready, 1)

        @block.vector
        def _(v):
            link = chain_of(v, s_dve)
            for t in range(TT):
                last = v.bn_stats(stats[:, t, :], ACC[:, t, :])
            link(last)
            for t in range(TT):
                last = v.bn_aggr(mv[:, t, :], stats[:, t, :])
            last.then_inc(mv_ready, 1)
            v.wait_ge(rstd_ready, 1)
            for t in range(TT):
                last = v.tensor_scalar(XN[:, t, :], ACC[:, t, :], mv[:, t, 0:1], rstd[:, t:t + 1], ALU.subtract, ALU.mult)
            last.then_inc(xn_ready, 1)
            v.wait_ge(b_pe, 1)
            v.tensor_copy(b1c[:].rearrange("p e a -> p (e a)"), S[0][:, 0:E1 * FQ])
            v.tensor_copy(rb1c[:], S[0][:, 64:64 + FQ]).then_inc(b_sb, 1)
            v.wait_ge(sc_pe, 1)
            v.wait_ge(w_ready, 1)
            link(v.tensor_tensor(sc[:], S[1][:, 0:TT * E1].rearrange("p (t e) -> p t e", e=E1),
                                 rb2[:].unsqueeze(1).to_broadcast([P, TT, E1]), ALU.add))
            top_k_route(v, link, sc, gate, m8, gt, eq, c0, c1, small, E1, K1, exp_ready, exp_done).then_inc(gate_ready, 1)
            for i in range(4):
                v.wait_ge(gt_pe, i + 1)
                v.tensor_copy(gateT[:, 4 * i:4 * i + 4, :].rearrange("e t p -> e (t p)"), S[2 + i % 2][0:E1, :]).then_inc(gt_sb, 1)
            for i in range(4):
                v.wait_ge(b2_pe, i + 1)
                a = ACC[:, 4 * i:4 * i + 4, :].rearrange("p t c -> p (t c)")
                v.tensor_tensor(a, a, S[2 + i % 2][:, :], ALU.add).then_inc(b2_sb, 1)

        @block.scalar
        def _(act):
            for b in range(B):
                act.wait_ge(xT_pe, b + 1)
                act.copy(xT[:, b, :], S[2 + b][:, :]).then_inc(xT_sb, 1)
            act.wait_ge(b_sb, 1)
            for i in range(16):
                a, b = i % 4, i // 4
                act.wait_ge(hr_pe, i + 1)
                act.activation(HR[:, a, b, :], S[2 + i % 6][:, :], ACT.Relu, bias=rb1c[:, a:a + 1]).then_inc(hr_sb, 1)
            act.wait_ge(exp_ready, 1)
            act.activation(gate[:], gate[:], ACT.Exp).then_inc(exp_done, 1)

        @block.tensor
        def _(pe):
            pe.wait_ge(d_w[0], 16 * 8)
            pe.transpose(S[0][:, 0:E1 * FQ], b1r[:], ident[0:E1 * FQ, 0:E1 * FQ])
            pe.transpose(S[0][:, 64:64 + FQ], rb1r[:], ident[0:FQ, 0:FQ]).then_inc(b_pe, 1)
            pe.wait_ge(xn_ready, 1)
            for b in range(B):
                for i in range(NT):
                    last = pe.transpose(S[2 + b][:, P * i:P * i + P], XN[:, NT * b + i, :], ident[:])
                last.then_inc(xT_pe, 1)
            pe.wait_ge(xT_sb, B)
            for i in range(16):
                a, b = i % 4, i // 4
                if i >= 6:
                    pe.wait_ge(hr_sb, i - 5)
                pe.matmul(S[2 + i % 6][:, :], rw1[:, P * a:P * a + P], xT[:, b, :], start=True, stop=True).then_inc(hr_pe, 1)
            pe.wait_ge(hr_sb, 16)
            for t in range(TT):
                for a in range(FQ):
                    last = pe.matmul(S[1][:, E1 * t:E1 * t + E1], HR[:, a, t // NT, P * (t % NT):P * (t % NT) + P], rw2[:, a, :],
                                     start=(a == 0), stop=(a == FQ - 1))
            last.then_inc(sc_pe, 1)
            pe.wait_ge(gate_ready, 1)
            for i in range(4):
                if i >= 2:
                    pe.wait_ge(gt_sb, i - 1)
                for n in range(4):
                    last = pe.transpose(S[2 + i % 2][0:E1, P * n:P * n + P], gate[:, 4 * i + n, :], ident[:])
                last.then_inc(gt_pe, 1)
            pe.wait_ge(gt_sb, 4)
            for i in range(4):
                if i >= 2:
                    pe.wait_ge(b2_sb, i - 1)
                for n in range(4):
                    last = pe.matmul(S[2 + i % 2][:, P * n:P * n + P], gateT[:, 4 * i + n, :], b2r1[:], start=True, stop=True)
                last.then_inc(b2_pe, 1)

    KS = sb("KS", [P, HQ, T], F32R, l1)
    QS = sb("QS", [P, HQ, T], F32R, l1)
    hi = sb("hi", [P, 2, 2, T], F32, l1)
    XB = sb("XB", [P, T], F32, l1)
    VA = sb("VA", [P, NT, H1, 32], F32, l1)
    MX = sb("MX", [P, NT, HQ, 4], F32, l1)
    NX = sb("NX", [P, NT, HQ, 4, 32], F32, l1)
    EX = sb("EX", [P, 2, 4, NT, T], F32, l1)
    ND = sb("ND", [P, T], F32, l1)
    RC = sb("RC", [P, T], F32, l1)
    AT = sb("AT", [P, HQ, T], F32, l1)
    HB = sb("HB", [P, 2, FQ, T], F32, l1)
    SS = psum("SS", [P, 2, 2, T], l1)
    PHh = psum("PHh", [P, 2, T], l1)
    PYy = psum("PYy", [P, 4, C], l1)
    PN = psum("PN", [P, T], l1)
    block = l1.enter_context(nc.Block())

    tasks = ["q0", "q1", "k0", "k1", "v"] + [f"s{h}.{i}" for h in range(H1) for i in range(2)]
    tasks += ["t0", "t1"] + [f"e{h}.{i}" for h in range(H1) for i in range(2)] + ["o"]
    USES = len(tasks)
    assert USES % 2 == 0
    use = {name: n for n, name in enumerate(tasks)}
    filled = sem("slot_filled")
    freed = [sem("slot0_freed"), sem("slot1_freed")]
    ms_ready, xb_ready, hi_ready, nx_lo, nx_ready = (sem(n) for n in ("ms_ready", "xb_ready", "hi_ready", "nx_hi", "nx_ready"))
    nd_ready, nd_copied, den_ready, rc_done, at_ready = (
        sem(n) for n in ("nd_ready1", "nd_copied", "den_ready", "rc_done", "at_ready"))
    h_ready, h_relu, y_ready, y_used, d_done = (sem(n) for n in ("h_ready1", "h_relu", "y_ready1", "y_used1", "d_done"))
    UH, UE = E1 * FQ, E1

    def slot_of(name):
        return use[name] % 2

    def is_filled(b, name):
        return USES * b + use[name] + 1

    def may_fill(b, name):
        return (USES // 2) * b + use[name] // 2 + 1

    def is_emptied(b, name):
        return may_fill(b, name) + 1

    @block.sync
    def _(sp):
        with sp.Fori(0, B) as b:
            sp.wait_ge(freed[slot_of("o")], is_emptied(b, "o"))
            sp.dma_start(outd[:, bass.ds(NT * b, NT), :], ACC[:, bass.ds(NT * b, NT), :]).then_inc(d_done, 16)
        sp.wait_ge(d_done, 16 * B)

    @block.gpsimd
    def _(pool):
        pool.sem_inc(freed[0], 1)
        pool.sem_inc(freed[1], 1)
        pool.sem_inc(h_relu, 2)
        pool.sem_inc(y_ready, 2)
        pool.sem_inc(y_used, 1)
        pool.sem_inc(rc_done, 1)
        pool.sem_inc(at_ready, 1)
        pool.memset(NX[:], 0.0)
        pool.memset(VA[:], 0.0).then_inc(ms_ready, 1)
        pool.wait_ge(ms_ready, 1)
        pool.memset(VA[:, :, :, HD:HD + 1], 1.0).then_inc(ms_ready, 1)

    @block.tensor
    def _(pe):
        def fill(b, name):
            pe.wait_ge(freed[slot_of(name)], may_fill(b, name))
            return SS[:, slot_of(name), :, :]

        def hidden(b, e):
            for a in range(FQ):
                pe.wait_ge(h_relu, UH * b + FQ * e + a + 1)
                pe.matmul(PHh[:, a % 2, :], W1[:, e, P * a:P * a + P], XB[:], start=True, stop=True).then_inc(h_ready, 1)

        def expert_out(b, e):
            pe.wait_ge(h_relu, UH * b + FQ * e + FQ + 2)
            pe.wait_ge(y_used, UE * b + e + 1)
            for i in range(NT):
                for a in range(FQ):
                    mm = pe.matmul(PYy[:, i, :], HB[:, e % 2, a, P * i:P * i + P], W2[:, e, a, :],
                                   start=(a == 0), stop=(a == FQ - 1))
            mm.then_inc(y_ready, 1)

        def scores(b, h, kind):
            r, q = 32 * (h % 4), h // 4
            rows, cols = (QS, KS) if kind == "s" else (KS, QS)
            for i in range(2):
                bank = fill(b, f"{kind}{h}.{i}")
                for n in range(2):
                    t = 2 * i + n
                    mm = pe.matmul(bank[:, n, :], rows[r:r + 32, q, P * t:P * t + P], cols[r:r + 32, q, :], start=True, stop=True)
                mm.then_inc(filled, 1)

        def values(b, q):
            for i in range(2):
                pe.wait_ge(freed[slot_of(f"e{4 * q + 3}.{i}")], is_emptied(b, f"e{4 * q + 3}.{i}"))
            pe.wait_ge(rc_done, HQ * b + q + 1)
            for t in range(NT):
                for hh in range(4):
                    mm = pe.matmul(PN[32 * hh:32 * hh + 32, :], VA[:, t, 4 * q + hh, :], EX[:, q % 2, hh, t, :],
                                   start=(t == 0), stop=(t == NT - 1))
            mm.then_inc(nd_ready, 1)

        def sums(b, q):
            pe.wait_ge(nd_copied, HQ * b + q + 1)
            pe.matmul(PN[:, :], sel[:], ND[:], start=True, stop=True).then_inc(den_ready, 1)

        pe.wait_ge(ms_ready, 2)
        def project(b, w, name):
            bank = fill(b, name)
            for n in range(2):
                mm = pe.matmul(bank[:, n, :], w[:, 2 * int(name[1]) + n].rearrange("p h s d -> p (h s d)"), XB[:], start=True, stop=True)
            mm.then_inc(filled, 1)

        with pe.Fori(0, B) as b:
            pe.wait_ge(xb_ready, b + 1)
            project(b, wq, "q0")
            project(b, wq, "q1")
            hidden(b, 0)
            project(b, wk, "k0")
            project(b, wk, "k1")
            bank = fill(b, "v")
            for i in range(NT):
                mm = pe.matmul(bank[:, 0, P * i:P * i + P], XB[:, P * i:P * i + P], wv[:], start=True, stop=True)
            mm.then_inc(filled, 1)
            hidden(b, 1)
            expert_out(b, 0)
            for k in ("k0", "k1"):
                pe.wait_ge(freed[slot_of(k)], is_emptied(b, k))
            for h in range(H1):
                scores(b, h, "s")
                if h == 3:
                    hidden(b, 2)
                if h == 7:
                    expert_out(b, 1)
                if h == 11:
                    hidden(b, 3)
            expert_out(b, 2)
            pe.wait_ge(nx_ready, b + 1)
            for i in range(2):
                bank = fill(b, f"t{i}")
                for n in range(2):
                    for t in range(NT):
                        mm = pe.transpose(bank[:, n, P * t:P * t + P], NX[:, t, 2 * i + n].rearrange("p h r -> p (h r)"), ident[:])
                mm.then_inc(filled, 1)
            hidden(b, 4)
            for i in range(2):
                pe.wait_ge(freed[slot_of(f"t{i}")], is_emptied(b, f"t{i}"))
            for q in range(HQ):
                for h in range(4 * q, 4 * q + 4):
                    scores(b, h, "e")
                if q == 0:
                    expert_out(b, 3)
                else:
                    values(b, q - 1)
                    hidden(b, q + 4)
                    sums(b, q - 1)
                    if q < HQ - 1:
                        expert_out(b, q + 3)
            values(b, HQ - 1)
            expert_out(b, 6)
            sums(b, HQ - 1)
            expert_out(b, 7)
            pe.wait_ge(at_ready, HQ * b + HQ + 1)
            bank = fill(b, "o")
            for i in range(NT):
                for q in range(HQ):
                    mm = pe.matmul(bank[:, 0, P * i:P * i + P], AT[:, q, P * i:P * i + P], wo[:, q, :],
                                   start=(q == 0), stop=(q == HQ - 1))
            mm.then_inc(filled, 1)

    @block.scalar
    def _(act):
        def relu(b, e):
            act.wait_ge(y_ready, UE * b + e + 1)
            for a in range(FQ):
                act.wait_ge(h_ready, UH * b + FQ * e + a + 1)
                act.activation(HB[:, e % 2, a, :], PHh[:, a % 2, :], ACT.Relu, bias=b1c[:, e, a:a + 1]).then_inc(h_relu, 1)

        def high_part(b, name):
            act.wait_ge(filled, is_filled(b, name))
            dst = hi[:, slot_of(name), :, :].bitcast(F32R)
            bias = zcol[:, 0:1] if name[0] == "q" else onesrow[:, 0:1]
            act.activation(dst, SS[:, slot_of(name), :, :], ACT.Identity, bias=bias).then_inc(hi_ready, 1)

        def exps(b, q):
            if q >= 2:
                act.wait_ge(nd_ready, HQ * b + q - 1)
            for h in range(4 * q, 4 * q + 4):
                for i in range(2):
                    name = f"e{h}.{i}"
                    act.wait_ge(filled, is_filled(b, name))
                    act.activation(EX[:, q % 2, h % 4, 2 * i:2 * i + 2, :], SS[:, slot_of(name), :, :], ACT.Exp, scale=SCALE1
                                   ).then_inc(freed[slot_of(name)], 1)

        def copy_nd(b, q):
            act.wait_ge(nd_ready, HQ * b + q + 1)
            act.wait_ge(at_ready, HQ * b + q + 1)
            act.copy(ND[:], PN[:]).then_inc(nd_copied, 1)

        act.wait_ge(ms_ready, 2)
        with act.Fori(0, B) as b:
            high_part(b, "q0")
            high_part(b, "q1")
            relu(b, 0)
            high_part(b, "k0")
            high_part(b, "k1")
            act.wait_ge(filled, is_filled(b, "v"))
            act.copy(VA[:, :, :, 0:HD], SS[:, slot_of("v"), 0, :].rearrange("p (t h e) -> p t h e", t=NT, e=HD)
                     ).then_inc(freed[slot_of("v")], 1)
            for e in range(1, 5):
                relu(b, e)
            exps(b, 0)
            for q in range(1, HQ):
                exps(b, q)
                relu(b, q + 4)
                copy_nd(b, q - 1)
            copy_nd(b, HQ - 1)

    @block.vector
    def _(v):
        def low_part(b, name, dst):
            s = slot_of(name)
            i = int(name[1])
            v.wait_ge(hi_ready, 4 * b + use[name] + 1)
            v.scalar_tensor_tensor(out=dst[:, 2 * i:2 * i + 2, :], in0=hi[:, s, :, :],
                                   scalar=neglo[:, 0:1] if name[0] == "q" else neglo[:, 1:2],
                                   in1=SS[:, s, :, :], op0=ALU.mult, op1=ALU.add).then_inc(freed[s], 1)

        def maxima(b, h):
            for i in range(2):
                name = f"s{h}.{i}"
                v.wait_ge(filled, is_filled(b, name))
                v.tensor_reduce(MX[:, 2 * i:2 * i + 2, h // 4, h % 4], SS[:, slot_of(name), :, :], AX.X, ALU.max
                                ).then_inc(freed[slot_of(name)], 1)

        def combine(b, e):
            v.wait_ge(y_ready, UE * b + e + 3)
            for i in range(NT):
                a = ACC[:, bass.ds(NT * b + i, 1), :].rearrange("p o c -> p (o c)")
                ins = v.scalar_tensor_tensor(out=a, in0=PYy[:, i, :], scalar=gate[:, bass.ds(NT * b + i, 1), e],
                                             in1=a, op0=ALU.mult, op1=ALU.add)
            ins.then_inc(y_used, 1)

        def normalise(b, q):
            v.wait_ge(den_ready, HQ * b + q + 1)
            v.reciprocal(RC[:], PN[:]).then_inc(rc_done, 1)
            v.wait_ge(rc_done, HQ * b + q + 2)
            v.tensor_tensor(AT[:, q, :], ND[:], RC[:], ALU.mult).then_inc(at_ready, 1)

        with v.Fori(0, B) as b:
            v.tensor_copy(XB[:], xT[:, bass.ds(b, 1), :].rearrange("p o t -> p (o t)")).then_inc(xb_ready, 1)
            for name, dst in (("q0", QS), ("q1", QS), ("k0", KS), ("k1", KS)):
                low_part(b, name, dst)
            for h in range(H1):
                maxima(b, h)
                if h == 3:
                    combine(b, 0)
                if h == 11:
                    combine(b, 1)
            for i in range(2):
                v.wait_ge(freed[slot_of(f"s15.{i}")], is_emptied(b, f"s15.{i}"))
            m = MX[:].rearrange("p t q h -> p (t q) h")
            nx = NX[:].rearrange("p t q h r -> p (t q) h r")
            v.tensor_scalar(nx[:, :, :, 24].bitcast(F32R), m, -1.0, None, ALU.mult).then_inc(nx_lo, 1)
            v.wait_ge(nx_lo, b + 1)
            v.scalar_tensor_tensor(out=nx[:, :, :, 25], in0=m, scalar=-1.0, in1=nx[:, :, :, 24], op0=ALU.mult,
                                   op1=ALU.subtract).then_inc(nx_ready, 1)
            combine(b, 2)
            for i in range(2):
                name = f"t{i}"
                v.wait_ge(filled, is_filled(b, name))
                part = QS[:, 2 * i:2 * i + 2, :]
                v.tensor_tensor(part, part.bitcast(F32), SS[:, slot_of(name), :, :], ALU.add).then_inc(freed[slot_of(name)], 1)
            combine(b, 3)
            for q in range(HQ - 1):
                normalise(b, q)
                if q < HQ - 2:
                    combine(b, q + 4)
            combine(b, 6)
            normalise(b, HQ - 1)
            combine(b, 7)
            v.wait_ge(filled, is_filled(b, "o"))
            v.wait_ge(y_used, UE * b + UE + 1)
            a = ACC[:, bass.ds(NT * b, NT), :].rearrange("p t c -> p (t c)")
            v.tensor_tensor(a, a, SS[:, slot_of("o"), 0, :], ALU.add).then_inc(freed[slot_of("o")], 1)


_OUT = ((B, T, C), "float32")


def kernel(**inputs):
    import numpy as np
    import concourse.bacc as bacc
    from concourse.bass_utils import run_bass_kernel_spmd

    nc = bacc.Bacc("TRN2", target_bir_lowering=False, num_devices=1)
    arrays, handles = {}, {}
    for name in inputs:
        a = np.ascontiguousarray(inputs[name])
        arrays[f"in_{name}"] = a
        handles[name] = nc.dram_tensor(f"in_{name}", a.shape, mybir.dt.from_np(a.dtype), kind="ExternalInput").ap()
    out = nc.dram_tensor("out", _OUT[0], F32, kind="ExternalOutput").ap()
    build(nc, handles, out)
    return run_bass_kernel_spmd(nc, [arrays], core_ids=[0]).results[0]["out"]
```

```python
from contextlib import ExitStack

import concourse.bass as bass
from concourse import mybir

F32 = mybir.dt.float32
F32R = mybir.dt.float32r
ALU = mybir.AluOpType
ACT = mybir.ActivationFunctionType
AX = mybir.AxisListType

P = 128
B, T, C = 4, 512, 128
NT = T // P
TT = B * NT
H0, BD, HS = 16, 16, 8
WIN = 64
G = 2
HG = H0 // G
PAD = WIN - 1
TP = PAD + T + 1
JQ = WIN // 4
E0, K0, I0 = 16, 4, 128
LIMIT, ALPHA = 7.0, 1.702
H1, HD = 16, 8
HQ = 4
E1, K1, FF = 8, 2, 512
FQ = FF // P
EPS = 1e-5
MASKED = -3.0e38
RING = 4
PE_ITEMS = (1, 4, 6)
NPE = len(PE_ITEMS)
SCALE1 = float(C) ** -0.5


class Count:

    def __init__(self, sem):
        self.sem, self.n = sem, 0

    def inc(self, instruction, by=1):
        instruction.then_inc(self.sem, by)
        self.n += by
        return self.n


def chain_of(engine, count):

    def link(instruction):
        engine.wait_ge(count.sem, count.inc(instruction))

    return link


def dram_rows(tensor, offset, dims):
    return bass.AP(tensor=tensor.tensor, offset=tensor.offset + offset, ap=dims)


def build(nc, t_in, out):
    ctx = ExitStack()
    with ctx:
        def sb(name, shape, dt=F32, where=ctx):
            return where.enter_context(nc.sbuf_tensor(name, shape, dt))

        def psum(name, shape, where=ctx):
            return where.enter_context(nc.psum_tensor(name, shape, F32))

        def sem(name):
            return ctx.enter_context(nc.semaphore(name))

        ident = sb("ident", [P, P])
        ACC = sb("ACC", [P, TT, C])
        nhalf = sb("nhalf", [P, TT])
        stats = sb("stats", [P, TT, 6])
        mv = sb("mv", [P, TT, 2])
        rstd = sb("rstd", [P, TT])

        with ExitStack() as l0:
            first_layer(nc, t_in, l0, sb, psum, sem, ident, ACC, nhalf, stats, mv, rstd)
        with ExitStack() as l1:
            second_layer(nc, t_in, out, l1, sb, psum, sem, ident, ACC, nhalf, stats, mv, rstd)


def top_k_route(v, link, scores, route, m8, gt, eq, c0, c1, small, n_exp, k, exp_ready, exp_done):
    n = scores.shape[1]
    for t in range(n):
        last = v.max(m8[:, t, :], scores[:, t, :])
    link(last)
    full = [P, n, n_exp]
    kth = m8[:, :, k - 1:k].to_broadcast(full)
    v.tensor_tensor(gt[:], scores[:], kth, ALU.is_gt)
    link(v.tensor_tensor(eq[:], scores[:], kth, ALU.is_equal))
    v.tensor_reduce(small[:, 0, :], gt[:], AX.X, ALU.add)
    src, dst = eq, c0
    step = 1
    while step < n_exp:
        v.tensor_copy(dst[:, :, 0:step], src[:, :, 0:step])
        link(v.tensor_tensor(dst[:, :, step:], src[:, :, step:], src[:, :, :n_exp - step], ALU.add))
        src, dst = dst, (c1 if dst is c0 else c0)
        step *= 2
    link(v.tensor_scalar(small[:, 1, :], small[:, 0, :], -1.0, float(k), ALU.mult, ALU.add))
    need = small[:, 1, :].unsqueeze(2).to_broadcast(full)
    link(v.tensor_tensor(dst[:], src[:], need, ALU.is_le))
    link(v.tensor_tensor(dst[:], dst[:], eq[:], ALU.mult))
    link(v.tensor_tensor(gt[:], gt[:], dst[:], ALU.add))
    v.tensor_tensor(route[:], scores[:], m8[:, :, 0:1].to_broadcast(full), ALU.subtract).then_inc(exp_ready, 1)
    v.wait_ge(exp_done, 1)
    link(v.tensor_tensor(route[:], route[:], gt[:], ALU.mult))
    link(v.tensor_reduce(small[:, 0, :], route[:], AX.X, ALU.add))
    link(v.reciprocal(small[:, 1, :], small[:, 0, :]))
    return v.tensor_tensor(route[:], route[:], small[:, 1, :].unsqueeze(2).to_broadcast(full), ALU.mult)


def first_layer(nc, t_in, l0, sb, psum, sem, ident, ACC, nhalf, stats, mv, rstd):
    x = t_in["L0_attn_x"].rearrange("b t c -> (b t) c").rearrange("(n p) c -> p n c", p=P)
    nv, ns, ng, npl, nt = nc.vector, nc.scalar, nc.gpsimd, nc.gpsimd, nc.tensor

    xnT = sb("xnT", [P, B, TP], F32, l0)
    tT = sb("tT", [P, B, T], F32, l0)
    w1T = sb("w1T", [P, E0, I0], F32, l0)
    w2T = sb("w2T", [P, E0, C], F32, l0)
    b1T = sb("b1T", [P, E0], F32, l0)
    route = sb("route", [P, TT, E0], F32, l0)
    wad = sb("wad", [P, G, 2, P], F32, l0)
    PT = sb("PT", [P, WIN], F32, l0)
    lred = sb("lred", [P, 2, 4, 32], F32, l0)
    mz = sb("mz", [P, JQ, WIN], F32, l0)
    bdmg = sb("bdmg", [P, 1], F32, l0)
    bdo = sb("bdo", [P, 1], F32, l0)
    wval = sb("wval", [P, C], F32, l0)
    wcp = sb("wcp", [P, G, C], F32, l0)
    lones = sb("lones", [P, 4, 32], F32, l0)
    DHL = sb("DHL", [P, 2, B, TP], F32R, l0)
    eyes = sb("eyes", [P, 2, P], F32R, l0)
    AD = sb("AD", [P, 2, B, TP], F32, l0)
    attT = sb("attT", [P, G, 2, T], F32, l0)
    Z = sb("Z", [P, JQ, T], F32, l0)

    d_x = [sem(f"d_x{b}") for b in range(B)]
    d_attn_w, d_gate_w, d_mlp_w, d_band0 = sem("d_attn_w"), sem("d_gate_w"), sem("d_mlp_w"), sem("d_band0")
    band = nc.dram_tensor("band", [2, 2, 32, 64, P], F32, kind="Internal").ap()

    with ExitStack() as su:
        X = sb("X", [P, TT, C], F32, su)
        XN = sb("XN", [P, TT, C], F32, su)
        TF = sb("TF", [P, TT, C], F32, su)
        w1r = sb("w1r", [P, E0, C], F32, su)
        w2r = sb("w2r", [P, E0, C], F32, su)
        b1r = sb("b1r", [E0, 2 * I0], F32, su)
        b2r = sb("b2r", [E0, C], F32, su)
        wdisp = sb("wdisp", [P, G, P], F32, su)
        wdispT = sb("wdispT", [P, G, P], F32, su)
        wrep = sb("wrep", [P, 2, BD], F32, su)
        wcol = sb("wcol", [P, 2], F32, su)
        wblk = sb("wblk", [P, 2, HG, BD], F32, su)
        rel = sb("rel", [WIN, BD], F32, su)
        relT = sb("relT", [BD, WIN], F32, su)
        wpos = sb("wpos", [BD, HG, BD], F32, su)
        gw = sb("gw", [E0, C], F32, su)
        gwT = sb("gwT", [P, E0], F32, su)
        gb = sb("gb", [P, E0], F32, su)
        scl = sb("scl", [P, 1], F32, su)
        mask8 = sb("mask8", [P, HG], F32, su)
        ones8 = sb("ones8", [P, HG], F32, su)
        mt = sb("mt", [WIN, WIN], F32, su)
        mt2 = sb("mt2", [WIN, JQ, 32, 4], F32, su)
        ss = sb("ss", [P, TT], F32, su)
        r2 = sb("r2", [P, TT], F32, su)
        gsc = sb("gsc", [P, TT, E0], F32, su)
        m8 = sb("m8", [P, TT, 8], F32, su)
        gt = sb("gt", [P, TT, E0], F32, su)
        eq = sb("eq", [P, TT, E0], F32, su)
        c0 = sb("c0", [P, TT, E0], F32, su)
        c1 = sb("c1", [P, TT, E0], F32, su)
        small = sb("small", [P, 2, TT], F32, su)
        routeT = sb("routeT", [E0, TT, P], F32, su)
        S = [psum(f"su{i}", [P, 512], su) for i in range(8)]
        block = su.enter_context(nc.Block())

        s_pool, s_dve = Count(sem("su_pool")), Count(sem("su_dve"))
        mv_ready, rstd_ready, ss_ready, r2_ready = (sem(n) for n in ("mv_ready", "rstd_ready", "ss_ready", "r2_ready"))
        const_ready, xn_ready, tf_ready = sem("const_ready"), sem("xn_ready"), sem("tf_ready")
        blk_ready, zero_ready, mt_ready = sem("blk_ready"), sem("zero_ready"), sem("mt_ready")
        xnT_pe, tT_pe, xnT_sb, tT_sb = sem("xnT_pe"), sem("tT_pe"), sem("xnT_sb"), sem("tT_sb")
        wt_pe, wt_sb, wad_pe, wad_sb = sem("wt_pe"), sem("wt_sb"), sem("wad_pe"), sem("wad_sb")
        gate_pe, exp_ready, exp_done, route_ready = sem("gate_pe"), sem("exp_ready"), sem("exp_done"), sem("route_ready")
        misc_pe, misc_sb, mlp_pe, mlp_sb = sem("misc_pe"), sem("misc_sb"), sem("mlp_pe"), sem("mlp_sb")
        mzt_pe, mzt_sb, rt_pe, rt_sb, b2_pe, b2_sb = (sem(n) for n in ("mzt_pe", "mzt_sb", "rt_pe", "rt_sb", "b2_pe", "b2_sb"))

        @block.sync
        def _(sp):
            for b in range(B):
                sp.dma_start(X[:, NT * b:NT * b + NT, :], x[:, NT * b:NT * b + NT, :]).then_inc(d_x[b], 16)
            wd = t_in["L0_attn_W_disp"]
            with nc.allow_non_contiguous_dma(reason="small weights"):
                sp.dma_start(wdisp[:], wd.rearrange("k (g n) -> k g n", g=G)).then_inc(d_attn_w, 16)
                for s, n in enumerate(("L0_attn_W_strain", "L0_attn_W_dmg")):
                    sp.dma_start(wrep[:, s, :], dram_rows(t_in[n], 0, [[0, HG], [BD, BD], [1, BD]])).then_inc(d_attn_w, 16)
                for s, n in enumerate(("L0_attn_W_bond", "L0_attn_W_dmg_out")):
                    sp.dma_start(wcol[:, s:s + 1], dram_rows(t_in[n], 0, [[0, HG], [1, BD], [1, 1]])).then_inc(d_attn_w, 16)
                sp.dma_start(bdmg[:], dram_rows(t_in["L0_attn_b_dmg"], 0, [[0, HG], [1, BD], [1, 1]])).then_inc(d_attn_w, 16)
                sp.dma_start(bdo[:], dram_rows(t_in["L0_attn_b_dmg_out"], 0, [[0, P], [1, 1]])).then_inc(d_attn_w, 16)
                sp.dma_start(rel[:], t_in["L0_attn_rel_pos_emb"]).then_inc(d_attn_w, 16)
                sp.dma_start(wpos[:], dram_rows(t_in["L0_attn_W_pos"], 0, [[BD, BD], [0, HG], [1, BD]])).then_inc(d_attn_w, 16)
                sp.dma_start(wval[:], t_in["L0_attn_W_val"]).then_inc(d_attn_w, 16)
                for half in range(2):
                    sp.dma_start(wcp[64 * half:64 * half + 64, :, :],
                                 t_in["L0_attn_W_cproj"].rearrange("(g r) n -> r g n", g=G)).then_inc(d_attn_w, 16)
                sp.dma_start(gw[:], t_in["L0_ffn_gate_w"]).then_inc(d_gate_w, 16)
                sp.dma_start(gb[:], dram_rows(t_in["L0_ffn_gate_b"], 0, [[0, P], [1, E0]])).then_inc(d_gate_w, 16)
                sp.dma_start(scl[:], dram_rows(t_in["L0_ffn_scale"], 0, [[1, P], [1, 1]])).then_inc(d_gate_w, 16)
                sp.dma_start(w1r[:], dram_rows(t_in["L0_ffn_mlp1_w"], 0, [[2 * C, I0], [2 * I0 * C, E0], [1, C]])).then_inc(d_mlp_w, 16)
                sp.dma_start(w2r[:], t_in["L0_ffn_mlp2_w"].rearrange("e h i -> h e i")).then_inc(d_mlp_w, 16)
                sp.dma_start(b1r[:], t_in["L0_ffn_mlp1_b"]).then_inc(d_mlp_w, 16)
                sp.dma_start(b2r[:], t_in["L0_ffn_mlp2_b"]).then_inc(d_mlp_w, 16)
            sp.wait_ge(zero_ready, 1)
            flat = band.rearrange("a k n r s -> (a k n r s)").rearrange("(p f) -> p f", p=P)
            for i in range(4):
                sp.dma_start(flat[:, 2048 * i:2048 * i + 2048], Z[:, 0:4, :].rearrange("p q t -> p (q t)")).then_inc(d_band0, 16)
            sp.wait_ge(d_band0, 64)

        @block.gpsimd
        def _(pool):
            link = chain_of(pool, s_pool)
            link(pool.memset(ident[:], 0.0))
            pool.affine_select(out=ident[:], in_=ident[:], compare_op=ALU.not_equal, fill=1.0, base=0,
                               pattern=[[-1, P]], channel_multiplier=1).then_inc(const_ready, 1)
            pool.memset(nhalf[:], -0.5)
            link(pool.memset(ones8[:], 1.0))
            link(pool.affine_select(out=mask8[:], in_=ones8[:], compare_op=ALU.is_ge, fill=0.0, base=0,
                                    pattern=[[-BD, HG]], channel_multiplier=1))
            pool.affine_select(out=mask8[:], in_=mask8[:], compare_op=ALU.is_ge, fill=0.0, base=BD - 1,
                               pattern=[[BD, HG]], channel_multiplier=-1).then_inc(const_ready, 1)
            link(pool.memset(Z[:, 0:4, :], 0.0))
            link(pool.affine_select(out=mt[:], in_=Z[0:WIN, 0, 0:WIN], compare_op=ALU.is_ge, fill=MASKED,
                                    base=-PAD, pattern=[[1, WIN]], channel_multiplier=1))
            pool.tensor_copy(mt2[:], mt[:].rearrange("t (q j) -> t q j", j=4).unsqueeze(2).to_broadcast([WIN, JQ, 32, 4])
                             ).then_inc(mt_ready, 1)
            link(pool.memset(lones[:], 0.0))
            for hh in range(4):
                last = pool.memset(lones[:, hh, 8 * hh:8 * hh + 8], 1.0)
            link(last)
            pool.memset(AD[:, :, :, 0:PAD], 0.0)
            pool.memset(AD[:, :, :, PAD + T:TP], 0.0)
            pool.memset(xnT[:, :, 0:PAD], 0.0)
            pool.memset(xnT[:, :, PAD + T:TP], 0.0).then_inc(zero_ready, 1)
            pool.wait_ge(mv_ready, 1)
            link(pool.tensor_scalar(rstd[:], mv[:, :, 1], EPS, 1.0, ALU.add, ALU.mult))
            pool.tensor_tensor(rstd[:], rstd[:], nhalf[:], ALU.pow).then_inc(rstd_ready, 1)
            pool.wait_ge(ss_ready, 1)
            link(pool.tensor_scalar(r2[:], ss[:], 1.0 / C, EPS, ALU.mult, ALU.add))
            pool.tensor_tensor(r2[:], r2[:], nhalf[:], ALU.pow).then_inc(r2_ready, 1)

        @block.vector
        def _(v):
            link = chain_of(v, s_dve)
            for b in range(B):
                v.wait_ge(d_x[b], 16)
                for t in range(NT * b, NT * b + NT):
                    last = v.bn_stats(stats[:, t, :], X[:, t, :])
            link(last)
            for t in range(TT):
                last = v.bn_aggr(mv[:, t, :], stats[:, t, :])
            last.then_inc(mv_ready, 1)
            v.wait_ge(d_attn_w, 16 * 12)
            v.wait_ge(const_ready, 2)
            for s in range(2):
                v.tensor_tensor(wblk[:, s, :, :], wrep[:, s, :].unsqueeze(1).to_broadcast([P, HG, BD]),
                                mask8[:].unsqueeze(2).to_broadcast([P, HG, BD]), ALU.mult)
            link(v.memset(lred[:], 0.0))
            for s in range(2):
                for a in range(4):
                    last = v.tensor_scalar(lred[:, s, a, a:32:4], mask8[:], wcol[:, s:s + 1], None, ALU.mult)
            v.tensor_copy(eyes[:, 0, :], ident[:])
            v.tensor_scalar(eyes[:, 1, :], ident[:], -1.0, None, ALU.mult)
            v.tensor_scalar(bdo[:], bdo[:], 0.5, None, ALU.mult).then_inc(blk_ready, 1)
            v.wait_ge(rstd_ready, 1)
            for t in range(TT):
                last = v.tensor_scalar(XN[:, t, :], X[:, t, :], mv[:, t, 0:1], rstd[:, t:t + 1], ALU.subtract, ALU.mult)
            last.then_inc(xn_ready, 1)
            v.wait_ge(xn_ready, 1)
            for t in range(TT):
                last = v.tensor_tensor_reduce(TF[:, t, :], XN[:, t, :], XN[:, t, :], 1.0, 0.0, ALU.mult, ALU.add,
                                              ss[:, t:t + 1])
            last.then_inc(ss_ready, 1)
            link(v.tensor_tensor(ACC[:], X[:], XN[:], ALU.add))
            v.wait_ge(r2_ready, 1)
            v.wait_ge(ss_ready, 1)
            for t in range(TT):
                last = v.tensor_scalar(TF[:, t, :], XN[:, t, :], r2[:, t:t + 1], None, ALU.mult)
            last.then_inc(tf_ready, 1)
            v.wait_ge(misc_pe, 1)
            v.tensor_copy(gwT[:], S[0][:, 0:E0])
            v.tensor_copy(relT[:], S[0][0:BD, 64:64 + WIN])
            v.tensor_copy(b1T[:], S[0][:, 128:128 + E0]).then_inc(misc_sb, 1)
            v.wait_ge(misc_pe, 2)
            v.tensor_copy(PT[:], S[0][:, 256:256 + WIN]).then_inc(misc_sb, 1)
            v.wait_ge(gate_pe, 1)
            v.wait_ge(d_gate_w, 48)
            link(v.tensor_tensor(gsc[:], S[1][:, 0:TT * E0].rearrange("p (t e) -> p t e", e=E0),
                                 gb[:].unsqueeze(1).to_broadcast([P, TT, E0]), ALU.add))
            top_k_route(v, link, gsc, route, m8, gt, eq, c0, c1, small, E0, K0, exp_ready, exp_done).then_inc(route_ready, 1)
            for i in range(4):
                v.wait_ge(rt_pe, i + 1)
                v.tensor_copy(routeT[:, 4 * i:4 * i + 4, :].rearrange("e t p -> e (t p)"), S[2 + i % 2][0:E0, :]).then_inc(rt_sb, 1)
            for i in range(4):
                v.wait_ge(b2_pe, i + 1)
                a = ACC[:, 4 * i:4 * i + 4, :].rearrange("p t c -> p (t c)")
                v.tensor_tensor(a, a, S[2 + i % 2][:, :], ALU.add).then_inc(b2_sb, 1)

        @block.scalar
        def _(act):
            for b in range(B):
                act.wait_ge(xnT_pe, b + 1)
                act.copy(xnT[:, b, PAD:PAD + T], S[2 + b][:, :]).then_inc(xnT_sb, 1)
            act.wait_ge(wt_pe, 1)
            act.copy(wdispT[:], S[6][:, 0:G * P]).then_inc(wt_sb, 1)
            act.wait_ge(wad_pe, 1)
            act.copy(wad[:], S[7][:]).then_inc(wad_sb, 1)
            act.wait_ge(d_gate_w, 48)
            for b in range(B):
                act.wait_ge(tT_pe, b + 1)
                act.activation(tT[:, b, :], S[2 + b][:, :], ACT.Copy, scale=scl[:, 0:1]).then_inc(tT_sb, 1)
            act.wait_ge(exp_ready, 1)
            act.activation(route[:], route[:], ACT.Exp).then_inc(exp_done, 1)
            for i in range(8):
                act.wait_ge(mlp_pe, i + 1)
                dst, e = (w1T, 4 * i) if i < 4 else (w2T, 4 * i - 16)
                act.activation(dst[:, e:e + 4, :].rearrange("p e c -> p (e c)"), S[6 + i % 2][:, :], ACT.Copy,
                               scale=1.0 if i < 4 else (LIMIT + 1.0) / 2).then_inc(mlp_sb, 1)
            for i in range(4):
                act.wait_ge(mzt_pe, i + 1)
                act.copy(mz[:, 4 * i:4 * i + 4, :].rearrange("p q t -> p (q t)"), S[4 + i % 2][:, 0:256]).then_inc(mzt_sb, 1)

        @block.tensor
        def _(pe):
            pe.wait_ge(const_ready, 1)
            pe.wait_ge(d_attn_w, 16 * 12)
            for g in range(G):
                last = pe.transpose(S[6][:, P * g:P * g + P], wdisp[:, g, :], ident[:])
            last.then_inc(wt_pe, 1)
            pe.wait_ge(d_gate_w, 48)
            pe.wait_ge(d_mlp_w, 64)
            pe.transpose(S[0][:, 0:E0], gw[:], ident[0:E0, 0:E0])
            pe.transpose(S[0][0:BD, 64:64 + WIN], rel[:], ident[0:WIN, 0:WIN])
            pe.transpose(S[0][:, 128:128 + E0], b1r[:, 0:2 * I0:2], ident[0:E0, 0:E0]).then_inc(misc_pe, 1)
            pe.wait_ge(xn_ready, 1)
            for b in range(B):
                for i in range(NT):
                    last = pe.transpose(S[2 + b][:, P * i:P * i + P], XN[:, NT * b + i, :], ident[:])
                last.then_inc(xnT_pe, 1)
            pe.wait_ge(wt_sb, 1)
            pe.wait_ge(blk_ready, 1)
            for g in range(G):
                for s in range(2):
                    at = P * (2 * g + s)
                    last = pe.matmul(S[7][:, at:at + P], wdispT[:, g, :], wblk[:, s, :, :].rearrange("p h c -> p (h c)"),
                                     start=True, stop=True)
            last.then_inc(wad_pe, 1)
            pe.wait_ge(tf_ready, 1)
            for b in range(B):
                pe.wait_ge(xnT_sb, b + 1)
                for i in range(NT):
                    last = pe.transpose(S[2 + b][:, P * i:P * i + P], TF[:, NT * b + i, :], ident[:])
                last.then_inc(tT_pe, 1)
            pe.wait_ge(misc_sb, 1)
            pe.matmul(S[0][:, 256:256 + WIN], wpos[:].rearrange("k h c -> k (h c)"), relT[:], start=True, stop=True).then_inc(misc_pe, 1)
            pe.wait_ge(tT_sb, B)
            for t in range(TT):
                last = pe.matmul(S[1][:, E0 * t:E0 * t + E0], tT[:, t // NT, P * (t % NT):P * (t % NT) + P], gwT[:],
                                 start=True, stop=True)
            last.then_inc(gate_pe, 1)
            pe.wait_ge(wad_sb, 1)
            for i in range(8):
                if i >= 2:
                    pe.wait_ge(mlp_sb, i - 1)
                src, e = (w1r, 4 * i) if i < 4 else (w2r, 4 * i - 16)
                for n in range(4):
                    last = pe.transpose(S[6 + i % 2][:, P * n:P * n + P], src[:, e + n, :], ident[:])
                last.then_inc(mlp_pe, 1)
            pe.wait_ge(mt_ready, 1)
            for i in range(4):
                if i >= 2:
                    pe.wait_ge(mzt_sb, i - 1)
                for n in range(4):
                    last = pe.transpose(S[4 + i % 2][:, WIN * n:WIN * n + WIN],
                                        mt2[:, 4 * i + n, :, :].rearrange("t n j -> t (n j)"), ident[0:WIN, 0:WIN])
                last.then_inc(mzt_pe, 1)
            pe.wait_ge(route_ready, 1)
            for i in range(4):
                if i >= 2:
                    pe.wait_ge(rt_sb, i - 1)
                for n in range(4):
                    last = pe.transpose(S[2 + i % 2][0:E0, P * n:P * n + P], route[:, 4 * i + n, :], ident[:])
                last.then_inc(rt_pe, 1)
            pe.wait_ge(rt_sb, 4)
            for i in range(4):
                if i >= 2:
                    pe.wait_ge(b2_sb, i - 1)
                for n in range(4):
                    last = pe.matmul(S[2 + i % 2][:, P * n:P * n + P], routeT[:, 4 * i + n, :], b2r[:], start=True, stop=True)
                last.then_inc(b2_pe, 1)

    items_reduced, banks_free = sem("items_reduced"), sem("banks_free")
    strain_ready, gelu_done, th_ready = sem("strain_ready"), sem("gelu_done"), sem("th_ready")
    w1_staged, h_ready, xg_ready, sig_ready, s_ready, y_ready, y_used = (
        sem(n) for n in ("w1_staged", "h_ready", "xg_ready", "sig_ready", "s_ready", "y_ready", "y_used"))
    ad_pe, ad_sb, dh_ready, dl_ready = sem("ad_pe"), sem("ad_sb"), sem("dh_ready"), sem("dl_ready")
    sd_ready, sd_taken = sem("sd_ready"), sem("sd_taken")
    zm_ready, zt_ready, mx_ready, zs_ready, ex_ready = (sem(n) for n in ("zm_ready", "zt_ready", "mx_ready", "zs_ready", "ex_ready"))
    d_out = [sem("d_skew0"), sem("d_skew1")]
    d_in = [sem("d_band_in0"), sem("d_band_in1")]
    band_pe, band_act, band_dve, vw_pe, vw_sb, nd_pe, rc_ready, att_ready = (
        sem(n) for n in ("band_pe", "band_act", "band_dve", "vw_pe", "vw_sb", "nd_pe", "rc_ready", "att_ready"))
    vp_zero, cp_pe = sem("vp_zero"), sem("cp_pe")

    for g in range(G):
        with ExitStack() as lp:
            ring = sb(f"ring{g}", [P, RING, 2, B, T], F32, lp)
            xg = sb(f"xg{g}", [P, 2, T], F32, lp)
            t2 = sb(f"t2{g}", [P, 2, T], F32, lp)
            w1s = sb(f"w1s{g}", [P, I0], F32, lp)
            LG = psum(f"LG{g}", [P, 2, 2, T], lp)
            SD = psum(f"SD{g}", [P, 2, T], lp)
            PH = psum(f"PH{g}", [P, T], lp)
            PY = psum(f"PY{g}", [P, 4, C], lp)
            block = lp.enter_context(nc.Block())
            N0 = g * WIN
            Q0 = g * JQ
            U0 = g * 32
            D0 = g * 8

            def runs(engine, body):
                with engine.Fori(0, 3) as it:
                    body(it, 32, 32)
                body(3, 32, 0)
                with engine.Fori(4, 7) as it:
                    body(it, 0, 0)
                body(7, 0, None)

            @block.gpsimd
            def _(pool):
                if g == 0:
                    pool.sem_inc(items_reduced, RING)
                    pool.sem_inc(banks_free, 2)
                    pool.sem_inc(y_used, 1)
                    pool.sem_inc(xg_ready, 1)
                def stage(it):
                    pool.tensor_copy(w1s[:], w1T[:, bass.ds(HG * g + it, 1), :]).then_inc(w1_staged, 1)
                stage(0)
                pool.memset(Z[:, 0:8, 0:32], 0.0)
                with pool.Fori(0, 7) as it:
                    pool.wait_ge(h_ready, U0 + 4 * it + 4)
                    stage(it + 1)

            @block.vector
            def _(v):
                for i in range(4):
                    v.wait_ge(ad_pe, 8 * g + 2 * i + 2)
                    v.tensor_copy(AD[:, i // 2, 2 * (i % 2) + 1, PAD:PAD + T], LG[:, i % 2, 1, :]).then_inc(ad_sb, 1)
                v.wait_ge(ad_sb, 8 * g + 8)

                def item(n, j, t0):
                    slot = n % RING
                    v.wait_ge(items_reduced, N0 + j + 1)
                    for s, extra in ((0, PT[:, bass.ds(j, 1)]), (1, bdmg[:, 0:1])):
                        if s == 0 or n not in PE_ITEMS:
                            ins = v.scalar_tensor_tensor(out=ring[:, slot, s, :, t0:T], in0=AD[:, s, :, bass.ds(j + t0, T - t0)],
                                                         scalar=extra, in1=AD[:, s, :, PAD + t0:PAD + T],
                                                         op0=ALU.add, op1=ALU.subtract)
                    ins.then_inc(strain_ready, 1)

                def logits(par, q, t0):
                    v.wait_ge(th_ready, Q0 + q + 1)
                    zq = Z[:, bass.ds(q, 1), t0:T].rearrange("p o t -> p (o t)")
                    v.scalar_tensor_tensor(out=zq, in0=zq, scalar=-5.0, in1=LG[:, par, 0, t0:T], op0=ALU.mult, op1=ALU.add
                                           ).then_inc(banks_free, 1)

                def glu_in(c, it, u):
                    v.wait_ge(h_ready, u + 1)
                    v.tensor_scalar(xg[:, c % 2, :], PH[:], b1T[:, bass.ds(HG * g + it, 1)], LIMIT,
                                    ALU.add, ALU.min).then_inc(xg_ready, 1)

                def glu_out(c, u):
                    v.wait_ge(sig_ready, u + 1)
                    v.scalar_tensor_tensor(out=xg[:, c % 2, :], in0=t2[:, c % 2, :], scalar=1.0, in1=xg[:, c % 2, :],
                                           op0=ALU.add, op1=ALU.mult).then_inc(s_ready, 1)

                def combine(c, it, u):
                    v.wait_ge(y_ready, u + 1)
                    for i in range(4):
                        a = ACC[:, 4 * c + i, :]
                        ins = v.scalar_tensor_tensor(out=a, in0=PY[:, i, :], scalar=route[:, 4 * c + i, bass.ds(HG * g + it, 1)],
                                                     in1=a, op0=ALU.mult, op1=ALU.add)
                    ins.then_inc(y_used, 1)

                def body(it, t0, t0_next):
                    j, u = 8 * it, U0 + 4 * it
                    glu_in(0, it, u)
                    item(3, j + 3, t0)
                    item(4, j + 4, t0)
                    glu_out(0, u)
                    glu_in(1, it, u + 1)
                    item(5, j + 5, t0)
                    combine(0, it, u)
                    glu_out(1, u + 1)
                    glu_in(2, it, u + 2)
                    item(6, j + 6, t0)
                    item(7, j + 7, t0)
                    combine(1, it, u + 1)
                    glu_out(2, u + 2)
                    glu_in(3, it, u + 3)
                    logits(0, 2 * it, t0)
                    if t0_next is not None:
                        item(0, j + 8, t0_next)
                    combine(2, it, u + 2)
                    glu_out(3, u + 3)
                    if t0_next is not None:
                        item(1, j + 9, t0_next)
                    combine(3, it, u + 3)
                    if t0_next is not None:
                        item(2, j + 10, t0_next)
                    logits(1, 2 * it + 1, t0)

                item(0, 0, 32)
                v.wait_ge(dh_ready, g + 1)
                v.tensor_tensor(DHL[:, 1], AD[:, 1], DHL[:, 0].bitcast(F32), ALU.subtract).then_inc(dl_ready, 1)
                item(1, 1, 32)
                item(2, 2, 32)
                runs(v, body)

            @block.scalar
            def _(act):
                for i in range(4):
                    act.wait_ge(ad_pe, 8 * g + 2 * i + 1)
                    act.copy(AD[:, i // 2, 2 * (i % 2), PAD:PAD + T], LG[:, i % 2, 0, :]).then_inc(ad_sb, 1)

                def gelu(n, it, t0):
                    j, slot = 8 * it + n, n % RING
                    act.wait_ge(strain_ready, N0 + j + 1)
                    if n not in PE_ITEMS:
                        tiles = ring[:, slot, :, :, t0:T]
                        act.activation(tiles, tiles, ACT.Gelu).then_inc(gelu_done, 1)
                        return
                    f = 2 * (NPE * (D0 + it) + PE_ITEMS.index(n))
                    act.wait_ge(sd_ready, f + 1)
                    act.activation(ring[:, slot, 1, 0:2, t0:T], SD[:, :, t0:T], ACT.Gelu, bias=bdmg[:, 0:1]).then_inc(sd_taken, 1)
                    tiles = ring[:, slot, 0, :, t0:T]
                    act.activation(tiles, tiles, ACT.Gelu)
                    act.wait_ge(sd_ready, f + 2)
                    act.activation(ring[:, slot, 1, 2:4, t0:T], SD[:, :, t0:T], ACT.Gelu, bias=bdmg[:, 0:1]).then_inc(gelu_done, 1)

                def tanh(par, q, t0):
                    act.wait_ge(items_reduced, RING + N0 + 4 * q + 4)
                    act.activation(Z[:, bass.ds(q, 1), t0:T].rearrange("p o t -> p (o t)"), LG[:, par, 1, t0:T], ACT.Tanh,
                                   bias=bdo[:, 0:1], scale=0.5).then_inc(th_ready, 1)

                def sig(c, u):
                    act.wait_ge(xg_ready, u + 2)
                    act.activation(t2[:, c % 2, :], xg[:, c % 2, :], ACT.Tanh, scale=ALPHA / 2).then_inc(sig_ready, 1)

                def body(it, t0, t0_next):
                    u = U0 + 4 * it
                    gelu(1, it, t0)
                    sig(0, u)
                    gelu(2, it, t0)
                    gelu(3, it, t0)
                    sig(1, u + 1)
                    gelu(4, it, t0)
                    tanh(0, 2 * it, t0)
                    gelu(5, it, t0)
                    sig(2, u + 2)
                    gelu(6, it, t0)
                    gelu(7, it, t0)
                    sig(3, u + 3)
                    if t0_next is not None:
                        gelu(0, it + 1, t0_next)
                    tanh(1, 2 * it + 1, t0)

                act.wait_ge(ad_sb, 8 * g + 8)
                if g:
                    act.wait_ge(items_reduced, RING + N0)
                act.copy(DHL[:, 0], AD[:, 1]).then_inc(dh_ready, 1)
                gelu(0, 0, 32)
                runs(act, body)

            @block.tensor
            def _(pe):
                for i in range(8):
                    s, b = i // 4, i % 4
                    bank = LG[:, (i // 2) % 2, i % 2, :]
                    if i >= 4:
                        pe.wait_ge(ad_sb, 8 * g + 4)
                    pe.matmul(bank, wad[:, g, s, :], xnT[:, b, PAD:PAD + T], start=True, stop=True).then_inc(ad_pe, 1)
                pe.wait_ge(ad_sb, 8 * g + 8)

                def reduce(n, j, q, t0):
                    slot, par = n % RING, (n // 4) % 2
                    if n % 4 == 0:
                        pe.wait_ge(banks_free, Q0 + q + 1)
                    pe.wait_ge(gelu_done, N0 + j + 1)
                    for s in range(2):
                        for b in range(B):
                            mm = pe.matmul(LG[32 * b:32 * b + 32, par, s, t0:T], lred[:, s, n % 4, :], ring[:, slot, s, b, t0:T],
                                           start=(n % 4 == 0), stop=(n % 4 == 3))
                    mm.then_inc(items_reduced, 1)

                def strain(n, it, half, t0):
                    if half:
                        pe.wait_ge(sd_taken, NPE * (D0 + it) + PE_ITEMS.index(n) + 1)
                    for part in range(2):
                        for i in range(2):
                            pe.matmul(SD[:, i, t0:T], eyes[:, 0, :], DHL[:, part, 2 * half + i, bass.ds(8 * it + n + t0, T - t0)],
                                      start=(part == 0), stop=False)
                    for part in range(2):
                        for i in range(2):
                            mm = pe.matmul(SD[:, i, t0:T], eyes[:, 1, :], DHL[:, part, 2 * half + i, PAD + t0:PAD + T],
                                           start=False, stop=(part == 1))
                    mm.then_inc(sd_ready, 1)

                def hidden(c, u, staged):
                    pe.wait_ge(w1_staged, staged)
                    pe.wait_ge(xg_ready, u + 1)
                    pe.matmul(PH[:], w1s[:], tT[:, c, :], start=True, stop=True).then_inc(h_ready, 1)

                def expert_out(c, it, u):
                    pe.wait_ge(s_ready, u + 1)
                    pe.wait_ge(y_used, u + 1)
                    for i in range(4):
                        mm = pe.matmul(PY[:, i, :], xg[:, c % 2, P * i:P * i + P], w2T[:, bass.ds(HG * g + it, 1), :].rearrange("p o c -> p (o c)"),
                                       start=True, stop=True)
                    mm.then_inc(y_ready, 1)

                def body(it, t0, t0_next):
                    j, u, w = 8 * it, U0 + 4 * it, HG * g + it + 1
                    strain(1, it, 1, t0)
                    reduce(0, j, 2 * it, t0)
                    hidden(1, u + 1, w)
                    reduce(1, j + 1, 2 * it, t0)
                    strain(4, it, 0, t0)
                    expert_out(0, it, u)
                    reduce(2, j + 2, 2 * it, t0)
                    hidden(2, u + 2, w)
                    strain(4, it, 1, t0)
                    reduce(3, j + 3, 2 * it, t0)
                    expert_out(1, it, u + 1)
                    reduce(4, j + 4, 2 * it + 1, t0)
                    strain(6, it, 0, t0)
                    hidden(3, u + 3, w)
                    strain(6, it, 1, t0)
                    reduce(5, j + 5, 2 * it + 1, t0)
                    reduce(6, j + 6, 2 * it + 1, t0)
                    if t0_next is not None:
                        strain(1, it + 1, 0, t0_next)
                    expert_out(2, it, u + 2)
                    if t0_next is not None:
                        hidden(0, u + 4, w + 1)
                    reduce(7, j + 7, 2 * it + 1, t0)
                    expert_out(3, it, u + 3)

                hidden(0, U0, HG * g + 1)
                pe.wait_ge(dl_ready, g + 1)
                strain(1, 0, 0, 32)
                runs(pe, body)

        with ExitStack() as sm:
            vp = sb(f"vp{g}", [P, 8, HG, 32], F32, sm)
            zs = sb(f"zs{g}", [P, 2, 32, JQ, 4], F32, sm)
            wide = sb(f"wide{g}", [P, 2, 32, P], F32, sm)
            wtT = sb(f"wtT{g}", [P, 32, P], F32, sm)
            mx = sb(f"mx{g}", [P, 2, 32], F32, sm)
            rc = sb(f"rc{g}", [P, 2, P], F32, sm)
            ZT = psum(f"ZT{g}", [P, JQ, P], sm)
            W = [psum(f"W{g}{i}", [P, 4, P], sm) for i in range(4)]
            block = sm.enter_context(nc.Block())
            M0 = NT * g

            def steps(weigh, gather):
                weigh(0)
                for ti in range(1, NT):
                    weigh(ti)
                    gather(ti - 1)
                gather(NT - 1)

            @block.gpsimd
            def _(pool):
                pool.memset(vp[:], 0.0).then_inc(vp_zero, 1)

            @block.sync
            def _(sp):
                for ti in range(NT):
                    m, par = M0 + ti, ti % 2
                    sp.wait_ge(ex_ready, m + 1)
                    for k in range(2):
                        dst = dram_rows(band, (par * 2 + k) * 32 * 64 * P, [[P + 1, 64], [64 * P, 32], [1, WIN]])
                        sp.dma_start(dst, zs[64 * k:64 * k + 64, par].rearrange("r n q j -> r n (q j)")).then_inc(d_out[par], 16)
                    sp.wait_ge(d_out[par], 32 * (m // 2 + 1))
                    if ti >= 2:
                        sp.wait_ge(band_pe, 8 * (m - 1))
                    for k in range(2):
                        sp.dma_start(wide[64 * k:64 * k + 64, par], band[par, k].rearrange("n r s -> r n s")).then_inc(d_in[par], 16)

            @block.vector
            def _(v):
                zh = Z[:, :, 0:WIN]
                v.tensor_tensor(zh, zh, mz[:], ALU.add).then_inc(zm_ready, 1)

                def weigh(ti):
                    m, par = M0 + ti, ti % 2
                    v.wait_ge(zt_ready, m + 1)
                    zt = ZT[:].rearrange("p q (n j) -> p n q j", j=4)
                    v.tensor_reduce(mx[:, par], zt, AX.XY, ALU.max).then_inc(mx_ready, 1)
                    v.wait_ge(mx_ready, m + 1)
                    if ti >= 2:
                        v.wait_ge(d_out[par], 32 * (m // 2))
                    v.tensor_tensor(zs[:, par], zt, mx[:, par].unsqueeze(2).unsqueeze(3).to_broadcast([P, 32, JQ, 4]),
                                    ALU.subtract).then_inc(zs_ready, 1)

                def gather(ti):
                    m = M0 + ti
                    for i in range(1, 8, 2):
                        v.wait_ge(band_pe, 8 * m + i + 1)
                        v.tensor_copy(wtT[:, 4 * i:4 * i + 4, :], W[i % 2][:]).then_inc(band_dve, 1)
                    v.wait_ge(nd_pe, m + 1)
                    v.reciprocal(rc[:], W[3][:, 0:2, :]).then_inc(rc_ready, 1)
                    v.wait_ge(rc_ready, m + 1)
                    v.tensor_tensor(attT[:, g, :, P * ti:P * ti + P], W[3][:, 2:4, :], rc[:], ALU.mult).then_inc(att_ready, 1)

                steps(weigh, gather)

            @block.scalar
            def _(act):
                def weigh(ti):
                    m, par = M0 + ti, ti % 2
                    act.wait_ge(zs_ready, m + 1)
                    act.activation(zs[:, par], zs[:, par], ACT.Exp).then_inc(ex_ready, 1)

                def gather(ti):
                    m = M0 + ti
                    act.wait_ge(vw_pe, m + 1)
                    act.wait_ge(vp_zero, g + 1)
                    act.wait_ge(nd_pe, m)
                    for hh in range(4):
                        ins = act.copy(vp[:, :, hh:HG:4, 8 * hh:8 * hh + 8],
                                       W[2][:].rearrange("p a c -> p (a c)").rearrange("p (n h e) -> p n h e", n=8, e=HS)[:, :, hh:HG:4, :])
                    ins.then_inc(vw_sb, 1)
                    for i in range(0, 8, 2):
                        act.wait_ge(band_pe, 8 * m + i + 1)
                        act.copy(wtT[:, 4 * i:4 * i + 4, :], W[i % 2][:]).then_inc(band_act, 1)

                steps(weigh, gather)

            @block.tensor
            def _(pe):
                def weigh(ti):
                    m = M0 + ti
                    pe.wait_ge(zs_ready, m)
                    for q in range(JQ):
                        mm = pe.transpose(ZT[:, q, :], Z[:, q, P * ti:P * ti + P], ident[:])
                    mm.then_inc(zt_ready, 1)

                def gather(ti):
                    m, par = M0 + ti, ti % 2
                    pe.wait_ge(vw_sb, m)
                    for n in range(8):
                        b, k = n // 2, 2 * ti + n % 2
                        mm = pe.matmul(W[2][:].rearrange("p a c -> p (a c)")[:, 64 * n:64 * n + 64], xnT[:, b, 64 * k:64 * k + P],
                                       wval[:, 64 * g:64 * g + 64], start=True, stop=True)
                    mm.then_inc(vw_pe, 1)
                    pe.wait_ge(d_in[par], 32 * (m // 2 + 1))
                    for i in range(8):
                        pe.wait_ge(band_dve if i % 2 else band_act, 4 * m + i // 2)
                        for n in range(4):
                            mm = pe.transpose(W[i % 2][:, n, :], wide[:, par, 4 * i + n, :], ident[:])
                        mm.then_inc(band_pe, 1)
                    pe.wait_ge(band_act, 4 * m + 4)
                    pe.wait_ge(band_dve, 4 * m + 4)
                    pe.wait_ge(vw_sb, m + 1)
                    pe.wait_ge(att_ready, m)
                    for bb in range(2):
                        for hh in range(4):
                            for t4 in range(4):
                                b, qd = 2 * bb + t4 // 2, t4 % 2
                                n = HG * b + 4 * qd + hh
                                pe.matmul(W[3][32 * t4:32 * t4 + 32, bb, :], lones[:, hh, :], wtT[:, n, :],
                                          start=(hh == 0), stop=(hh == 3))
                    for bb in range(2):
                        for k in range(2):
                            for hh in range(4):
                                for t4 in range(4):
                                    b, qd = 2 * bb + t4 // 2, t4 % 2
                                    n = HG * b + 4 * qd + hh
                                    mm = pe.matmul(W[3][32 * t4:32 * t4 + 32, 2 + bb, 64 * k:64 * k + 64],
                                                   vp[:, 2 * b + k, 4 * qd + hh, :], wtT[:, n, 64 * k:64 * k + 64],
                                                   start=(hh == 0), stop=(hh == 3))
                    mm.then_inc(nd_pe, 1)

                pe.wait_ge(zm_ready, g + 1)
                steps(weigh, gather)

    with ExitStack() as cp:
        O = [psum(f"O{i}", [P, 4, C], cp) for i in range(4)]
        block = cp.enter_context(nc.Block())

        @block.tensor
        def _(pe):
            for b in range(B):
                r = 64 * (b % 2)
                for i in range(NT):
                    for g in range(G):
                        mm = pe.matmul(O[b][:, i, :], attT[r:r + 64, g, b // 2, P * i:P * i + P], wcp[r:r + 64, g, :],
                                       start=(g == 0), stop=(g == G - 1))
                mm.then_inc(cp_pe, 1)

        @block.vector
        def _(v):
            for b in range(B):
                v.wait_ge(cp_pe, b + 1)
                a = ACC[:, NT * b:NT * b + NT, :]
                v.tensor_tensor(a, a, O[b][:], ALU.add)


def second_layer(nc, t_in, out, l1, sb, psum, sem, ident, ACC, nhalf, stats, mv, rstd):
    xT = sb("xT", [P, B, T], F32, l1)
    W1 = sb("W1", [P, E1, FF], F32, l1)
    W2 = sb("W2", [P, E1, FQ, C], F32, l1)
    b1c = sb("b1c", [P, E1, FQ], F32, l1)
    rw1 = sb("rw1", [P, FF], F32, l1)
    rb1c = sb("rb1c", [P, FQ], F32, l1)
    rw2 = sb("rw2", [P, FQ, E1], F32, l1)
    wq = sb("wq", [P, HQ, 4, 4, 8], F32, l1)
    wk = sb("wk", [P, HQ, 4, 4, 8], F32, l1)
    wv = sb("wv", [P, C], F32, l1)
    wo = sb("wo", [P, HQ, C], F32, l1)
    gate = sb("gate", [P, TT, E1], F32, l1)
    gateT = sb("gateT", [E1, TT, P], F32, l1)
    b2r1 = sb("b2r1", [E1, C], F32, l1)
    neglo = sb("neglo", [P, 2], F32, l1)
    onesrow = sb("onesrow", [P, 1], F32, l1)
    zcol = sb("zcol", [P, 1], F32, l1)
    sel = sb("sel", [P, P], F32, l1)
    outd = out.rearrange("b t c -> (b t) c").rearrange("(n p) c -> p n c", p=P)

    d_w = [sem(f"l1_w{i}") for i in range(3)]
    with ExitStack() as su:
        wqkv = sb("wqkv", [P, 3, C], F32, su)
        XN = sb("XN2", [P, TT, C], F32, su)
        b1r = sb("b1r1", [E1 * FQ, P], F32, su)
        rb1r = sb("rb1r", [FQ, P], F32, su)
        rb2 = sb("rb2", [P, E1], F32, su)
        HR = sb("HR", [P, FQ, B, T], F32, su)
        sc = sb("sc", [P, TT, E1], F32, su)
        m8 = sb("m81", [P, TT, 8], F32, su)
        gt = sb("gt1", [P, TT, E1], F32, su)
        eq = sb("eq1", [P, TT, E1], F32, su)
        c0 = sb("c01", [P, TT, E1], F32, su)
        c1 = sb("c11", [P, TT, E1], F32, su)
        small = sb("small1", [P, 2, TT], F32, su)
        ones = sb("ones1", [P, P], F32, su)
        S = [psum(f"sv{i}", [P, 512], su) for i in range(8)]
        block = su.enter_context(nc.Block())
        s_pool, s_dve = Count(sem("sv_pool")), Count(sem("sv_dve"))
        mv_ready, rstd_ready, xn_ready = sem("mv_ready1"), sem("rstd_ready1"), sem("xn_ready1")
        w_zero, w_ready, xT_pe, xT_sb = sem("w_zero"), sem("w_ready"), sem("xT_pe"), sem("xT_sb")
        b_pe, b_sb, hr_pe, hr_sb, sc_pe = sem("b_pe"), sem("b_sb"), sem("hr_pe"), sem("hr_sb"), sem("sc_pe")
        exp_ready, exp_done, gate_ready = sem("exp_ready1"), sem("exp_done1"), sem("gate_ready")
        gt_pe, gt_sb, b2_pe, b2_sb = sem("gt_pe"), sem("gt_sb"), sem("b2_pe1"), sem("b2_sb1")

        @block.sync
        def _(sp):
            with nc.allow_non_contiguous_dma(reason="small weights"):
                sp.dma_start(wqkv[:], t_in["L1_attn_w_qkv"].rearrange("k (s n) -> k s n", s=3)).then_inc(d_w[0], 16)
                sp.dma_start(wv[:], t_in["L1_attn_w_qkv"][:, 2 * C:3 * C]).then_inc(d_w[0], 16)
                sp.dma_start(rw1[:], t_in["L1_ffn_rw1"]).then_inc(d_w[0], 16)
                sp.dma_start(rb1r[:], t_in["L1_ffn_rb1"].rearrange("(a p) -> a p", p=P)).then_inc(d_w[0], 16)
                sp.dma_start(rw2[:], t_in["L1_ffn_rw2"].rearrange("(a p) e -> p a e", p=P)).then_inc(d_w[0], 16)
                sp.dma_start(rb2[:], dram_rows(t_in["L1_ffn_rb2"], 0, [[0, P], [1, E1]])).then_inc(d_w[0], 16)
                sp.dma_start(b1r[:], t_in["L1_ffn_b1"].rearrange("e (a p) -> (e a) p", p=P)).then_inc(d_w[0], 16)
                sp.dma_start(b2r1[:], t_in["L1_ffn_b2"]).then_inc(d_w[0], 16)
                sp.dma_start(W1[:], t_in["L1_ffn_W1"].rearrange("e k f -> k e f")).then_inc(d_w[1], 16)
                sp.dma_start(W2[:], t_in["L1_ffn_W2"].rearrange("e (a p) c -> p e a c", p=P)).then_inc(d_w[1], 16)
                sp.wait_ge(w_zero, 1)
                wout = t_in["L1_attn_w_out"].rearrange("(q h e) n -> h e q n", q=HQ, e=HD)
                for hh in range(4):
                    sp.dma_start(wo[32 * hh:32 * hh + HD, :, :], wout[hh]).then_inc(d_w[2], 16)
            sp.wait_ge(d_w[1], 32)
            sp.wait_ge(d_w[2], 64)

        @block.gpsimd
        def _(pool):
            link = chain_of(pool, s_pool)
            pool.memset(wo[:], 0.0).then_inc(w_zero, 1)
            pool.memset(wq[:], 0.0)
            pool.memset(wk[:], 0.0)
            link(pool.memset(ones[:], 1.0))
            pool.wait_ge(mv_ready, 1)
            link(pool.tensor_scalar(rstd[:], mv[:, :, 1], EPS, 1.0, ALU.add, ALU.mult))
            pool.tensor_tensor(rstd[:], rstd[:], nhalf[:], ALU.pow).then_inc(rstd_ready, 1)
            def pick(out_ap, in_ap, op, base, pattern, mult, fill):
                return pool.affine_select(out=out_ap, in_=in_ap, compare_op=op, fill=fill, base=base, pattern=pattern,
                                          channel_multiplier=mult)
            link(pool.memset(sel[:], 0.0))
            link(pick(sel[:].rearrange("p (a c) -> p a c", a=4), sel[:].rearrange("p (a c) -> p a c", a=4), ALU.not_equal,
                      -HD, [[-32, 4], [0, 32]], 1, 1.0))
            def rows(lo, hi, dst):
                pool_tmp = small[:, 0, 0:4]
                link(pick(pool_tmp, ones[:, 0:4], ALU.is_ge, -lo, [[-32, 4]], 1, 0.0))
                link(pick(pool_tmp, pool_tmp, ALU.is_ge, hi, [[32, 4]], -1, 0.0))
                link(pool.tensor_tensor(small[:, 1, 0:2], small[:, 0, 0:2], small[:, 0, 2:4], ALU.add))
                link(pool.tensor_tensor(dst, small[:, 1, 0:1], small[:, 1, 1:2], ALU.add))
            rows(16, 23, neglo[:, 0:1])
            rows(8, 15, neglo[:, 1:2])
            link(pool.tensor_scalar(neglo[:], neglo[:], -1.0, 1.0, ALU.mult, ALU.mult))
            rows(24, 25, onesrow[:, 0:1])
            link(pool.tensor_tensor(neglo[:, 1:2], neglo[:, 1:2], onesrow[:], ALU.add))
            pool.memset(zcol[:], 0.0)
            pool.wait_ge(d_w[0], 16 * 8)
            for q in range(HQ):
                for dst, n in ((wq, 0), (wk, 1)):
                    for s in range(3):
                        last = pool.tensor_copy(dst[:, q, :, s, :], wqkv[:, n, 32 * q:32 * q + 32].rearrange("p (h d) -> p h d", d=HD))
            last.then_inc(w_ready, 1)

        @block.vector
        def _(v):
            link = chain_of(v, s_dve)
            for t in range(TT):
                last = v.bn_stats(stats[:, t, :], ACC[:, t, :])
            link(last)
            for t in range(TT):
                last = v.bn_aggr(mv[:, t, :], stats[:, t, :])
            last.then_inc(mv_ready, 1)
            v.wait_ge(rstd_ready, 1)
            for t in range(TT):
                last = v.tensor_scalar(XN[:, t, :], ACC[:, t, :], mv[:, t, 0:1], rstd[:, t:t + 1], ALU.subtract, ALU.mult)
            last.then_inc(xn_ready, 1)
            v.wait_ge(b_pe, 1)
            v.tensor_copy(b1c[:].rearrange("p e a -> p (e a)"), S[0][:, 0:E1 * FQ])
            v.tensor_copy(rb1c[:], S[0][:, 64:64 + FQ]).then_inc(b_sb, 1)
            v.wait_ge(sc_pe, 1)
            v.wait_ge(w_ready, 1)
            link(v.tensor_tensor(sc[:], S[1][:, 0:TT * E1].rearrange("p (t e) -> p t e", e=E1),
                                 rb2[:].unsqueeze(1).to_broadcast([P, TT, E1]), ALU.add))
            top_k_route(v, link, sc, gate, m8, gt, eq, c0, c1, small, E1, K1, exp_ready, exp_done).then_inc(gate_ready, 1)
            for i in range(4):
                v.wait_ge(gt_pe, i + 1)
                v.tensor_copy(gateT[:, 4 * i:4 * i + 4, :].rearrange("e t p -> e (t p)"), S[2 + i % 2][0:E1, :]).then_inc(gt_sb, 1)
            for i in range(4):
                v.wait_ge(b2_pe, i + 1)
                a = ACC[:, 4 * i:4 * i + 4, :].rearrange("p t c -> p (t c)")
                v.tensor_tensor(a, a, S[2 + i % 2][:, :], ALU.add).then_inc(b2_sb, 1)

        @block.scalar
        def _(act):
            for b in range(B):
                act.wait_ge(xT_pe, b + 1)
                act.copy(xT[:, b, :], S[2 + b][:, :]).then_inc(xT_sb, 1)
            act.wait_ge(b_sb, 1)
            for i in range(16):
                a, b = i % 4, i // 4
                act.wait_ge(hr_pe, i + 1)
                act.activation(HR[:, a, b, :], S[2 + i % 6][:, :], ACT.Relu, bias=rb1c[:, a:a + 1]).then_inc(hr_sb, 1)
            act.wait_ge(exp_ready, 1)
            act.activation(gate[:], gate[:], ACT.Exp).then_inc(exp_done, 1)

        @block.tensor
        def _(pe):
            pe.wait_ge(d_w[0], 16 * 8)
            pe.transpose(S[0][:, 0:E1 * FQ], b1r[:], ident[0:E1 * FQ, 0:E1 * FQ])
            pe.transpose(S[0][:, 64:64 + FQ], rb1r[:], ident[0:FQ, 0:FQ]).then_inc(b_pe, 1)
            pe.wait_ge(xn_ready, 1)
            for b in range(B):
                for i in range(NT):
                    last = pe.transpose(S[2 + b][:, P * i:P * i + P], XN[:, NT * b + i, :], ident[:])
                last.then_inc(xT_pe, 1)
            pe.wait_ge(xT_sb, B)
            for i in range(16):
                a, b = i % 4, i // 4
                if i >= 6:
                    pe.wait_ge(hr_sb, i - 5)
                pe.matmul(S[2 + i % 6][:, :], rw1[:, P * a:P * a + P], xT[:, b, :], start=True, stop=True).then_inc(hr_pe, 1)
            pe.wait_ge(hr_sb, 16)
            for t in range(TT):
                for a in range(FQ):
                    last = pe.matmul(S[1][:, E1 * t:E1 * t + E1], HR[:, a, t // NT, P * (t % NT):P * (t % NT) + P], rw2[:, a, :],
                                     start=(a == 0), stop=(a == FQ - 1))
            last.then_inc(sc_pe, 1)
            pe.wait_ge(gate_ready, 1)
            for i in range(4):
                if i >= 2:
                    pe.wait_ge(gt_sb, i - 1)
                for n in range(4):
                    last = pe.transpose(S[2 + i % 2][0:E1, P * n:P * n + P], gate[:, 4 * i + n, :], ident[:])
                last.then_inc(gt_pe, 1)
            pe.wait_ge(gt_sb, 4)
            for i in range(4):
                if i >= 2:
                    pe.wait_ge(b2_sb, i - 1)
                for n in range(4):
                    last = pe.matmul(S[2 + i % 2][:, P * n:P * n + P], gateT[:, 4 * i + n, :], b2r1[:], start=True, stop=True)
                last.then_inc(b2_pe, 1)

    KS = sb("KS", [P, HQ, T], F32R, l1)
    QS = sb("QS", [P, HQ, T], F32R, l1)
    hi = sb("hi", [P, 2, 2, T], F32, l1)
    XB = sb("XB", [P, T], F32, l1)
    VA = sb("VA", [P, NT, H1, 32], F32, l1)
    MX = sb("MX", [P, NT, HQ, 4], F32, l1)
    NX = sb("NX", [P, NT, HQ, 4, 32], F32, l1)
    EX = sb("EX", [P, 2, 4, NT, T], F32, l1)
    ND = sb("ND", [P, 2, T], F32, l1)
    RC = sb("RC", [P, T], F32, l1)
    AT = sb("AT", [P, HQ, T], F32, l1)
    HB = sb("HB", [P, 2, FQ, T], F32, l1)
    SS = psum("SS", [P, 2, 2, T], l1)
    PHh = psum("PHh", [P, 2, T], l1)
    PYy = psum("PYy", [P, 4, C], l1)
    PN = psum("PN", [P, T], l1)
    block = l1.enter_context(nc.Block())

    tasks = ["q0", "q1", "k0", "k1", "v"] + [f"s{h}.{i}" for h in range(H1) for i in range(2)] + ["t0", "t1"]
    for q in range(HQ):
        tasks += [f"e{h}.{i}" for h in range(4 * q, 4 * q + 4) for i in range(2)]
        if q >= 1:
            tasks += [f"d{q - 1}"]
    tasks += [f"d{HQ - 1}", "o"]
    USES = len(tasks)
    assert USES % 2 == 0
    use = {name: n for n, name in enumerate(tasks)}
    filled = sem("slot_filled")
    freed = [sem("slot0_freed"), sem("slot1_freed")]
    ms_ready, xb_ready, hi_ready, nx_hi, nx_ready = (sem(n) for n in ("ms_ready", "xb_ready", "hi_ready", "nx_hi", "nx_ready"))
    nd_ready, nd_copied, at_ready = (sem(n) for n in ("nd_ready1", "nd_copied", "at_ready"))
    h_ready, h_relu, y_ready, y_used, d_done = (sem(n) for n in ("h_ready1", "h_relu", "y_ready1", "y_used1", "d_done"))
    UH, UE = E1 * FQ, E1

    def slot_of(name):
        return use[name] % 2

    def is_filled(b, name):
        return USES * b + use[name] + 1

    def may_fill(b, name):
        return (USES // 2) * b + use[name] // 2 + 1

    def is_emptied(b, name):
        return may_fill(b, name) + 1

    blocks = [("h", 0)]
    for e in range(1, E1):
        blocks += [("h", e), ("y", e - 1)]
    blocks += [("y", E1 - 1)]

    def pieces(first, end):
        return [(*blocks[n // 4], n % 4) for n in range(first, end)]

    def after_scores(h):
        return 12 + 3 * h // 2, 12 + 3 * (h + 1) // 2

    @block.sync
    def _(sp):
        with sp.Fori(0, B) as b:
            sp.wait_ge(freed[slot_of("o")], is_emptied(b, "o"))
            sp.dma_start(outd[:, bass.ds(NT * b, NT), :], ACC[:, bass.ds(NT * b, NT), :]).then_inc(d_done, 16)
        sp.wait_ge(d_done, 16 * B)

    @block.gpsimd
    def _(pool):
        pool.sem_inc(freed[0], 1)
        pool.sem_inc(freed[1], 1)
        pool.sem_inc(h_relu, 2)
        pool.sem_inc(y_ready, 2)
        pool.sem_inc(y_used, 1)
        pool.sem_inc(nd_copied, 1)
        pool.sem_inc(at_ready, 2)
        pool.memset(NX[:], 0.0)
        pool.memset(VA[:], 0.0).then_inc(ms_ready, 1)
        pool.wait_ge(ms_ready, 1)
        pool.memset(VA[:, :, :, HD:HD + 1], 1.0).then_inc(ms_ready, 1)

    @block.tensor
    def _(pe):
        def fill(b, name):
            pe.wait_ge(freed[slot_of(name)], may_fill(b, name))
            return SS[:, slot_of(name), :, :]

        def experts(b, first, end):
            for kind, e, n in pieces(first, end):
                if kind == "h":
                    pe.wait_ge(h_relu, UH * b + FQ * e + n + 1)
                    pe.matmul(PHh[:, n % 2, :], W1[:, e, P * n:P * n + P], XB[:], start=True, stop=True).then_inc(h_ready, 1)
                    continue
                if n == 0:
                    pe.wait_ge(h_relu, UH * b + FQ * e + FQ + 2)
                    pe.wait_ge(y_used, UE * b + e + 1)
                for a in range(FQ):
                    mm = pe.matmul(PYy[:, n, :], HB[:, e % 2, a, P * n:P * n + P], W2[:, e, a, :],
                                   start=(a == 0), stop=(a == FQ - 1))
                if n == NT - 1:
                    mm.then_inc(y_ready, 1)

        def project(b, w, name):
            bank = fill(b, name)
            for n in range(2):
                mm = pe.matmul(bank[:, n, :], w[:, 2 * int(name[1]) + n].rearrange("p h s d -> p (h s d)"), XB[:], start=True, stop=True)
            mm.then_inc(filled, 1)

        def scores(b, h, kind):
            r, q = 32 * (h % 4), h // 4
            rows, cols = (QS, KS) if kind == "s" else (KS, QS)
            for i in range(2):
                bank = fill(b, f"{kind}{h}.{i}")
                for n in range(2):
                    t = 2 * i + n
                    mm = pe.matmul(bank[:, n, :], rows[r:r + 32, q, P * t:P * t + P], cols[r:r + 32, q, :], start=True, stop=True)
                mm.then_inc(filled, 1)

        def values(b, q, t):
            if t == 0:
                for i in range(2):
                    pe.wait_ge(freed[slot_of(f"e{4 * q + 3}.{i}")], is_emptied(b, f"e{4 * q + 3}.{i}"))
                pe.wait_ge(nd_copied, HQ * b + q + 1)
            for hh in range(4):
                mm = pe.matmul(PN[32 * hh:32 * hh + 32, :], VA[:, t, 4 * q + hh, :], EX[:, q % 2, hh, t, :],
                               start=(t == 0), stop=(t == NT - 1))
            if t == NT - 1:
                mm.then_inc(nd_ready, 1)

        def sums(b, q):
            bank = fill(b, f"d{q}")
            pe.wait_ge(nd_copied, HQ * b + q + 2)
            pe.matmul(bank[:, 0, :], sel[:], ND[:, q % 2, :], start=True, stop=True).then_inc(filled, 1)

        pe.wait_ge(ms_ready, 2)
        with pe.Fori(0, B) as b:
            pe.wait_ge(xb_ready, b + 1)
            project(b, wq, "q0")
            project(b, wq, "q1")
            experts(b, 0, 4)
            project(b, wk, "k0")
            project(b, wk, "k1")
            bank = fill(b, "v")
            for i in range(NT):
                mm = pe.matmul(bank[:, 0, P * i:P * i + P], XB[:, P * i:P * i + P], wv[:], start=True, stop=True)
            mm.then_inc(filled, 1)
            experts(b, 4, 12)
            for k in ("k0", "k1"):
                pe.wait_ge(freed[slot_of(k)], is_emptied(b, k))
            for h in range(H1):
                scores(b, h, "s")
                experts(b, *after_scores(h))
            experts(b, 36, 40)
            pe.wait_ge(nx_ready, b + 1)
            for i in range(2):
                bank = fill(b, f"t{i}")
                for n in range(2):
                    for t in range(NT):
                        mm = pe.transpose(bank[:, n, P * t:P * t + P], NX[:, t, 2 * i + n].rearrange("p h r -> p (h r)"), ident[:])
                mm.then_inc(filled, 1)
            experts(b, 40, 44)
            for i in range(2):
                pe.wait_ge(freed[slot_of(f"t{i}")], is_emptied(b, f"t{i}"))
            for q in range(HQ):
                for hh in range(4):
                    scores(b, 4 * q + hh, "e")
                    if q == 0:
                        experts(b, 44 + hh, 45 + hh)
                    else:
                        values(b, q - 1, hh)
                if q >= 1:
                    experts(b, 44 + 4 * q, 46 + 4 * q)
                    sums(b, q - 1)
                    experts(b, 46 + 4 * q, 48 + 4 * q)
            for t in range(NT):
                values(b, HQ - 1, t)
            experts(b, 60, 62)
            sums(b, HQ - 1)
            experts(b, 62, 64)
            pe.wait_ge(at_ready, HQ * b + HQ + 2)
            bank = fill(b, "o")
            for i in range(NT):
                for q in range(HQ):
                    mm = pe.matmul(bank[:, 0, P * i:P * i + P], AT[:, q, P * i:P * i + P], wo[:, q, :],
                                   start=(q == 0), stop=(q == HQ - 1))
            mm.then_inc(filled, 1)

    @block.scalar
    def _(act):
        def experts(b, first, end):
            for kind, e, n in pieces(first, end):
                if kind == "h":
                    if n == 0:
                        act.wait_ge(y_ready, UE * b + e + 1)
                    act.wait_ge(h_ready, UH * b + FQ * e + n + 1)
                    act.activation(HB[:, e % 2, n, :], PHh[:, n % 2, :], ACT.Relu, bias=b1c[:, e, n:n + 1]).then_inc(h_relu, 1)

        def high_part(b, name):
            act.wait_ge(filled, is_filled(b, name))
            dst = hi[:, slot_of(name), :, :].bitcast(F32R)
            bias = zcol[:, 0:1] if name[0] == "q" else onesrow[:, 0:1]
            act.activation(dst, SS[:, slot_of(name), :, :], ACT.Identity, bias=bias).then_inc(hi_ready, 1)

        def exps(b, h):
            for i in range(2):
                name = f"e{h}.{i}"
                act.wait_ge(filled, is_filled(b, name))
                act.activation(EX[:, h // 4 % 2, h % 4, 2 * i:2 * i + 2, :], SS[:, slot_of(name), :, :], ACT.Exp, scale=SCALE1
                               ).then_inc(freed[slot_of(name)], 1)

        def copy_nd(b, q):
            act.wait_ge(nd_ready, HQ * b + q + 1)
            act.wait_ge(at_ready, HQ * b + q + 1)
            act.copy(ND[:, q % 2, :], PN[:]).then_inc(nd_copied, 1)

        act.wait_ge(ms_ready, 2)
        with act.Fori(0, B) as b:
            high_part(b, "q0")
            high_part(b, "q1")
            experts(b, 0, 4)
            high_part(b, "k0")
            high_part(b, "k1")
            act.wait_ge(filled, is_filled(b, "v"))
            act.copy(VA[:, :, :, 0:HD], SS[:, slot_of("v"), 0, :].rearrange("p (t h e) -> p t h e", t=NT, e=HD)
                     ).then_inc(freed[slot_of("v")], 1)
            experts(b, 4, 44)
            for q in range(HQ):
                if q >= 2:
                    act.wait_ge(nd_ready, HQ * b + q - 1)
                for hh in range(4):
                    exps(b, 4 * q + hh)
                    if q == 0:
                        experts(b, 44 + hh, 45 + hh)
                if q >= 1:
                    copy_nd(b, q - 1)
                    experts(b, 44 + 4 * q, 48 + 4 * q)
            copy_nd(b, HQ - 1)

    @block.vector
    def _(v):
        def low_part(b, name, dst):
            s = slot_of(name)
            i = int(name[1])
            v.wait_ge(hi_ready, 4 * b + use[name] + 1)
            v.scalar_tensor_tensor(out=dst[:, 2 * i:2 * i + 2, :], in0=hi[:, s, :, :],
                                   scalar=neglo[:, 0:1] if name[0] == "q" else neglo[:, 1:2],
                                   in1=SS[:, s, :, :], op0=ALU.mult, op1=ALU.add).then_inc(freed[s], 1)

        def maxima(b, h):
            for i in range(2):
                name = f"s{h}.{i}"
                v.wait_ge(filled, is_filled(b, name))
                v.tensor_reduce(MX[:, 2 * i:2 * i + 2, h // 4, h % 4], SS[:, slot_of(name), :, :], AX.X, ALU.max
                                ).then_inc(freed[slot_of(name)], 1)

        def experts(b, first, end):
            for kind, e, n in pieces(first, end):
                if kind == "y" and n == NT - 1:
                    v.wait_ge(y_ready, UE * b + e + 3)
                    for i in range(NT):
                        a = ACC[:, bass.ds(NT * b + i, 1), :].rearrange("p o c -> p (o c)")
                        ins = v.scalar_tensor_tensor(out=a, in0=PYy[:, i, :], scalar=gate[:, bass.ds(NT * b + i, 1), e],
                                                     in1=a, op0=ALU.mult, op1=ALU.add)
                    ins.then_inc(y_used, 1)

        def normalise(b, q):
            slot = slot_of(f"d{q}")
            v.wait_ge(filled, is_filled(b, f"d{q}"))
            v.wait_ge(at_ready, HQ * b + q + 2)
            v.reciprocal(RC[:], SS[:, slot, 0, :]).then_inc(freed[slot], 1)
            v.wait_ge(freed[slot], is_emptied(b, f"d{q}"))
            v.tensor_tensor(AT[:, q, :], ND[:, q % 2, :], RC[:], ALU.mult).then_inc(at_ready, 1)

        with v.Fori(0, B) as b:
            v.tensor_copy(XB[:], xT[:, bass.ds(b, 1), :].rearrange("p o t -> p (o t)")).then_inc(xb_ready, 1)
            for name, dst in (("q0", QS), ("q1", QS), ("k0", KS), ("k1", KS)):
                low_part(b, name, dst)
            experts(b, 4, 12)
            for h in range(H1):
                maxima(b, h)
                experts(b, *after_scores(h))
            for i in range(2):
                v.wait_ge(freed[slot_of(f"s15.{i}")], is_emptied(b, f"s15.{i}"))
            m = MX[:].rearrange("p t q h -> p (t q) h")
            nx = NX[:].rearrange("p t q h r -> p (t q) h r")
            v.tensor_scalar(nx[:, :, :, 24].bitcast(F32R), m, -1.0, None, ALU.mult).then_inc(nx_hi, 1)
            v.wait_ge(nx_hi, b + 1)
            v.scalar_tensor_tensor(out=nx[:, :, :, 25], in0=m, scalar=-1.0, in1=nx[:, :, :, 24], op0=ALU.mult,
                                   op1=ALU.subtract).then_inc(nx_ready, 1)
            for i in range(2):
                name = f"t{i}"
                v.wait_ge(filled, is_filled(b, name))
                part = QS[:, 2 * i:2 * i + 2, :]
                v.tensor_tensor(part, part.bitcast(F32), SS[:, slot_of(name), :, :], ALU.add).then_inc(freed[slot_of(name)], 1)
            experts(b, 40, 48)
            for q in range(1, HQ):
                normalise(b, q - 1)
                experts(b, 44 + 4 * q, 48 + 4 * q)
            normalise(b, HQ - 1)
            experts(b, 60, 64)
            v.wait_ge(filled, is_filled(b, "o"))
            v.wait_ge(y_used, UE * b + UE + 1)
            a = ACC[:, bass.ds(NT * b, NT), :].rearrange("p t c -> p (t c)")
            v.tensor_tensor(a, a, SS[:, slot_of("o"), 0, :], ALU.add).then_inc(freed[slot_of("o")], 1)


_OUT = ((B, T, C), "float32")


def kernel(**inputs):
    import numpy as np
    import concourse.bacc as bacc
    from concourse.bass_utils import run_bass_kernel_spmd

    nc = bacc.Bacc("TRN2", target_bir_lowering=False, num_devices=1)
    arrays, handles = {}, {}
    for name in inputs:
        a = np.ascontiguousarray(inputs[name])
        arrays[f"in_{name}"] = a
        handles[name] = nc.dram_tensor(f"in_{name}", a.shape, mybir.dt.from_np(a.dtype), kind="ExternalInput").ap()
    out = nc.dram_tensor("out", _OUT[0], F32, kind="ExternalOutput").ap()
    build(nc, handles, out)
    return run_bass_kernel_spmd(nc, [arrays], core_ids=[0]).results[0]["out"]
```

```python
from contextlib import ExitStack

import concourse.bass as bass
from concourse import mybir

F32 = mybir.dt.float32
F32R = mybir.dt.float32r
ALU = mybir.AluOpType
ACT = mybir.ActivationFunctionType
AX = mybir.AxisListType

P = 128
B, T, C = 4, 512, 128
NT = T // P
TT = B * NT
H0, BD, HS = 16, 16, 8
WIN = 64
G = 2
HG = H0 // G
PAD = WIN - 1
TP = PAD + T + 1
JQ = WIN // 4
E0, K0, I0 = 16, 4, 128
LIMIT, ALPHA = 7.0, 1.702
H1, HD = 16, 8
HQ = 4
E1, K1, FF = 8, 2, 512
FQ = FF // P
EPS = 1e-5
MASKED = -3.0e38
RING = 4
PE_ITEMS = (1, 4, 6)
NPE = len(PE_ITEMS)
SCALE1 = float(C) ** -0.5


class Count:

    def __init__(self, sem):
        self.sem, self.n = sem, 0

    def inc(self, instruction, by=1):
        instruction.then_inc(self.sem, by)
        self.n += by
        return self.n


def chain_of(engine, count):

    def link(instruction):
        engine.wait_ge(count.sem, count.inc(instruction))

    return link


def dram_rows(tensor, offset, dims):
    return bass.AP(tensor=tensor.tensor, offset=tensor.offset + offset, ap=dims)


def build(nc, t_in, out):
    ctx = ExitStack()
    with ctx:
        def sb(name, shape, dt=F32, where=ctx):
            return where.enter_context(nc.sbuf_tensor(name, shape, dt))

        def psum(name, shape, where=ctx):
            return where.enter_context(nc.psum_tensor(name, shape, F32))

        def sem(name):
            return ctx.enter_context(nc.semaphore(name))

        ident = sb("ident", [P, P])
        ACC = sb("ACC", [P, TT, C])
        nhalf = sb("nhalf", [P, TT])
        stats = sb("stats", [P, TT, 6])
        mv = sb("mv", [P, TT, 2])
        rstd = sb("rstd", [P, TT])
        attT = sb("attT", [P, G, 2, T])
        wcp = sb("wcp", [P, G, C])
        route = sb("route", [P, TT, E0])
        b2r = sb("b2r", [E0, C])
        carried = (attT, wcp, route, b2r)

        with ExitStack() as l0:
            first_layer(nc, t_in, l0, sb, psum, sem, ident, ACC, nhalf, stats, mv, rstd, carried)
        with ExitStack() as l1:
            second_layer(nc, t_in, out, l1, sb, psum, sem, ident, ACC, nhalf, stats, mv, rstd, carried)


def top_k_route(v, link, scores, route, m8, gt, eq, c0, c1, small, n_exp, k, exp_ready, exp_done):
    n = scores.shape[1]
    for t in range(n):
        last = v.max(m8[:, t, :], scores[:, t, :])
    link(last)
    full = [P, n, n_exp]
    kth = m8[:, :, k - 1:k].to_broadcast(full)
    v.tensor_tensor(gt[:], scores[:], kth, ALU.is_gt)
    link(v.tensor_tensor(eq[:], scores[:], kth, ALU.is_equal))
    v.tensor_reduce(small[:, 0, :], gt[:], AX.X, ALU.add)
    src, dst = eq, c0
    step = 1
    while step < n_exp:
        v.tensor_copy(dst[:, :, 0:step], src[:, :, 0:step])
        link(v.tensor_tensor(dst[:, :, step:], src[:, :, step:], src[:, :, :n_exp - step], ALU.add))
        src, dst = dst, (c1 if dst is c0 else c0)
        step *= 2
    link(v.tensor_scalar(small[:, 1, :], small[:, 0, :], -1.0, float(k), ALU.mult, ALU.add))
    need = small[:, 1, :].unsqueeze(2).to_broadcast(full)
    link(v.tensor_tensor(dst[:], src[:], need, ALU.is_le))
    link(v.tensor_tensor(dst[:], dst[:], eq[:], ALU.mult))
    link(v.tensor_tensor(gt[:], gt[:], dst[:], ALU.add))
    v.tensor_tensor(route[:], scores[:], m8[:, :, 0:1].to_broadcast(full), ALU.subtract).then_inc(exp_ready, 1)
    v.wait_ge(exp_done, 1)
    link(v.tensor_tensor(route[:], route[:], gt[:], ALU.mult))
    link(v.tensor_reduce(small[:, 0, :], route[:], AX.X, ALU.add))
    link(v.reciprocal(small[:, 1, :], small[:, 0, :]))
    return v.tensor_tensor(route[:], route[:], small[:, 1, :].unsqueeze(2).to_broadcast(full), ALU.mult)


def first_layer(nc, t_in, l0, sb, psum, sem, ident, ACC, nhalf, stats, mv, rstd, carried):
    x = t_in["L0_attn_x"].rearrange("b t c -> (b t) c").rearrange("(n p) c -> p n c", p=P)
    attT, wcp, route, b2r = carried

    xnT = sb("xnT", [P, B, TP], F32, l0)
    tT = sb("tT", [P, B, T], F32, l0)
    w1T = sb("w1T", [P, E0, I0], F32, l0)
    w2T = sb("w2T", [P, E0, C], F32, l0)
    b1T = sb("b1T", [P, E0], F32, l0)
    wad = sb("wad", [P, G, 2, P], F32, l0)
    PT = sb("PT", [P, WIN], F32, l0)
    lred = sb("lred", [P, 2, 4, 32], F32, l0)
    mz = sb("mz", [P, JQ, WIN], F32, l0)
    bdmg = sb("bdmg", [P, 1], F32, l0)
    bdo = sb("bdo", [P, 1], F32, l0)
    wval = sb("wval", [P, C], F32, l0)
    lones = sb("lones", [P, 4, 32], F32, l0)
    DHL = sb("DHL", [P, 2, B, TP], F32R, l0)
    eyes = sb("eyes", [P, 2, P], F32R, l0)
    AD = sb("AD", [P, 2, B, TP], F32, l0)
    Z = sb("Z", [P, JQ, T], F32, l0)

    d_x = [sem(f"d_x{b}") for b in range(B)]
    ad_pe, ad_sb, dh_ready, dl_ready = sem("ad_pe"), sem("ad_sb"), sem("dh_ready"), sem("dl_ready")
    d_attn_w, d_gate_w, d_mlp_w, d_band0 = sem("d_attn_w"), sem("d_gate_w"), sem("d_mlp_w"), sem("d_band0")
    band = nc.dram_tensor("band", [2, 2, 32, 64, P], F32, kind="Internal").ap()

    with ExitStack() as su:
        X = sb("X", [P, TT, C], F32, su)
        XN = sb("XN", [P, TT, C], F32, su)
        TF = sb("TF", [P, TT, C], F32, su)
        w1r = sb("w1r", [P, E0, C], F32, su)
        w2r = sb("w2r", [P, E0, C], F32, su)
        b1r = sb("b1r", [E0, 2 * I0], F32, su)
        wdisp = sb("wdisp", [P, G, P], F32, su)
        wdispT = sb("wdispT", [P, G, P], F32, su)
        wrep = sb("wrep", [P, 2, BD], F32, su)
        wcol = sb("wcol", [P, 2], F32, su)
        wblk = sb("wblk", [P, 2, HG, BD], F32, su)
        rel = sb("rel", [WIN, BD], F32, su)
        relT = sb("relT", [BD, WIN], F32, su)
        wpos = sb("wpos", [BD, HG, BD], F32, su)
        gw = sb("gw", [E0, C], F32, su)
        gwT = sb("gwT", [P, 32], F32, su)
        gscT = sb("gscT", [P, T], F32, su)
        gb = sb("gb", [P, E0], F32, su)
        scl = sb("scl", [P, 1], F32, su)
        mask8 = sb("mask8", [P, HG], F32, su)
        ones8 = sb("ones8", [P, HG], F32, su)
        mt = sb("mt", [WIN, WIN], F32, su)
        mt2 = sb("mt2", [WIN, JQ, 32, 4], F32, su)
        ss = sb("ss", [P, TT], F32, su)
        r2 = sb("r2", [P, TT], F32, su)
        gsc = sb("gsc", [P, TT, E0], F32, su)
        m8 = sb("m8", [P, TT, 8], F32, su)
        gt = sb("gt", [P, TT, E0], F32, su)
        eq = sb("eq", [P, TT, E0], F32, su)
        c0 = sb("c0", [P, TT, E0], F32, su)
        c1 = sb("c1", [P, TT, E0], F32, su)
        small = sb("small", [P, 2, TT], F32, su)
        S = [psum(f"su{i}", [P, 512], su) for i in range(8)]
        block = su.enter_context(nc.Block())

        s_pool, s_dve = Count(sem("su_pool")), Count(sem("su_dve"))
        mv_ready, rstd_ready, ss_ready, r2_ready = (sem(n) for n in ("mv_ready", "rstd_ready", "ss_ready", "r2_ready"))
        const_ready, xn_ready, tf_ready = sem("const_ready"), sem("xn_ready"), sem("tf_ready")
        blk_ready, zero_ready, mt_ready = sem("blk_ready"), sem("zero_ready"), sem("mt_ready")
        xnT_pe, tT_pe, xnT_sb, tT_sb = sem("xnT_pe"), sem("tT_pe"), sem("xnT_sb"), sem("tT_sb")
        wt_pe, wt_sb, wad_pe, wad_sb = sem("wt_pe"), sem("wt_sb"), sem("wad_pe"), sem("wad_sb")
        gate_pe, exp_ready, exp_done = sem("gate_pe"), sem("exp_ready"), sem("exp_done")
        misc_pe, misc_sb, mlp_pe, mlp_sb = sem("misc_pe"), sem("misc_sb"), sem("mlp_pe"), sem("mlp_sb")
        mzt_pe, mzt_sb, gT_sb, sT_pe = sem("mzt_pe"), sem("mzt_sb"), sem("gT_sb"), sem("sT_pe")

        @block.sync
        def _(sp):
            for b in range(B):
                sp.dma_start(X[:, NT * b:NT * b + NT, :], x[:, NT * b:NT * b + NT, :]).then_inc(d_x[b], 16)
            wd = t_in["L0_attn_W_disp"]
            with nc.allow_non_contiguous_dma(reason="small weights"):
                sp.dma_start(wdisp[:], wd.rearrange("k (g n) -> k g n", g=G)).then_inc(d_attn_w, 16)
                for s, n in enumerate(("L0_attn_W_strain", "L0_attn_W_dmg")):
                    sp.dma_start(wrep[:, s, :], dram_rows(t_in[n], 0, [[0, HG], [BD, BD], [1, BD]])).then_inc(d_attn_w, 16)
                for s, n in enumerate(("L0_attn_W_bond", "L0_attn_W_dmg_out")):
                    sp.dma_start(wcol[:, s:s + 1], dram_rows(t_in[n], 0, [[0, HG], [1, BD], [1, 1]])).then_inc(d_attn_w, 16)
                sp.dma_start(bdmg[:], dram_rows(t_in["L0_attn_b_dmg"], 0, [[0, HG], [1, BD], [1, 1]])).then_inc(d_attn_w, 16)
                sp.dma_start(bdo[:], dram_rows(t_in["L0_attn_b_dmg_out"], 0, [[0, P], [1, 1]])).then_inc(d_attn_w, 16)
                sp.dma_start(rel[:], t_in["L0_attn_rel_pos_emb"]).then_inc(d_attn_w, 16)
                sp.dma_start(wpos[:], dram_rows(t_in["L0_attn_W_pos"], 0, [[BD, BD], [0, HG], [1, BD]])).then_inc(d_attn_w, 16)
                sp.dma_start(wval[:], t_in["L0_attn_W_val"]).then_inc(d_attn_w, 16)
                for half in range(2):
                    sp.dma_start(wcp[64 * half:64 * half + 64, :, :],
                                 t_in["L0_attn_W_cproj"].rearrange("(g r) n -> r g n", g=G)).then_inc(d_attn_w, 16)
                sp.dma_start(gw[:], t_in["L0_ffn_gate_w"]).then_inc(d_gate_w, 16)
                sp.dma_start(gb[:], dram_rows(t_in["L0_ffn_gate_b"], 0, [[0, P], [1, E0]])).then_inc(d_gate_w, 16)
                sp.dma_start(scl[:], dram_rows(t_in["L0_ffn_scale"], 0, [[1, P], [1, 1]])).then_inc(d_gate_w, 16)
                sp.dma_start(b1r[:], t_in["L0_ffn_mlp1_b"]).then_inc(d_gate_w, 16)
                sp.dma_start(w1r[:], dram_rows(t_in["L0_ffn_mlp1_w"], 0, [[2 * C, I0], [2 * I0 * C, E0], [1, C]])).then_inc(d_mlp_w, 16)
                sp.dma_start(w2r[:], t_in["L0_ffn_mlp2_w"].rearrange("e h i -> h e i")).then_inc(d_mlp_w, 16)
                sp.dma_start(b2r[:], t_in["L0_ffn_mlp2_b"]).then_inc(d_mlp_w, 16)
            sp.wait_ge(zero_ready, 1)
            flat = band.rearrange("a k n r s -> (a k n r s)").rearrange("(p f) -> p f", p=P)
            for i in range(4):
                sp.dma_start(flat[:, 2048 * i:2048 * i + 2048], Z[:, 0:4, :].rearrange("p q t -> p (q t)")).then_inc(d_band0, 16)
            sp.wait_ge(d_band0, 64)

        @block.gpsimd
        def _(pool):
            link = chain_of(pool, s_pool)
            link(pool.memset(ident[:], 0.0))
            pool.affine_select(out=ident[:], in_=ident[:], compare_op=ALU.not_equal, fill=1.0, base=0,
                               pattern=[[-1, P]], channel_multiplier=1).then_inc(const_ready, 1)
            pool.memset(nhalf[:], -0.5)
            link(pool.memset(ones8[:], 1.0))
            link(pool.affine_select(out=mask8[:], in_=ones8[:], compare_op=ALU.is_ge, fill=0.0, base=0,
                                    pattern=[[-BD, HG]], channel_multiplier=1))
            pool.affine_select(out=mask8[:], in_=mask8[:], compare_op=ALU.is_ge, fill=0.0, base=BD - 1,
                               pattern=[[BD, HG]], channel_multiplier=-1).then_inc(const_ready, 1)
            pool.wait_ge(mv_ready, 1)
            link(pool.tensor_scalar(rstd[:], mv[:, :, 1], EPS, 1.0, ALU.add, ALU.mult))
            pool.tensor_tensor(rstd[:], rstd[:], nhalf[:], ALU.pow).then_inc(rstd_ready, 1)
            link(pool.memset(Z[:, 0:4, :], 0.0))
            link(pool.affine_select(out=mt[:], in_=Z[0:WIN, 0, 0:WIN], compare_op=ALU.is_ge, fill=MASKED,
                                    base=-PAD, pattern=[[1, WIN]], channel_multiplier=1))
            pool.tensor_copy(mt2[:], mt[:].rearrange("t (q j) -> t q j", j=4).unsqueeze(2).to_broadcast([WIN, JQ, 32, 4])
                             ).then_inc(mt_ready, 1)
            pool.wait_ge(ss_ready, 1)
            link(pool.tensor_scalar(r2[:], ss[:], 1.0 / C, EPS, ALU.mult, ALU.add))
            pool.tensor_tensor(r2[:], r2[:], nhalf[:], ALU.pow).then_inc(r2_ready, 1)
            link(pool.memset(lones[:], 0.0))
            for hh in range(4):
                last = pool.memset(lones[:, hh, 8 * hh:8 * hh + 8], 1.0)
            link(last)
            pool.memset(AD[:, :, :, 0:PAD], 0.0)
            pool.memset(AD[:, :, :, PAD + T:TP], 0.0)
            pool.memset(xnT[:, :, 0:PAD], 0.0)
            pool.memset(xnT[:, :, PAD + T:TP], 0.0).then_inc(zero_ready, 1)

        @block.vector
        def _(v):
            link = chain_of(v, s_dve)
            for b in range(B):
                v.wait_ge(d_x[b], 16)
                for t in range(NT * b, NT * b + NT):
                    last = v.bn_stats(stats[:, t, :], X[:, t, :])
            link(last)
            for t in range(TT):
                last = v.bn_aggr(mv[:, t, :], stats[:, t, :])
            last.then_inc(mv_ready, 1)
            v.wait_ge(rstd_ready, 1)
            for t in range(TT):
                last = v.tensor_scalar(XN[:, t, :], X[:, t, :], mv[:, t, 0:1], rstd[:, t:t + 1], ALU.subtract, ALU.mult)
            last.then_inc(xn_ready, 1)
            v.wait_ge(xn_ready, 1)
            for t in range(TT):
                last = v.tensor_tensor_reduce(TF[:, t, :], XN[:, t, :], XN[:, t, :], 1.0, 0.0, ALU.mult, ALU.add,
                                              ss[:, t:t + 1])
            last.then_inc(ss_ready, 1)
            v.wait_ge(d_attn_w, 16 * 12)
            v.wait_ge(const_ready, 2)
            for s in range(2):
                v.tensor_tensor(wblk[:, s, :, :], wrep[:, s, :].unsqueeze(1).to_broadcast([P, HG, BD]),
                                mask8[:].unsqueeze(2).to_broadcast([P, HG, BD]), ALU.mult)
            link(v.memset(lred[:], 0.0))
            for s in range(2):
                for a in range(4):
                    last = v.tensor_scalar(lred[:, s, a, a:32:4], mask8[:], wcol[:, s:s + 1], None, ALU.mult)
            v.tensor_copy(eyes[:, 0, :], ident[:])
            v.tensor_scalar(eyes[:, 1, :], ident[:], -1.0, None, ALU.mult)
            v.tensor_scalar(bdo[:], bdo[:], 0.5, None, ALU.mult).then_inc(blk_ready, 1)
            v.wait_ge(r2_ready, 1)
            for t in range(TT):
                last = v.tensor_scalar(TF[:, t, :], XN[:, t, :], r2[:, t:t + 1], None, ALU.mult)
            last.then_inc(tf_ready, 1)
            v.wait_ge(misc_pe, 1)
            v.memset(gwT[:, E0:], 0.0)
            v.tensor_copy(gwT[:, 0:E0], S[0][:, 0:E0])
            v.tensor_copy(relT[:], S[0][0:BD, 64:64 + WIN])
            v.tensor_copy(b1T[:], S[0][:, 128:128 + E0]).then_inc(misc_sb, 1)
            v.wait_ge(misc_pe, 2)
            v.tensor_copy(PT[:], S[0][:, 256:256 + WIN]).then_inc(misc_sb, 1)
            v.tensor_tensor(ACC[:], X[:], XN[:], ALU.add)
            v.wait_ge(sT_pe, 1)
            link(v.tensor_tensor(gsc[:].rearrange("p (b i) e -> p b i e", b=B),
                                 S[0][:, :].rearrange("p (i b e) -> p b i e", i=NT, b=B)[:, :, :, 0:E0],
                                 gb[:].unsqueeze(1).unsqueeze(1).to_broadcast([P, B, NT, E0]), ALU.add))
            top_k_route(v, link, gsc, route, m8, gt, eq, c0, c1, small, E0, K0, exp_ready, exp_done)

        @block.scalar
        def _(act):
            act.wait_ge(wt_pe, 1)
            act.copy(wdispT[:], S[6][:, 0:G * P]).then_inc(wt_sb, 1)
            act.wait_ge(wad_pe, 1)
            act.copy(wad[:], S[7][:]).then_inc(wad_sb, 1)
            for b in range(B):
                act.wait_ge(xnT_pe, b + 1)
                act.copy(xnT[:, b, PAD:PAD + T], S[2 + b][:, :]).then_inc(xnT_sb, 1)
            act.wait_ge(d_gate_w, 64)
            for b in range(B):
                act.wait_ge(tT_pe, b + 1)
                act.activation(tT[:, b, :], S[2 + b][:, :], ACT.Copy, scale=scl[:, 0:1]).then_inc(tT_sb, 1)
            act.wait_ge(gate_pe, 1)
            act.copy(gscT[:], S[1][:, :]).then_inc(gT_sb, 1)
            for i in range(8):
                act.wait_ge(ad_pe, i + 1)
                act.copy(AD[:, i // 4, i % 4, PAD:PAD + T], S[2 + i % 4][:, :]).then_inc(ad_sb, 1)
            for i in range(0, 4):
                act.wait_ge(mlp_pe, i + 1)
                dst, e = (w1T, 4 * i) if i < 4 else (w2T, 4 * i - 16)
                act.activation(dst[:, e:e + 4, :].rearrange("p e c -> p (e c)"), S[6 + i % 2][:, :], ACT.Copy,
                               scale=1.0 if i < 4 else (LIMIT + 1.0) / 2).then_inc(mlp_sb, 1)
            act.wait_ge(exp_ready, 1)
            act.activation(route[:], route[:], ACT.Exp).then_inc(exp_done, 1)
            for i in range(4, 8):
                act.wait_ge(mlp_pe, i + 1)
                dst, e = (w1T, 4 * i) if i < 4 else (w2T, 4 * i - 16)
                act.activation(dst[:, e:e + 4, :].rearrange("p e c -> p (e c)"), S[6 + i % 2][:, :], ACT.Copy,
                               scale=1.0 if i < 4 else (LIMIT + 1.0) / 2).then_inc(mlp_sb, 1)
            for i in range(4):
                act.wait_ge(mzt_pe, i + 1)
                act.copy(mz[:, 4 * i:4 * i + 4, :].rearrange("p q t -> p (q t)"), S[6 + i % 2][:, 0:256]).then_inc(mzt_sb, 1)

        @block.tensor
        def _(pe):
            pe.wait_ge(const_ready, 1)
            pe.wait_ge(d_attn_w, 16 * 12)
            for g in range(G):
                last = pe.transpose(S[6][:, P * g:P * g + P], wdisp[:, g, :], ident[:])
            last.then_inc(wt_pe, 1)
            pe.wait_ge(wt_sb, 1)
            pe.wait_ge(blk_ready, 1)
            for g in range(G):
                for s in range(2):
                    at = P * (2 * g + s)
                    last = pe.matmul(S[7][:, at:at + P], wdispT[:, g, :], wblk[:, s, :, :].rearrange("p h c -> p (h c)"),
                                     start=True, stop=True)
            last.then_inc(wad_pe, 1)
            pe.wait_ge(d_gate_w, 64)
            pe.transpose(S[0][:, 0:E0], gw[:], ident[0:E0, 0:E0])
            pe.transpose(S[0][0:BD, 64:64 + WIN], rel[:], ident[0:WIN, 0:WIN])
            pe.transpose(S[0][:, 128:128 + E0], b1r[:, 0:2 * I0:2], ident[0:E0, 0:E0]).then_inc(misc_pe, 1)
            pe.wait_ge(xn_ready, 1)
            for b in range(B):
                for i in range(NT):
                    last = pe.transpose(S[2 + b][:, P * i:P * i + P], XN[:, NT * b + i, :], ident[:])
                last.then_inc(xnT_pe, 1)
            pe.wait_ge(misc_sb, 1)
            pe.matmul(S[0][:, 256:256 + WIN], wpos[:].rearrange("k h c -> k (h c)"), relT[:], start=True, stop=True).then_inc(misc_pe, 1)
            pe.wait_ge(tf_ready, 1)
            for b in range(B):
                pe.wait_ge(xnT_sb, b + 1)
                for i in range(NT):
                    last = pe.transpose(S[2 + b][:, P * i:P * i + P], TF[:, NT * b + i, :], ident[:])
                last.then_inc(tT_pe, 1)
            pe.wait_ge(misc_sb, 1)
            pe.wait_ge(tT_sb, B)
            for b in range(B):
                last = pe.matmul(S[1][32 * b:32 * b + 32, :], gwT[:], tT[:, b, :], start=True, stop=True)
            last.then_inc(gate_pe, 1)
            pe.wait_ge(wad_sb, 1)
            for i in range(8):
                if i == 2:
                    pe.wait_ge(gT_sb, 1)
                    pe.wait_ge(misc_sb, 2)
                    for n in range(NT):
                        last = pe.transpose(S[0][:, P * n:P * n + P], gscT[:, P * n:P * n + P], ident[:])
                    last.then_inc(sT_pe, 1)
                if i >= 4:
                    pe.wait_ge(ad_sb, i - 3)
                pe.matmul(S[2 + i % 4][:, :], wad[:, 0, i // 4, :], xnT[:, i % 4, PAD:PAD + T], start=True, stop=True).then_inc(ad_pe, 1)
            pe.wait_ge(d_mlp_w, 48)
            for i in range(8):
                if i >= 2:
                    pe.wait_ge(mlp_sb, i - 1)
                src, e = (w1r, 4 * i) if i < 4 else (w2r, 4 * i - 16)
                for n in range(4):
                    last = pe.transpose(S[6 + i % 2][:, P * n:P * n + P], src[:, e + n, :], ident[:])
                last.then_inc(mlp_pe, 1)
            pe.wait_ge(mt_ready, 1)
            pe.wait_ge(mlp_sb, 8)
            for i in range(4):
                if i >= 2:
                    pe.wait_ge(mzt_sb, i - 1)
                for n in range(4):
                    last = pe.transpose(S[6 + i % 2][:, WIN * n:WIN * n + WIN],
                                        mt2[:, 4 * i + n, :, :].rearrange("t n j -> t (n j)"), ident[0:WIN, 0:WIN])
                last.then_inc(mzt_pe, 1)

    items_reduced, banks_free = sem("items_reduced"), sem("banks_free")
    strain_ready, gelu_done, th_ready = sem("strain_ready"), sem("gelu_done"), sem("th_ready")
    w1_staged, h_ready, xg_ready, sig_ready, s_ready, y_ready, y_used = (
        sem(n) for n in ("w1_staged", "h_ready", "xg_ready", "sig_ready", "s_ready", "y_ready", "y_used"))
    sd_ready, sd_taken = sem("sd_ready"), sem("sd_taken")
    zm_ready, zt_ready, mx_ready, zs_ready, ex_ready = (sem(n) for n in ("zm_ready", "zt_ready", "mx_ready", "zs_ready", "ex_ready"))
    d_out = [sem("d_skew0"), sem("d_skew1")]
    d_in = [sem("d_band_in0"), sem("d_band_in1")]
    band_pe, band_act, band_dve, vw_pe, vw_sb, nd_pe, rc_ready, att_ready = (
        sem(n) for n in ("band_pe", "band_act", "band_dve", "vw_pe", "vw_sb", "nd_pe", "rc_ready", "att_ready"))
    vp_zero = sem("vp_zero")

    for g in range(G):
        with ExitStack() as lp:
            ring = sb(f"ring{g}", [P, RING, 2, B, T], F32, lp)
            xg = sb(f"xg{g}", [P, 2, T], F32, lp)
            t2 = sb(f"t2{g}", [P, 2, T], F32, lp)
            w1s = sb(f"w1s{g}", [P, I0], F32, lp)
            LG = psum(f"LG{g}", [P, 2, 2, T], lp)
            SD = psum(f"SD{g}", [P, 2, T], lp)
            PH = psum(f"PH{g}", [P, T], lp)
            PY = psum(f"PY{g}", [P, 4, C], lp)
            block = lp.enter_context(nc.Block())
            N0 = g * WIN
            Q0 = g * JQ
            U0 = g * 32
            D0 = g * 8

            def runs(engine, body):
                with engine.Fori(0, 3) as it:
                    body(it, 32, 32)
                body(3, 32, 0)
                with engine.Fori(4, 7) as it:
                    body(it, 0, 0)
                body(7, 0, None)

            @block.gpsimd
            def _(pool):
                if g == 0:
                    pool.sem_inc(items_reduced, RING)
                    pool.sem_inc(banks_free, 2)
                    pool.sem_inc(y_used, 1)
                    pool.sem_inc(xg_ready, 1)
                def stage(it):
                    pool.tensor_copy(w1s[:], w1T[:, bass.ds(HG * g + it, 1), :]).then_inc(w1_staged, 1)
                stage(0)
                pool.memset(Z[:, 0:8, 0:32], 0.0)
                with pool.Fori(0, 7) as it:
                    pool.wait_ge(h_ready, U0 + 4 * it + 4)
                    stage(it + 1)

            @block.vector
            def _(v):
                def item(n, j, t0):
                    slot = n % RING
                    v.wait_ge(items_reduced, N0 + j + 1)
                    for s, extra in ((0, PT[:, bass.ds(j, 1)]), (1, bdmg[:, 0:1])):
                        if s == 0 or n not in PE_ITEMS:
                            ins = v.scalar_tensor_tensor(out=ring[:, slot, s, :, t0:T], in0=AD[:, s, :, bass.ds(j + t0, T - t0)],
                                                         scalar=extra, in1=AD[:, s, :, PAD + t0:PAD + T],
                                                         op0=ALU.add, op1=ALU.subtract)
                    ins.then_inc(strain_ready, 1)

                def logits(par, q, t0):
                    v.wait_ge(th_ready, Q0 + q + 1)
                    zq = Z[:, bass.ds(q, 1), t0:T].rearrange("p o t -> p (o t)")
                    v.scalar_tensor_tensor(out=zq, in0=zq, scalar=-5.0, in1=LG[:, par, 0, t0:T], op0=ALU.mult, op1=ALU.add
                                           ).then_inc(banks_free, 1)

                def glu_in(c, it, u):
                    v.wait_ge(h_ready, u + 1)
                    v.tensor_scalar(xg[:, c % 2, :], PH[:], b1T[:, bass.ds(HG * g + it, 1)], LIMIT,
                                    ALU.add, ALU.min).then_inc(xg_ready, 1)

                def glu_out(c, u):
                    v.wait_ge(sig_ready, u + 1)
                    v.scalar_tensor_tensor(out=xg[:, c % 2, :], in0=t2[:, c % 2, :], scalar=1.0, in1=xg[:, c % 2, :],
                                           op0=ALU.add, op1=ALU.mult).then_inc(s_ready, 1)

                def combine(c, it, u):
                    v.wait_ge(y_ready, u + 1)
                    for i in range(4):
                        a = ACC[:, 4 * c + i, :]
                        ins = v.scalar_tensor_tensor(out=a, in0=PY[:, i, :], scalar=route[:, 4 * c + i, bass.ds(HG * g + it, 1)],
                                                     in1=a, op0=ALU.mult, op1=ALU.add)
                    ins.then_inc(y_used, 1)

                def body(it, t0, t0_next):
                    j, u = 8 * it, U0 + 4 * it
                    glu_in(0, it, u)
                    item(3, j + 3, t0)
                    item(4, j + 4, t0)
                    glu_out(0, u)
                    glu_in(1, it, u + 1)
                    item(5, j + 5, t0)
                    combine(0, it, u)
                    glu_out(1, u + 1)
                    glu_in(2, it, u + 2)
                    item(6, j + 6, t0)
                    item(7, j + 7, t0)
                    combine(1, it, u + 1)
                    glu_out(2, u + 2)
                    glu_in(3, it, u + 3)
                    logits(0, 2 * it, t0)
                    if t0_next is not None:
                        item(0, j + 8, t0_next)
                    combine(2, it, u + 2)
                    glu_out(3, u + 3)
                    if t0_next is not None:
                        item(1, j + 9, t0_next)
                    combine(3, it, u + 3)
                    if t0_next is not None:
                        item(2, j + 10, t0_next)
                    logits(1, 2 * it + 1, t0)

                item(0, 0, 32)
                v.wait_ge(dh_ready, g + 1)
                v.tensor_tensor(DHL[:, 1], AD[:, 1], DHL[:, 0].bitcast(F32), ALU.subtract).then_inc(dl_ready, 1)
                item(1, 1, 32)
                item(2, 2, 32)
                runs(v, body)

            @block.scalar
            def _(act):
                def gelu(n, it, t0):
                    j, slot = 8 * it + n, n % RING
                    act.wait_ge(strain_ready, N0 + j + 1)
                    if n not in PE_ITEMS:
                        tiles = ring[:, slot, :, :, t0:T]
                        act.activation(tiles, tiles, ACT.Gelu).then_inc(gelu_done, 1)
                        return
                    f = 2 * (NPE * (D0 + it) + PE_ITEMS.index(n))
                    act.wait_ge(sd_ready, f + 1)
                    act.activation(ring[:, slot, 1, 0:2, t0:T], SD[:, :, t0:T], ACT.Gelu, bias=bdmg[:, 0:1]).then_inc(sd_taken, 1)
                    tiles = ring[:, slot, 0, :, t0:T]
                    act.activation(tiles, tiles, ACT.Gelu)
                    act.wait_ge(sd_ready, f + 2)
                    act.activation(ring[:, slot, 1, 2:4, t0:T], SD[:, :, t0:T], ACT.Gelu, bias=bdmg[:, 0:1]).then_inc(gelu_done, 1)

                def tanh(par, q, t0):
                    act.wait_ge(items_reduced, RING + N0 + 4 * q + 4)
                    act.activation(Z[:, bass.ds(q, 1), t0:T].rearrange("p o t -> p (o t)"), LG[:, par, 1, t0:T], ACT.Tanh,
                                   bias=bdo[:, 0:1], scale=0.5).then_inc(th_ready, 1)

                def sig(c, u):
                    act.wait_ge(xg_ready, u + 2)
                    act.activation(t2[:, c % 2, :], xg[:, c % 2, :], ACT.Tanh, scale=ALPHA / 2).then_inc(sig_ready, 1)

                def body(it, t0, t0_next):
                    u = U0 + 4 * it
                    gelu(1, it, t0)
                    sig(0, u)
                    gelu(2, it, t0)
                    gelu(3, it, t0)
                    sig(1, u + 1)
                    gelu(4, it, t0)
                    tanh(0, 2 * it, t0)
                    gelu(5, it, t0)
                    sig(2, u + 2)
                    gelu(6, it, t0)
                    gelu(7, it, t0)
                    sig(3, u + 3)
                    if t0_next is not None:
                        gelu(0, it + 1, t0_next)
                    tanh(1, 2 * it + 1, t0)

                act.copy(DHL[:, 0], AD[:, 1]).then_inc(dh_ready, 1)
                gelu(0, 0, 32)
                runs(act, body)

            @block.tensor
            def _(pe):
                def reduce(n, j, q, t0):
                    slot, par = n % RING, (n // 4) % 2
                    if n % 4 == 0:
                        pe.wait_ge(banks_free, Q0 + q + 1)
                    pe.wait_ge(gelu_done, N0 + j + 1)
                    for s in range(2):
                        for b in range(B):
                            mm = pe.matmul(LG[32 * b:32 * b + 32, par, s, t0:T], lred[:, s, n % 4, :], ring[:, slot, s, b, t0:T],
                                           start=(n % 4 == 0), stop=(n % 4 == 3))
                    mm.then_inc(items_reduced, 1)

                def strain(n, it, half, t0):
                    if half:
                        pe.wait_ge(sd_taken, NPE * (D0 + it) + PE_ITEMS.index(n) + 1)
                    for part in range(2):
                        for i in range(2):
                            pe.matmul(SD[:, i, t0:T], eyes[:, 0, :], DHL[:, part, 2 * half + i, bass.ds(8 * it + n + t0, T - t0)],
                                      start=(part == 0), stop=False)
                    for part in range(2):
                        for i in range(2):
                            mm = pe.matmul(SD[:, i, t0:T], eyes[:, 1, :], DHL[:, part, 2 * half + i, PAD + t0:PAD + T],
                                           start=False, stop=(part == 1))
                    mm.then_inc(sd_ready, 1)

                def hidden(c, u, staged):
                    pe.wait_ge(w1_staged, staged)
                    pe.wait_ge(xg_ready, u + 1)
                    pe.matmul(PH[:], w1s[:], tT[:, c, :], start=True, stop=True).then_inc(h_ready, 1)

                def expert_out(c, it, u):
                    pe.wait_ge(s_ready, u + 1)
                    pe.wait_ge(y_used, u + 1)
                    for i in range(4):
                        mm = pe.matmul(PY[:, i, :], xg[:, c % 2, P * i:P * i + P], w2T[:, bass.ds(HG * g + it, 1), :].rearrange("p o c -> p (o c)"),
                                       start=True, stop=True)
                    mm.then_inc(y_ready, 1)

                def body(it, t0, t0_next):
                    j, u, w = 8 * it, U0 + 4 * it, HG * g + it + 1
                    strain(1, it, 1, t0)
                    reduce(0, j, 2 * it, t0)
                    hidden(1, u + 1, w)
                    reduce(1, j + 1, 2 * it, t0)
                    strain(4, it, 0, t0)
                    expert_out(0, it, u)
                    reduce(2, j + 2, 2 * it, t0)
                    hidden(2, u + 2, w)
                    strain(4, it, 1, t0)
                    reduce(3, j + 3, 2 * it, t0)
                    expert_out(1, it, u + 1)
                    reduce(4, j + 4, 2 * it + 1, t0)
                    strain(6, it, 0, t0)
                    hidden(3, u + 3, w)
                    strain(6, it, 1, t0)
                    reduce(5, j + 5, 2 * it + 1, t0)
                    reduce(6, j + 6, 2 * it + 1, t0)
                    if t0_next is not None:
                        strain(1, it + 1, 0, t0_next)
                    expert_out(2, it, u + 2)
                    if t0_next is not None:
                        hidden(0, u + 4, w + 1)
                    reduce(7, j + 7, 2 * it + 1, t0)
                    expert_out(3, it, u + 3)

                hidden(0, U0, HG * g + 1)
                pe.wait_ge(dl_ready, g + 1)
                strain(1, 0, 0, 32)
                runs(pe, body)

        with ExitStack() as sm:
            vp = sb(f"vp{g}", [P, 8, HG, 32], F32, sm)
            zs = sb(f"zs{g}", [P, 2, 32, JQ, 4], F32, sm)
            wide = sb(f"wide{g}", [P, 2, 32, P], F32, sm)
            wtT = sb(f"wtT{g}", [P, 32, P], F32, sm)
            mx = sb(f"mx{g}", [P, 2, 32], F32, sm)
            rc = sb(f"rc{g}", [P, 2, P], F32, sm)
            ZT = psum(f"ZT{g}", [P, JQ, P], sm)
            W = [psum(f"W{g}{i}", [P, 4, P], sm) for i in range(4)]
            block = sm.enter_context(nc.Block())
            M0 = NT * g

            @block.gpsimd
            def _(pool):
                pool.memset(vp[:], 0.0).then_inc(vp_zero, 1)

            @block.sync
            def _(sp):
                for ti in range(NT):
                    m, par = M0 + ti, ti % 2
                    sp.wait_ge(ex_ready, m + 1)
                    if ti >= 2:
                        sp.wait_ge(d_in[par], 32 * (m // 2))
                    for k in range(2):
                        dst = dram_rows(band, (par * 2 + k) * 32 * 64 * P, [[P + 1, 64], [64 * P, 32], [1, WIN]])
                        sp.dma_start(dst, zs[64 * k:64 * k + 64, par].rearrange("r n q j -> r n (q j)")).then_inc(d_out[par], 16)
                    sp.wait_ge(d_out[par], 32 * (m // 2 + 1))
                    if ti >= 2:
                        sp.wait_ge(band_pe, 8 * (m - 1))
                    for k in range(2):
                        sp.dma_start(wide[64 * k:64 * k + 64, par], band[par, k].rearrange("n r s -> r n s")).then_inc(d_in[par], 16)

            @block.vector
            def _(v):
                zh = Z[:, :, 0:WIN]
                v.tensor_tensor(zh, zh, mz[:], ALU.add).then_inc(zm_ready, 1)

                def weigh(ti):
                    m, par = M0 + ti, ti % 2
                    v.wait_ge(zt_ready, m + 1)
                    zt = ZT[:].rearrange("p q (n j) -> p n q j", j=4)
                    v.tensor_reduce(mx[:, par], zt, AX.XY, ALU.max).then_inc(mx_ready, 1)
                    v.wait_ge(mx_ready, m + 1)
                    if ti >= 2:
                        v.wait_ge(d_out[par], 32 * (m // 2))
                    v.tensor_tensor(zs[:, par], zt, mx[:, par].unsqueeze(2).unsqueeze(3).to_broadcast([P, 32, JQ, 4]),
                                    ALU.subtract).then_inc(zs_ready, 1)

                def turn(ti):
                    for i in range(1, 8, 2):
                        v.wait_ge(band_pe, 8 * (M0 + ti) + i + 1)
                        v.tensor_copy(wtT[:, 4 * i:4 * i + 4, :], W[i % 2][:]).then_inc(band_dve, 1)

                def divide(ti):
                    m = M0 + ti
                    v.wait_ge(nd_pe, m + 1)
                    v.reciprocal(rc[:], W[3][:, 0:2, :]).then_inc(rc_ready, 1)
                    v.wait_ge(rc_ready, m + 1)
                    v.tensor_tensor(attT[:, g, :, P * ti:P * ti + P], W[3][:, 2:4, :], rc[:], ALU.mult).then_inc(att_ready, 1)

                weigh(0)
                weigh(1)
                weigh(2)
                turn(0)
                divide(0)
                turn(1)
                weigh(3)
                divide(1)
                for ti in range(2, NT):
                    turn(ti)
                    divide(ti)

            @block.scalar
            def _(act):
                def weigh(ti):
                    m, par = M0 + ti, ti % 2
                    act.wait_ge(zs_ready, m + 1)
                    act.activation(zs[:, par], zs[:, par], ACT.Exp).then_inc(ex_ready, 1)

                def next_ad():
                    for i in range(8):
                        act.wait_ge(ad_pe, 8 + i + 1)
                        act.copy(AD[:, i // 4, i % 4, PAD:PAD + T], W[i % 2][:].rearrange("p n t -> p (n t)")).then_inc(ad_sb, 1)

                def gather(ti):
                    m = M0 + ti
                    act.wait_ge(vw_pe, m + 1)
                    act.wait_ge(vp_zero, g + 1)
                    act.wait_ge(nd_pe, m)
                    for hh in range(4):
                        ins = act.copy(vp[:, :, hh:HG:4, 8 * hh:8 * hh + 8],
                                       W[2][:].rearrange("p a c -> p (a c)").rearrange("p (n h e) -> p n h e", n=8, e=HS)[:, :, hh:HG:4, :])
                    ins.then_inc(vw_sb, 1)
                    for i in range(0, 8, 2):
                        act.wait_ge(band_pe, 8 * m + i + 1)
                        act.copy(wtT[:, 4 * i:4 * i + 4, :], W[i % 2][:]).then_inc(band_act, 1)

                weigh(0)
                weigh(1)
                if g < G - 1:
                    next_ad()
                weigh(2)
                gather(0)
                gather(1)
                weigh(3)
                gather(2)
                gather(3)

            @block.tensor
            def _(pe):
                def weigh(ti):
                    m = M0 + ti
                    pe.wait_ge(zs_ready, m)
                    for q in range(JQ):
                        mm = pe.transpose(ZT[:, q, :], Z[:, q, P * ti:P * ti + P], ident[:])
                    mm.then_inc(zt_ready, 1)

                def next_ad():
                    for i in range(8):
                        if i >= 2:
                            pe.wait_ge(ad_sb, 8 + i - 1)
                        pe.matmul(W[i % 2][:].rearrange("p n t -> p (n t)"), wad[:, 1, i // 4, :], xnT[:, i % 4, PAD:PAD + T],
                                  start=True, stop=True).then_inc(ad_pe, 1)
                    pe.wait_ge(ad_sb, 16)

                def gather(ti):
                    m, par = M0 + ti, ti % 2
                    pe.wait_ge(vw_sb, m)
                    for n in range(8):
                        b, k = n // 2, 2 * ti + n % 2
                        mm = pe.matmul(W[2][:].rearrange("p a c -> p (a c)")[:, 64 * n:64 * n + 64], xnT[:, b, 64 * k:64 * k + P],
                                       wval[:, 64 * g:64 * g + 64], start=True, stop=True)
                    mm.then_inc(vw_pe, 1)
                    pe.wait_ge(d_in[par], 32 * (m // 2 + 1))
                    for i in range(8):
                        pe.wait_ge(band_dve if i % 2 else band_act, 4 * m + i // 2)
                        for n in range(4):
                            mm = pe.transpose(W[i % 2][:, n, :], wide[:, par, 4 * i + n, :], ident[:])
                        mm.then_inc(band_pe, 1)
                    pe.wait_ge(band_act, 4 * m + 4)
                    pe.wait_ge(band_dve, 4 * m + 4)
                    pe.wait_ge(vw_sb, m + 1)
                    pe.wait_ge(att_ready, m)
                    for bb in range(2):
                        for hh in range(4):
                            for t4 in range(4):
                                b, qd = 2 * bb + t4 // 2, t4 % 2
                                n = HG * b + 4 * qd + hh
                                pe.matmul(W[3][32 * t4:32 * t4 + 32, bb, :], lones[:, hh, :], wtT[:, n, :],
                                          start=(hh == 0), stop=(hh == 3))
                    for bb in range(2):
                        for k in range(2):
                            for hh in range(4):
                                for t4 in range(4):
                                    b, qd = 2 * bb + t4 // 2, t4 % 2
                                    n = HG * b + 4 * qd + hh
                                    mm = pe.matmul(W[3][32 * t4:32 * t4 + 32, 2 + bb, 64 * k:64 * k + 64],
                                                   vp[:, 2 * b + k, 4 * qd + hh, :], wtT[:, n, 64 * k:64 * k + 64],
                                                   start=(hh == 0), stop=(hh == 3))
                    mm.then_inc(nd_pe, 1)

                pe.wait_ge(zm_ready, g + 1)
                weigh(0)
                weigh(1)
                if g < G - 1:
                    next_ad()
                weigh(2)
                gather(0)
                weigh(3)
                for ti in range(1, NT):
                    gather(ti)


def second_layer(nc, t_in, out, l1, sb, psum, sem, ident, ACC, nhalf, stats, mv, rstd, carried):
    attT, wcp, route, b2r = carried
    xT = sb("xT", [P, B, T], F32, l1)
    W1 = sb("W1", [P, 2, E1, FF], F32R, l1)
    W2 = sb("W2", [P, E1, FQ, C], F32, l1)
    b1c = sb("b1c", [P, E1, FQ], F32, l1)
    rb1c = sb("rb1c", [P, FQ], F32, l1)
    rw2 = sb("rw2", [P, FQ, 32], F32, l1)
    VA = sb("VA", [P, NT, H1, 32], F32, l1)
    NX = sb("NX", [P, NT, HQ, 4, 32], F32, l1)
    wq = sb("wq", [P, HQ, 4, 4, 8], F32, l1)
    wk = sb("wk", [P, HQ, 4, 4, 8], F32, l1)
    wv = sb("wv", [P, C], F32, l1)
    wo = sb("wo", [P, HQ, C], F32, l1)
    gate = sb("gate", [P, TT, E1], F32, l1)
    b2r1 = sb("b2r1", [E1, C], F32, l1)
    neglo = sb("neglo", [P, 2], F32, l1)
    onesrow = sb("onesrow", [P, 1], F32, l1)
    zcol = sb("zcol", [P, 1], F32, l1)
    sel = sb("sel", [P, P], F32, l1)
    outd = out.rearrange("b t c -> (b t) c").rearrange("(n p) c -> p n c", p=P)

    d_w = [sem(f"l1_w{i}") for i in range(3)]
    ms_ready = sem("ms_ready")
    with ExitStack() as su:
        rw1 = sb("rw1", [P, FF], F32, su)
        W1f = sb("W1f", [P, E1, FF], F32, su)
        wqkv = sb("wqkv", [P, 3, C], F32, su)
        XN = sb("XN2", [P, TT, C], F32, su)
        b1r = sb("b1r1", [E1 * FQ, P], F32, su)
        rb1r = sb("rb1r", [FQ, P], F32, su)
        rb2 = sb("rb2", [P, E1], F32, su)
        HR = sb("HR", [P, FQ, B, T], F32, su)
        sc = sb("sc", [P, TT, E1], F32, su)
        m8 = sb("m81", [P, TT, 8], F32, su)
        gt = sb("gt1", [P, TT, E1], F32, su)
        eq = sb("eq1", [P, TT, E1], F32, su)
        c0 = sb("c01", [P, TT, E1], F32, su)
        c1 = sb("c11", [P, TT, E1], F32, su)
        small = sb("small1", [P, 2, TT], F32, su)
        gateT = sb("gateT", [E1, TT, P], F32, su)
        picked = sb("picked", [P, 2, 4], F32, su)
        routeT = sb("routeT", [E0, TT, P], F32, su)
        scT = sb("scT", [P, T], F32, su)
        ones = sb("ones1", [P, P], F32, su)
        S = [psum(f"sv{i}", [P, 512], su) for i in range(8)]
        block = su.enter_context(nc.Block())
        s_pool, s_dve = Count(sem("sv_pool")), Count(sem("sv_dve"))
        mv_ready, rstd_ready, xn_ready = sem("mv_ready1"), sem("rstd_ready1"), sem("xn_ready1")
        w_zero, w_ready, xT_pe, xT_sb = sem("w_zero"), sem("w_ready"), sem("xT_pe"), sem("xT_sb")
        w1_high = sem("w1_high")
        b_pe, b_sb, hr_pe, hr_sb, sc_pe = sem("b_pe"), sem("b_sb"), sem("hr_pe"), sem("hr_sb"), sem("sc_pe")
        exp_ready, exp_done, gate_ready = sem("exp_ready1"), sem("exp_done1"), sem("gate_ready")
        rt_pe, rt_sb, cp_pe, sT_sb, sT_pe = (sem(n) for n in ("rt_pe", "rt_sb", "cp_pe", "sT_sb1", "sT_pe1"))
        gt_pe, gt_sb, b2_pe, b2_sb = sem("gt_pe"), sem("gt_sb"), sem("b2_pe1"), sem("b2_sb1")

        @block.sync
        def _(sp):
            with nc.allow_non_contiguous_dma(reason="small weights"):
                sp.dma_start(wqkv[:], t_in["L1_attn_w_qkv"].rearrange("k (s n) -> k s n", s=3)).then_inc(d_w[0], 16)
                sp.dma_start(wv[:], t_in["L1_attn_w_qkv"][:, 2 * C:3 * C]).then_inc(d_w[0], 16)
                sp.dma_start(rw1[:], t_in["L1_ffn_rw1"]).then_inc(d_w[0], 16)
                sp.dma_start(rb1r[:], t_in["L1_ffn_rb1"].rearrange("(a p) -> a p", p=P)).then_inc(d_w[0], 16)
                sp.dma_start(rb2[:], dram_rows(t_in["L1_ffn_rb2"], 0, [[0, P], [1, E1]])).then_inc(d_w[0], 16)
                sp.dma_start(b1r[:], t_in["L1_ffn_b1"].rearrange("e (a p) -> (e a) p", p=P)).then_inc(d_w[0], 16)
                sp.dma_start(b2r1[:], t_in["L1_ffn_b2"]).then_inc(d_w[0], 16)
                sp.dma_start(W1f[:], t_in["L1_ffn_W1"].rearrange("e k f -> k e f")).then_inc(d_w[1], 16)
                sp.dma_start(W2[:], t_in["L1_ffn_W2"].rearrange("e (a p) c -> p e a c", p=P)).then_inc(d_w[1], 16)
                sp.wait_ge(w_zero, 1)
                sp.dma_start(rw2[:, :, 0:E1], t_in["L1_ffn_rw2"].rearrange("(a p) e -> p a e", p=P)).then_inc(d_w[2], 16)
                wout = t_in["L1_attn_w_out"].rearrange("(q h e) n -> h e q n", q=HQ, e=HD)
                for hh in range(4):
                    sp.dma_start(wo[32 * hh:32 * hh + HD, :, :], wout[hh]).then_inc(d_w[2], 16)
            sp.wait_ge(d_w[1], 32)
            sp.wait_ge(d_w[2], 80)

        @block.gpsimd
        def _(pool):
            link = chain_of(pool, s_pool)
            pool.memset(wo[:], 0.0)
            pool.memset(rw2[:], 0.0).then_inc(w_zero, 1)
            pool.memset(wq[:], 0.0)
            pool.memset(wk[:], 0.0)
            link(pool.memset(ones[:], 1.0))
            for b in range(B):
                r = slice(NT * b, NT * b + NT)
                pool.wait_ge(mv_ready, b + 1)
                link(pool.tensor_scalar(rstd[:, r], mv[:, r, 1], EPS, 1.0, ALU.add, ALU.mult))
                pool.tensor_tensor(rstd[:, r], rstd[:, r], nhalf[:, r], ALU.pow).then_inc(rstd_ready, 1)
            pool.memset(NX[:], 0.0)
            pool.memset(VA[:], 0.0).then_inc(ms_ready, 1)
            pool.wait_ge(ms_ready, 1)
            pool.memset(VA[:, :, :, HD:HD + 1], 1.0).then_inc(ms_ready, 1)
            def pick(out_ap, in_ap, op, base, pattern, mult, fill):
                return pool.affine_select(out=out_ap, in_=in_ap, compare_op=op, fill=fill, base=base, pattern=pattern,
                                          channel_multiplier=mult)
            link(pool.memset(sel[:], 0.0))
            link(pick(sel[:].rearrange("p (a c) -> p a c", a=4), sel[:].rearrange("p (a c) -> p a c", a=4), ALU.not_equal,
                      -HD, [[-32, 4], [0, 32]], 1, 1.0))
            def rows(lo, hi, dst):
                pool_tmp = picked[:, 0, 0:4]
                link(pick(pool_tmp, ones[:, 0:4], ALU.is_ge, -lo, [[-32, 4]], 1, 0.0))
                link(pick(pool_tmp, pool_tmp, ALU.is_ge, hi, [[32, 4]], -1, 0.0))
                link(pool.tensor_tensor(picked[:, 1, 0:2], picked[:, 0, 0:2], picked[:, 0, 2:4], ALU.add))
                link(pool.tensor_tensor(dst, picked[:, 1, 0:1], picked[:, 1, 1:2], ALU.add))
            rows(16, 23, neglo[:, 0:1])
            rows(8, 15, neglo[:, 1:2])
            link(pool.tensor_scalar(neglo[:], neglo[:], -1.0, 1.0, ALU.mult, ALU.mult))
            rows(24, 25, onesrow[:, 0:1])
            link(pool.tensor_tensor(neglo[:, 1:2], neglo[:, 1:2], onesrow[:], ALU.add))
            pool.memset(zcol[:], 0.0)
            pool.wait_ge(d_w[0], 16 * 7)
            for q in range(HQ):
                for dst, n in ((wq, 0), (wk, 1)):
                    for s in range(3):
                        last = pool.tensor_copy(dst[:, q, :, s, :], wqkv[:, n, 32 * q:32 * q + 32].rearrange("p (h d) -> p h d", d=HD))
            last.then_inc(w_ready, 1)

        @block.vector
        def _(v):
            link = chain_of(v, s_dve)
            def normalised(b):
                v.wait_ge(rstd_ready, b + 1)
                for t in range(NT * b, NT * b + NT):
                    last = v.tensor_scalar(XN[:, t, :], ACC[:, t, :], mv[:, t, 0:1], rstd[:, t:t + 1], ALU.subtract, ALU.mult)
                last.then_inc(xn_ready, 1)

            for b in range(B):
                v.wait_ge(cp_pe, b + 1)
                a = ACC[:, NT * b:NT * b + NT, :]
                link(v.tensor_tensor(a, a, S[4 + b][:, :].rearrange("p (i c) -> p i c", i=NT), ALU.add))
                for t in range(NT * b, NT * b + NT):
                    last = v.bn_stats(stats[:, t, :], ACC[:, t, :])
                link(last)
                for t in range(NT * b, NT * b + NT):
                    last = v.bn_aggr(mv[:, t, :], stats[:, t, :])
                last.then_inc(mv_ready, 1)
                if b:
                    normalised(b - 1)
            normalised(B - 1)
            v.wait_ge(b_pe, 1)
            v.tensor_copy(b1c[:].rearrange("p e a -> p (e a)"), S[1][:, 0:E1 * FQ])
            v.tensor_copy(rb1c[:], S[1][:, 64:64 + FQ]).then_inc(b_sb, 1)
            v.wait_ge(d_w[1], 32)
            v.tensor_copy(W1[:, 0], W1f[:]).then_inc(w1_high, 1)
            v.wait_ge(w1_high, 1)
            v.tensor_tensor(W1[:, 1], W1f[:], W1[:, 0].bitcast(F32), ALU.subtract)
            v.wait_ge(sT_pe, 1)
            link(v.tensor_tensor(sc[:].rearrange("p (b i) e -> p b i e", b=B),
                                 S[0][:, :].rearrange("p (i b e) -> p b i e", i=NT, b=B)[:, :, :, 0:E1],
                                 rb2[:].unsqueeze(1).unsqueeze(1).to_broadcast([P, B, NT, E1]), ALU.add))
            top_k_route(v, link, sc, gate, m8, gt, eq, c0, c1, small, E1, K1, exp_ready, exp_done).then_inc(gate_ready, 1)
            for i in range(4):
                v.wait_ge(gt_pe, i + 1)
                v.tensor_copy(gateT[:, 4 * i:4 * i + 4, :].rearrange("e t p -> e (t p)"), S[2 + i % 2][0:E1, :]).then_inc(gt_sb, 1)
            for i in range(4):
                v.wait_ge(b2_pe, i + 1)
                a = ACC[:, 4 * i:4 * i + 4, :].rearrange("p t c -> p (t c)")
                v.tensor_tensor(a, a, S[2 + i % 2][:, :], ALU.add).then_inc(b2_sb, 1)

        @block.scalar
        def _(act):
            for i in range(4):
                act.wait_ge(rt_pe, i + 1)
                act.copy(routeT[:, 4 * i:4 * i + 4, :].rearrange("e t p -> e (t p)"), S[i % 2][0:E0, :]).then_inc(rt_sb, 1)
            for b in range(B):
                act.wait_ge(xT_pe, b + 1)
                act.copy(xT[:, b, :], S[b][:, :]).then_inc(xT_sb, 1)
            act.wait_ge(b_sb, 1)
            for i in range(16):
                a, b = i % 4, i // 4
                act.wait_ge(hr_pe, i + 1)
                act.activation(HR[:, a, b, :], S[2 + i % 6][:, :], ACT.Relu, bias=rb1c[:, a:a + 1]).then_inc(hr_sb, 1)
            act.wait_ge(sc_pe, 1)
            act.copy(scT[:], S[1][:, :]).then_inc(sT_sb, 1)
            act.wait_ge(exp_ready, 1)
            act.activation(gate[:], gate[:], ACT.Exp).then_inc(exp_done, 1)

        @block.tensor
        def _(pe):
            def turn(b):
                pe.wait_ge(xn_ready, b + 1)
                for i in range(NT):
                    last = pe.transpose(S[b][:, P * i:P * i + P], XN[:, NT * b + i, :], ident[:])
                last.then_inc(xT_pe, 1)

            for i in range(4):
                if i >= 2:
                    pe.wait_ge(rt_sb, i - 1)
                for n in range(4):
                    last = pe.transpose(S[i % 2][0:E0, P * n:P * n + P], route[:, 4 * i + n, :], ident[:])
                last.then_inc(rt_pe, 1)
            for b in range(B):
                r = 64 * (b % 2)
                pe.wait_ge(rt_sb, b + 1)
                for i in range(NT):
                    o = S[4 + b][:, P * i:P * i + P]
                    pe.matmul(o, routeT[:, NT * b + i, :], b2r[:], start=True, stop=False)
                    for g in range(G):
                        last = pe.matmul(o, attT[r:r + 64, g, b // 2, P * i:P * i + P], wcp[r:r + 64, g, :],
                                         start=False, stop=(g == G - 1))
                last.then_inc(cp_pe, 1)
                if b >= 2:
                    turn(b - 2)
            turn(B - 2)
            turn(B - 1)
            pe.wait_ge(xT_sb, B)
            pe.wait_ge(d_w[0], 16 * 7)
            pe.transpose(S[1][:, 0:E1 * FQ], b1r[:], ident[0:E1 * FQ, 0:E1 * FQ])
            pe.transpose(S[1][:, 64:64 + FQ], rb1r[:], ident[0:FQ, 0:FQ]).then_inc(b_pe, 1)
            for i in range(16):
                a, b = i % 4, i // 4
                if i >= 6:
                    pe.wait_ge(hr_sb, i - 5)
                pe.matmul(S[2 + i % 6][:, :], rw1[:, P * a:P * a + P], xT[:, b, :], start=True, stop=True).then_inc(hr_pe, 1)
            pe.wait_ge(hr_sb, 16)
            pe.wait_ge(b_sb, 1)
            pe.wait_ge(d_w[2], 80)
            for a in range(FQ):
                for b in range(B):
                    last = pe.matmul(S[1][32 * b:32 * b + 32, :], rw2[:, a, :], HR[:, a, b, :], start=(a == 0), stop=(a == FQ - 1))
            last.then_inc(sc_pe, 1)
            pe.wait_ge(sT_sb, 1)
            for n in range(NT):
                last = pe.transpose(S[0][:, P * n:P * n + P], scT[:, P * n:P * n + P], ident[:])
            last.then_inc(sT_pe, 1)
            pe.wait_ge(gate_ready, 1)
            for i in range(4):
                if i >= 2:
                    pe.wait_ge(gt_sb, i - 1)
                for n in range(4):
                    last = pe.transpose(S[2 + i % 2][0:E1, P * n:P * n + P], gate[:, 4 * i + n, :], ident[:])
                last.then_inc(gt_pe, 1)
            pe.wait_ge(gt_sb, 4)
            for i in range(4):
                if i >= 2:
                    pe.wait_ge(b2_sb, i - 1)
                for n in range(4):
                    last = pe.matmul(S[2 + i % 2][:, P * n:P * n + P], gateT[:, 4 * i + n, :], b2r1[:], start=True, stop=True)
                last.then_inc(b2_pe, 1)

    KS = sb("KS", [P, HQ, T], F32R, l1)
    QS = sb("QS", [P, HQ, T], F32R, l1)
    XB = sb("XB", [P, T], F32, l1)
    XP = sb("XP", [P, 2, T], F32R, l1)
    MX = sb("MX", [P, NT, HQ, 4], F32, l1)
    EX = sb("EX", [P, 2, 4, NT, T], F32, l1)
    hi = EX[:, 1, 0:2, 0:2, :]
    ND = sb("ND", [P, 2, T], F32, l1)
    AT = attT[:].rearrange("p g b t -> p (g b) t")
    HB = sb("HB", [P, 2, FQ, T], F32, l1)
    SS = psum("SS", [P, 2, 2, T], l1)
    PHh = psum("PHh", [P, 2, T], l1)
    PYy = psum("PYy", [P, 4, C], l1)
    PN = psum("PN", [P, T], l1)
    block = l1.enter_context(nc.Block())

    tasks = ["q0", "q1", "k0", "k1", "v"] + [f"s{h}.{i}" for h in range(H1) for i in range(2)] + ["t0", "t1"]
    for q in range(HQ):
        tasks += [f"e{h}.{i}" for h in range(4 * q, 4 * q + 4) for i in range(2)]
        if q >= 1:
            tasks += [f"d{q - 1}"]
    tasks += [f"d{HQ - 1}", "o"]
    USES = len(tasks)
    assert USES % 2 == 0
    use = {name: n for n, name in enumerate(tasks)}
    filled = sem("slot_filled")
    freed = [sem("slot0_freed"), sem("slot1_freed")]
    xp_high, xp_ready = sem("xp_high"), sem("xp_ready")
    xb_ready, hi_ready, nx_hi, nx_ready = (sem(n) for n in ("xb_ready", "hi_ready", "nx_hi", "nx_ready"))
    nd_ready, nd_copied, at_ready = (sem(n) for n in ("nd_ready1", "nd_copied", "at_ready"))
    h_ready, h_relu, y_ready, y_used, d_done = (sem(n) for n in ("h_ready1", "h_relu", "y_ready1", "y_used1", "d_done"))
    UH, UE = E1 * FQ, E1

    def slot_of(name):
        return use[name] % 2

    def is_filled(b, name):
        return USES * b + use[name] + 1

    def may_fill(b, name):
        return (USES // 2) * b + use[name] // 2 + 1

    def is_emptied(b, name):
        return may_fill(b, name) + 1

    blocks = [("h", 0)]
    for e in range(1, E1):
        blocks += [("h", e), ("y", e - 1)]
    blocks += [("y", E1 - 1)]

    def pieces(first, end):
        return [(*blocks[n // 4], n % 4) for n in range(first, end)]

    def after_scores(h, i=None):
        first, end = (2 * h, 2 * h + 2) if i is None else (2 * h + i, 2 * h + i + 1)
        return 12 + first, 12 + end

    share = [(48, 52), (52, 56), (56, 60), (60, 62)]

    @block.sync
    def _(sp):
        with sp.Fori(0, B) as b:
            sp.wait_ge(freed[slot_of("o")], is_emptied(b, "o"))
            sp.dma_start(outd[:, bass.ds(NT * b, NT), :], ACC[:, bass.ds(NT * b, NT), :]).then_inc(d_done, 16)
        sp.wait_ge(d_done, 16 * B)

    @block.gpsimd
    def _(pool):
        pool.sem_inc(freed[0], 1)
        pool.sem_inc(freed[1], 1)
        pool.sem_inc(h_relu, 2)
        pool.sem_inc(y_ready, 2)
        pool.sem_inc(y_used, 1)
        pool.sem_inc(nd_copied, 1)
        pool.sem_inc(at_ready, 2)

    @block.tensor
    def _(pe):
        def fill(b, name):
            pe.wait_ge(freed[slot_of(name)], may_fill(b, name))
            return SS[:, slot_of(name), :, :]

        def experts(b, first, end):
            for kind, e, n in pieces(first, end):
                if kind == "h":
                    pe.wait_ge(h_relu, UH * b + FQ * e + n + 1)
                    for k, (wp, xp) in enumerate(((0, 0), (0, 1), (1, 0))):
                        mm = pe.matmul(PHh[:, n % 2, :], W1[:, wp, e, P * n:P * n + P], XP[:, xp, :], start=(k == 0), stop=(k == 2))
                    mm.then_inc(h_ready, 1)
                    continue
                if n == 0:
                    pe.wait_ge(h_relu, UH * b + FQ * e + FQ + 2)
                    pe.wait_ge(y_used, UE * b + e + 1)
                for a in range(FQ):
                    mm = pe.matmul(PYy[:, n, :], HB[:, e % 2, a, P * n:P * n + P], W2[:, e, a, :],
                                   start=(a == 0), stop=(a == FQ - 1))
                if n == NT - 1:
                    mm.then_inc(y_ready, 1)

        def project(b, w, name):
            bank = fill(b, name)
            for n in range(2):
                mm = pe.matmul(bank[:, n, :], w[:, 2 * int(name[1]) + n].rearrange("p h s d -> p (h s d)"), XB[:], start=True, stop=True)
            mm.then_inc(filled, 1)

        def scores(b, h, kind, halves=(0, 1)):
            r, q = 32 * (h % 4), h // 4
            rows, cols = (QS, KS) if kind == "s" else (KS, QS)
            for i in halves:
                bank = fill(b, f"{kind}{h}.{i}")
                for n in range(2):
                    t = 2 * i + n
                    mm = pe.matmul(bank[:, n, :], rows[r:r + 32, q, P * t:P * t + P], cols[r:r + 32, q, :], start=True, stop=True)
                mm.then_inc(filled, 1)

        def values(b, q, t):
            if t == 0:
                for i in range(2):
                    pe.wait_ge(freed[slot_of(f"e{4 * q + 3}.{i}")], is_emptied(b, f"e{4 * q + 3}.{i}"))
                pe.wait_ge(nd_copied, HQ * b + q + 1)
            for hh in range(4):
                mm = pe.matmul(PN[32 * hh:32 * hh + 32, :], VA[:, t, 4 * q + hh, :], EX[:, q % 2, hh, t, :],
                               start=(t == 0), stop=(t == NT - 1))
            if t == NT - 1:
                mm.then_inc(nd_ready, 1)

        def sums(b, q):
            bank = fill(b, f"d{q}")
            pe.wait_ge(nd_copied, HQ * b + q + 2)
            pe.matmul(bank[:, 0, :], sel[:], ND[:, q % 2, :], start=True, stop=True).then_inc(filled, 1)

        pe.wait_ge(ms_ready, 2)
        with pe.Fori(0, B) as b:
            pe.wait_ge(xb_ready, b + 1)
            project(b, wq, "q0")
            project(b, wq, "q1")
            pe.wait_ge(xp_ready, b + 1)
            experts(b, 0, 4)
            project(b, wk, "k0")
            project(b, wk, "k1")
            bank = fill(b, "v")
            for i in range(NT):
                mm = pe.matmul(bank[:, 0, P * i:P * i + P], XB[:, P * i:P * i + P], wv[:], start=True, stop=True)
            mm.then_inc(filled, 1)
            experts(b, 4, 12)
            for k in ("k0", "k1"):
                pe.wait_ge(freed[slot_of(k)], is_emptied(b, k))
            for h in range(H1):
                for i in range(2):
                    scores(b, h, "s", [i])
                    experts(b, *after_scores(h, i))
            experts(b, 44, 46)
            pe.wait_ge(nx_ready, b + 1)
            for i in range(2):
                bank = fill(b, f"t{i}")
                for n in range(2):
                    for t in range(NT):
                        mm = pe.transpose(bank[:, n, P * t:P * t + P], NX[:, t, 2 * i + n].rearrange("p h r -> p (h r)"), ident[:])
                mm.then_inc(filled, 1)
            experts(b, 46, 48)
            for i in range(2):
                pe.wait_ge(freed[slot_of(f"t{i}")], is_emptied(b, f"t{i}"))
            for q in range(HQ):
                for hh in range(4):
                    scores(b, 4 * q + hh, "e", [0])
                    if q == 0:
                        experts(b, share[0][0] + hh, share[0][0] + hh + 1)
                    else:
                        values(b, q - 1, hh)
                    scores(b, 4 * q + hh, "e", [1])
                if q >= 1:
                    first, end = share[q]
                    experts(b, first, (first + end) // 2)
                    sums(b, q - 1)
                    experts(b, (first + end) // 2, end)
            for t in range(NT):
                values(b, HQ - 1, t)
            experts(b, 62, 63)
            sums(b, HQ - 1)
            experts(b, 63, 64)
            pe.wait_ge(at_ready, HQ * b + HQ + 2)
            bank = fill(b, "o")
            for i in range(NT):
                for q in range(HQ):
                    mm = pe.matmul(bank[:, 0, P * i:P * i + P], AT[:, q, P * i:P * i + P], wo[:, q, :],
                                   start=(q == 0), stop=(q == HQ - 1))
            mm.then_inc(filled, 1)

    @block.scalar
    def _(act):
        def experts(b, first, end):
            for kind, e, n in pieces(first, end):
                if kind == "h":
                    if n == 0:
                        act.wait_ge(y_ready, UE * b + e + 1)
                    act.wait_ge(h_ready, UH * b + FQ * e + n + 1)
                    act.activation(HB[:, e % 2, n, :], PHh[:, n % 2, :], ACT.Relu, bias=b1c[:, e, n:n + 1]).then_inc(h_relu, 1)

        def high_part(b, name):
            act.wait_ge(filled, is_filled(b, name))
            dst = hi[:, slot_of(name)].bitcast(F32R)
            bias = zcol[:, 0:1] if name[0] == "q" else onesrow[:, 0:1]
            act.activation(dst, SS[:, slot_of(name), :, :], ACT.Identity, bias=bias).then_inc(hi_ready, 1)

        def exps(b, h):
            for i in range(2):
                name = f"e{h}.{i}"
                act.wait_ge(filled, is_filled(b, name))
                act.activation(EX[:, h // 4 % 2, h % 4, 2 * i:2 * i + 2, :], SS[:, slot_of(name), :, :], ACT.Exp, scale=SCALE1
                               ).then_inc(freed[slot_of(name)], 1)

        def copy_nd(b, q):
            act.wait_ge(nd_ready, HQ * b + q + 1)
            act.wait_ge(at_ready, HQ * b + q + 1)
            act.copy(ND[:, q % 2, :], PN[:]).then_inc(nd_copied, 1)

        act.wait_ge(ms_ready, 2)
        with act.Fori(0, B) as b:
            high_part(b, "q0")
            high_part(b, "q1")
            experts(b, 0, 4)
            high_part(b, "k0")
            high_part(b, "k1")
            act.wait_ge(filled, is_filled(b, "v"))
            act.copy(VA[:, :, :, 0:HD], SS[:, slot_of("v"), 0, :].rearrange("p (t h e) -> p t h e", t=NT, e=HD)
                     ).then_inc(freed[slot_of("v")], 1)
            experts(b, 4, 48)
            for q in range(HQ):
                if q >= 2:
                    act.wait_ge(nd_ready, HQ * b + q - 1)
                for hh in range(4):
                    exps(b, 4 * q + hh)
                    if q == 0:
                        experts(b, share[0][0] + hh, share[0][0] + hh + 1)
                if q >= 1:
                    copy_nd(b, q - 1)
                    experts(b, *share[q])
            copy_nd(b, HQ - 1)

    @block.vector
    def _(v):
        def low_part(b, name, dst):
            s = slot_of(name)
            i = int(name[1])
            v.wait_ge(hi_ready, 4 * b + use[name] + 1)
            v.scalar_tensor_tensor(out=dst[:, 2 * i:2 * i + 2, :], in0=hi[:, s],
                                   scalar=neglo[:, 0:1] if name[0] == "q" else neglo[:, 1:2],
                                   in1=SS[:, s, :, :], op0=ALU.mult, op1=ALU.add).then_inc(freed[s], 1)

        def maxima(b, h):
            for i in range(2):
                name = f"s{h}.{i}"
                v.wait_ge(filled, is_filled(b, name))
                v.tensor_reduce(MX[:, 2 * i:2 * i + 2, h // 4, h % 4], SS[:, slot_of(name), :, :], AX.X, ALU.max
                                ).then_inc(freed[slot_of(name)], 1)

        def experts(b, first, end):
            for kind, e, n in pieces(first, end):
                if kind == "y" and n == NT - 1:
                    v.wait_ge(y_ready, UE * b + e + 3)
                    for i in range(NT):
                        a = ACC[:, bass.ds(NT * b + i, 1), :].rearrange("p o c -> p (o c)")
                        ins = v.scalar_tensor_tensor(out=a, in0=PYy[:, i, :], scalar=gate[:, bass.ds(NT * b + i, 1), e],
                                                     in1=a, op0=ALU.mult, op1=ALU.add)
                    ins.then_inc(y_used, 1)

        def normalise(b, q):
            slot = slot_of(f"d{q}")
            v.wait_ge(filled, is_filled(b, f"d{q}"))
            v.reciprocal(AT[:, q, :], SS[:, slot, 0, :]).then_inc(freed[slot], 1)
            v.wait_ge(freed[slot], is_emptied(b, f"d{q}"))
            v.tensor_tensor(AT[:, q, :], ND[:, q % 2, :], AT[:, q, :], ALU.mult).then_inc(at_ready, 1)

        with v.Fori(0, B) as b:
            xb = xT[:, bass.ds(b, 1), :].rearrange("p o t -> p (o t)")
            v.tensor_copy(XB[:], xb).then_inc(xb_ready, 1)
            v.tensor_copy(XP[:, 0, :], xb).then_inc(xp_high, 1)
            v.wait_ge(xp_high, b + 1)
            v.tensor_tensor(XP[:, 1, :], xb, XP[:, 0, :].bitcast(F32), ALU.subtract).then_inc(xp_ready, 1)
            for name, dst in (("q0", QS), ("q1", QS), ("k0", KS), ("k1", KS)):
                low_part(b, name, dst)
            experts(b, 4, 12)
            for h in range(H1):
                maxima(b, h)
                experts(b, *after_scores(h))
            for i in range(2):
                v.wait_ge(freed[slot_of(f"s15.{i}")], is_emptied(b, f"s15.{i}"))
            m = MX[:].rearrange("p t q h -> p (t q) h")
            nx = NX[:].rearrange("p t q h r -> p (t q) h r")
            v.tensor_scalar(nx[:, :, :, 24].bitcast(F32R), m, -1.0, None, ALU.mult).then_inc(nx_hi, 1)
            v.wait_ge(nx_hi, b + 1)
            v.scalar_tensor_tensor(out=nx[:, :, :, 25], in0=m, scalar=-1.0, in1=nx[:, :, :, 24], op0=ALU.mult,
                                   op1=ALU.subtract).then_inc(nx_ready, 1)
            for i in range(2):
                name = f"t{i}"
                v.wait_ge(filled, is_filled(b, name))
                part = QS[:, 2 * i:2 * i + 2, :]
                v.tensor_tensor(part, part.bitcast(F32), SS[:, slot_of(name), :, :], ALU.add).then_inc(freed[slot_of(name)], 1)
            experts(b, 44, 52)
            for q in range(1, HQ):
                normalise(b, q - 1)
                experts(b, *share[q])
            normalise(b, HQ - 1)
            experts(b, 62, 64)
            v.wait_ge(filled, is_filled(b, "o"))
            v.wait_ge(y_used, UE * b + UE + 1)
            a = ACC[:, bass.ds(NT * b, NT), :].rearrange("p t c -> p (t c)")
            v.tensor_tensor(a, a, SS[:, slot_of("o"), 0, :], ALU.add).then_inc(freed[slot_of("o")], 1)


_OUT = ((B, T, C), "float32")


def kernel(**inputs):
    import numpy as np
    import concourse.bacc as bacc
    from concourse.bass_utils import run_bass_kernel_spmd

    nc = bacc.Bacc("TRN2", target_bir_lowering=False, num_devices=1)
    arrays, handles = {}, {}
    for name in inputs:
        a = np.ascontiguousarray(inputs[name])
        arrays[f"in_{name}"] = a
        handles[name] = nc.dram_tensor(f"in_{name}", a.shape, mybir.dt.from_np(a.dtype), kind="ExternalInput").ap()
    out = nc.dram_tensor("out", _OUT[0], F32, kind="ExternalOutput").ap()
    build(nc, handles, out)
    return run_bass_kernel_spmd(nc, [arrays], core_ids=[0]).results[0]["out"]
```
